# Optimizing a Trainium2 kernel written in Bass

```python
import numpy as np
import jax
import jax.numpy as jnp

def _softmax(x, axis=-1):
    return jax.nn.softmax(x, axis=axis)

def _gelu(x):
    return jax.nn.gelu(x, approximate=True)

def _silu(x):
    return jax.nn.silu(x)

def _sigmoid(x):
    return jax.nn.sigmoid(x)

def _layernorm(x, axis=-1, eps=1e-05):
    m = jnp.mean(x, axis=axis, keepdims=True)
    v = jnp.var(x, axis=axis, keepdims=True)
    return (x - m) / jnp.sqrt(v + eps)

def _scatter_add(tgt, idx, src, axis=0):
    return tgt.at[idx].add(src)

def _segment_sum(src, seg, n):
    return jax.ops.segment_sum(src, seg, n)
kernel_name = 'mk_gnn_preln_d4_gnn_r8_26c93a'

def setup_inputs(seed: int=0):
    np.random.seed(seed)
    _w = jnp.asarray

    def _rec_inputs():
        import jax
        import jax.numpy as jnp
        _gk = jax.random.key(seed)
        x = -0.000202 + 1 * jax.random.normal(jax.random.fold_in(_gk, 1), (6250, 128), jnp.float32)
        _s = jax.random.randint(jax.random.fold_in(_gk, 2), (50000,), 0, 6250, jnp.int32)
        _d = jax.random.randint(jax.random.fold_in(_gk, 3), (50000,), 0, 6250, jnp.int32)
        _loop = jnp.arange(6250, dtype=jnp.int32)
        src = jnp.concatenate([_s, _d, _loop])
        dst = jnp.concatenate([_d, _s, _loop])
        _o = jnp.argsort(dst, stable=True)
        src = src[_o]
        dst = dst[_o]
        edge_attr_128 = 2.93046e-05 + 1.00006 * jax.random.normal(jax.random.fold_in(_gk, 11), (106250, 128), jnp.float32)
        edge_attr_64 = 0.000155561 + 1.00019 * jax.random.normal(jax.random.fold_in(_gk, 12), (106250, 64), jnp.float32)
        return (x, src, dst, edge_attr_128, edge_attr_64)
    x, src, dst, edge_attr_128, edge_attr_64 = _rec_inputs()

    def _L0_gnn_setup():
        import jax, jax.numpy as jnp
        import numpy as np
        HIDDEN = 128
        EDGE_DIM = 64
        N_NODES = 6250
        N_EDGES = 75000

        def _linear_params(key, fan_in, fan_out):
            kw, kb = jax.random.split(key)
            bound = 1.0 / np.sqrt(fan_in)
            W = jax.random.uniform(kw, (fan_in, fan_out), minval=-bound, maxval=bound, dtype=jnp.float32)
            b = jax.random.uniform(kb, (fan_out,), minval=-bound, maxval=bound, dtype=jnp.float32)
            return (W, b)
        key = jax.random.key(seed)
        ks = jax.random.split(key, 10)
        h = jax.random.normal(ks[0], (N_NODES, HIDDEN), dtype=jnp.float32)
        edge_index = jax.random.randint(ks[1], (2, N_EDGES), 0, N_NODES, dtype=jnp.int64)
        edge_attr = jax.random.normal(ks[2], (N_EDGES, EDGE_DIM), dtype=jnp.float32)
        mW1, mb1 = _linear_params(ks[3], 2 * HIDDEN + EDGE_DIM, HIDDEN)
        mW2, mb2 = _linear_params(ks[4], HIDDEN, HIDDEN)
        mW3, mb3 = _linear_params(ks[5], HIDDEN, HIDDEN)
        uW1, ub1 = _linear_params(ks[6], 2 * HIDDEN, HIDDEN)
        uW2, ub2 = _linear_params(ks[7], HIDDEN, HIDDEN)
        gamma = jnp.ones((HIDDEN,), dtype=jnp.float32)
        beta = jnp.zeros((HIDDEN,), dtype=jnp.float32)
        return {'h': h, 'edge_index': edge_index, 'edge_attr': edge_attr, 'mW1': mW1, 'mb1': mb1, 'mW2': mW2, 'mb2': mb2, 'mW3': mW3, 'mb3': mb3, 'uW1': uW1, 'ub1': ub1, 'uW2': uW2, 'ub2': ub2, 'gamma': gamma, 'beta': beta}
    _L0_gnn_all = _L0_gnn_setup()
    _L0_gnn_in = {k: v for k, v in _L0_gnn_all.items() if k in ('mW1', 'mb1', 'mW2', 'mb2', 'mW3', 'mb3', 'uW1', 'ub1', 'uW2', 'ub2', 'gamma', 'beta')}
    del _L0_gnn_all

    def _L1_gnn_setup():
        import jax, jax.numpy as jnp
        import numpy as np
        N_NODES = 6250
        N_EDGES = 80000
        IN_DIM = 128
        HID_DIM = 128
        key = jax.random.key(seed)
        k1, k2, k3 = jax.random.split(key, 3)
        x = jax.random.normal(k1, (N_NODES, IN_DIM), dtype=jnp.float32)
        edge_index = jax.random.randint(k2, (2, N_EDGES), 0, N_NODES, dtype=jnp.int64)
        W = jax.random.normal(k3, (IN_DIM, HID_DIM), dtype=jnp.float32) * (1.0 / np.sqrt(IN_DIM))
        b = jnp.zeros((HID_DIM,), dtype=jnp.float32)
        return {'x': x, 'edge_index': edge_index, 'W': W, 'b': b}
    _L1_gnn_all = _L1_gnn_setup()
    _L1_gnn_in = {k: v for k, v in _L1_gnn_all.items() if k in ('W', 'b')}
    del _L1_gnn_all

    def _L2_gnn_setup():
        import jax, jax.numpy as jnp
        import numpy as np
        N = 6250
        E = 75000
        DIN = 128
        DH = 256
        DOUT = 128
        key = jax.random.key(seed)
        ks = jax.random.split(key, 8)
        x = jax.random.normal(ks[0], (N, DIN), dtype=jnp.float32)
        edge_index = jax.random.randint(ks[1], (2, E), 0, N, dtype=jnp.int64)
        lin_w = jax.random.normal(ks[2], (DIN, DOUT), dtype=jnp.float32) / np.sqrt(DIN)
        lin_b = jnp.zeros((DOUT,), dtype=jnp.float32)
        w1 = jax.random.normal(ks[3], (DOUT, DH), dtype=jnp.float32) / np.sqrt(DOUT)
        b1 = jnp.zeros((DH,), dtype=jnp.float32)
        w2 = jax.random.normal(ks[4], (DH, DOUT), dtype=jnp.float32) / np.sqrt(DH)
        b2 = jnp.zeros((DOUT,), dtype=jnp.float32)
        return {'x': x, 'edge_index': edge_index, 'lin_w': lin_w, 'lin_b': lin_b, 'w1': w1, 'b1': b1, 'w2': w2, 'b2': b2}
    _L2_gnn_all = _L2_gnn_setup()
    _L2_gnn_in = {k: v for k, v in _L2_gnn_all.items() if k in ('lin_w', 'lin_b', 'w1', 'b1', 'w2', 'b2')}
    del _L2_gnn_all

    def _L3_gnn_setup():
        import jax, jax.numpy as jnp
        import numpy as np
        N_NODES = 6250
        N_EDGES = 80000
        DIM = 128
        key = jax.random.key(seed)
        k_x, k_ei, k_ea, k_w1, k_w2 = jax.random.split(key, 5)
        x = jax.random.normal(k_x, (N_NODES, DIM), dtype=jnp.float32)
        edge_index = jax.random.randint(k_ei, (2, N_EDGES), 0, N_NODES, dtype=jnp.int32)
        edge_attr = jax.random.normal(k_ea, (N_EDGES, DIM), dtype=jnp.float32)
        s = 1.0 / np.sqrt(DIM)
        W1 = jax.random.normal(k_w1, (DIM, DIM), dtype=jnp.float32) * s
        b1 = jnp.zeros((DIM,), dtype=jnp.float32)
        W2 = jax.random.normal(k_w2, (DIM, DIM), dtype=jnp.float32) * s
        b2 = jnp.zeros((DIM,), dtype=jnp.float32)
        return {'x': x, 'edge_index': edge_index, 'edge_attr': edge_attr, 'W1': W1, 'b1': b1, 'W2': W2, 'b2': b2}
    _L3_gnn_all = _L3_gnn_setup()
    _L3_gnn_in = {k: v for k, v in _L3_gnn_all.items() if k in ('W1', 'b1', 'W2', 'b2')}
    del _L3_gnn_all
    return {'x': x, 'src': src, 'dst': dst, 'edge_attr_128': edge_attr_128, 'edge_attr_64': edge_attr_64, 'L0_gnn_mW1': _L0_gnn_in['mW1'], 'L0_gnn_mb1': _L0_gnn_in['mb1'], 'L0_gnn_mW2': _L0_gnn_in['mW2'], 'L0_gnn_mb2': _L0_gnn_in['mb2'], 'L0_gnn_mW3': _L0_gnn_in['mW3'], 'L0_gnn_mb3': _L0_gnn_in['mb3'], 'L0_gnn_uW1': _L0_gnn_in['uW1'], 'L0_gnn_ub1': _L0_gnn_in['ub1'], 'L0_gnn_uW2': _L0_gnn_in['uW2'], 'L0_gnn_ub2': _L0_gnn_in['ub2'], 'L0_gnn_gamma': _L0_gnn_in['gamma'], 'L0_gnn_beta': _L0_gnn_in['beta'], 'L1_gnn_W': _L1_gnn_in['W'], 'L1_gnn_b': _L1_gnn_in['b'], 'L2_gnn_lin_w': _L2_gnn_in['lin_w'], 'L2_gnn_lin_b': _L2_gnn_in['lin_b'], 'L2_gnn_w1': _L2_gnn_in['w1'], 'L2_gnn_b1': _L2_gnn_in['b1'], 'L2_gnn_w2': _L2_gnn_in['w2'], 'L2_gnn_b2': _L2_gnn_in['b2'], 'L3_gnn_W1': _L3_gnn_in['W1'], 'L3_gnn_b1': _L3_gnn_in['b1'], 'L3_gnn_W2': _L3_gnn_in['W2'], 'L3_gnn_b2': _L3_gnn_in['b2']}

def reference(x, src, dst, edge_attr_128, edge_attr_64, L0_gnn_mW1, L0_gnn_mb1, L0_gnn_mW2, L0_gnn_mb2, L0_gnn_mW3, L0_gnn_mb3, L0_gnn_uW1, L0_gnn_ub1, L0_gnn_uW2, L0_gnn_ub2, L0_gnn_gamma, L0_gnn_beta, L1_gnn_W, L1_gnn_b, L2_gnn_lin_w, L2_gnn_lin_b, L2_gnn_w1, L2_gnn_b1, L2_gnn_w2, L2_gnn_b2, L3_gnn_W1, L3_gnn_b1, L3_gnn_W2, L3_gnn_b2):
    import jax
    import jax.numpy as jnp

    def _L0_gnn_ref(h, edge_index, edge_attr, mW1, mb1, mW2, mb2, mW3, mb3, uW1, ub1, uW2, ub2, gamma, beta):
        import jax, jax.numpy as jnp
        import numpy as np
        HIDDEN = 128
        EDGE_DIM = 64
        N_NODES = 6250
        N_EDGES = 75000

        def _linear_params(key, fan_in, fan_out):
            kw, kb = jax.random.split(key)
            bound = 1.0 / np.sqrt(fan_in)
            W = jax.random.uniform(kw, (fan_in, fan_out), minval=-bound, maxval=bound, dtype=jnp.float32)
            b = jax.random.uniform(kb, (fan_out,), minval=-bound, maxval=bound, dtype=jnp.float32)
            return (W, b)
        src, dst = (edge_index[0], edge_index[1])
        x = jnp.concatenate([h[src], h[dst], edge_attr], axis=-1)
        x = jax.nn.gelu(x @ mW1 + mb1)
        x = jax.nn.gelu(x @ mW2 + mb2)
        msgs = x @ mW3 + mb3
        agg = jax.ops.segment_sum(msgs, dst, num_segments=h.shape[0])
        count = jax.ops.segment_sum(jnp.ones((dst.shape[0], 1), dtype=h.dtype), dst, num_segments=h.shape[0])
        agg = agg / (count + 1e-08)
        u = jnp.concatenate([h, agg], axis=-1)
        u = jax.nn.gelu(u @ uW1 + ub1)
        out = u @ uW2 + ub2
        y = out + h
        mu = jnp.mean(y, axis=-1, keepdims=True)
        var = jnp.var(y, axis=-1, keepdims=True)
        return (y - mu) / jnp.sqrt(var + 1e-05) * gamma + beta

    def _L1_gnn_ref(x, edge_index, W, b):
        import jax, jax.numpy as jnp
        import numpy as np
        N_NODES = 6250
        N_EDGES = 80000
        IN_DIM = 128
        HID_DIM = 128
        N = x.shape[0]
        loops = jnp.arange(N, dtype=edge_index.dtype)
        src = jnp.concatenate([edge_index[0], loops])
        dst = jnp.concatenate([edge_index[1], loops])
        ones = jnp.ones(src.shape[0], dtype=x.dtype)
        deg = jax.ops.segment_sum(ones, dst, num_segments=N)
        dinv = jnp.where(deg > 0, jax.lax.rsqrt(deg), 0.0)
        norm = dinv[src] * dinv[dst]
        h = x @ W
        msg = h[src] * norm[:, None]
        agg = jax.ops.segment_sum(msg, dst, num_segments=N)
        return jax.nn.relu(agg + b)

    def _L2_gnn_ref(x, edge_index, lin_w, lin_b, w1, b1, w2, b2):
        import jax, jax.numpy as jnp
        import numpy as np
        N = 6250
        E = 75000
        DIN = 128
        DH = 256
        DOUT = 128
        n = x.shape[0]
        x_lin = x @ lin_w + lin_b
        loop = jnp.arange(n, dtype=edge_index.dtype)
        rows = jnp.concatenate([edge_index[0], loop])
        cols = jnp.concatenate([edge_index[1], loop])
        deg = jax.ops.segment_sum(jnp.ones_like(rows, dtype=x_lin.dtype), rows, num_segments=n)
        dis = jax.lax.rsqrt(deg)
        norm = dis[rows] * dis[cols]
        msgs = x_lin[cols] * norm[:, None]
        m = jax.ops.segment_sum(msgs, rows, num_segments=n)
        z = jax.nn.relu(m)
        return jax.nn.relu(z @ w1 + b1) @ w2 + b2

    def _L3_gnn_ref(x, edge_index, edge_attr, W1, b1, W2, b2):
        import jax, jax.numpy as jnp
        import numpy as np
        N_NODES = 6250
        N_EDGES = 80000
        DIM = 128
        src = edge_index[0]
        dst = edge_index[1]
        n = x.shape[0]
        msg = jax.nn.silu(x[src] + edge_attr)
        msg_sum = jax.ops.segment_sum(msg, dst, num_segments=n)
        cnt = jax.ops.segment_sum(jnp.ones_like(dst, dtype=x.dtype), dst, num_segments=n)
        aggr = msg_sum / jnp.maximum(cnt, 1.0)[:, None]
        h = x + aggr
        h = jax.nn.silu(h @ W1 + b1) @ W2 + b2
        return x + h
    edge_index = jnp.stack([src, dst])
    h = jnp.maximum(_layernorm(x, axis=-1), 0.0)
    x = x + _L0_gnn_ref(h, edge_index, edge_attr_64, L0_gnn_mW1, L0_gnn_mb1, L0_gnn_mW2, L0_gnn_mb2, L0_gnn_mW3, L0_gnn_mb3, L0_gnn_uW1, L0_gnn_ub1, L0_gnn_uW2, L0_gnn_ub2, L0_gnn_gamma, L0_gnn_beta)
    h = jnp.maximum(_layernorm(x, axis=-1), 0.0)
    x = x + _L1_gnn_ref(h, edge_index, L1_gnn_W, L1_gnn_b)
    h = jnp.maximum(_layernorm(x, axis=-1), 0.0)
    x = x + _L2_gnn_ref(h, edge_index, L2_gnn_lin_w, L2_gnn_lin_b, L2_gnn_w1, L2_gnn_b1, L2_gnn_w2, L2_gnn_b2)
    h = jnp.maximum(_layernorm(x, axis=-1), 0.0)
    x = x + _L3_gnn_ref(h, edge_index, edge_attr_128, L3_gnn_W1, L3_gnn_b1, L3_gnn_W2, L3_gnn_b2)
    return x

_drawn_inputs = setup_inputs


def setup_inputs(seed=0):
    import zlib

    import numpy as np

    out = dict(_drawn_inputs(seed))
    spreads = {'L0_gnn_gamma': (1.0, 0.2),
     'L0_gnn_beta': (0.0, 0.1),
     'L1_gnn_b': (0.0, 0.1),
     'L2_gnn_lin_b': (0.0, 0.364),
     'L2_gnn_b1': (0.0, 0.1),
     'L2_gnn_b2': (0.0, 0.1),
     'L3_gnn_b1': (0.0, 0.344),
     'L3_gnn_b2': (0.0, 0.1)}
    factors = {'edge_attr_64': 8.0,
     'L0_gnn_mW1': 8.0,
     'L0_gnn_mb1': 61.79,
     'L0_gnn_mW2': 8.0,
     'L0_gnn_mb2': 64.0,
     'L0_gnn_mW3': 8.0,
     'L0_gnn_mb3': 200.0,
     'L0_gnn_ub1': 174.087,
     'L0_gnn_ub2': 40.475}
    for name, (base, spread) in spreads.items():
        noise = np.random.default_rng([zlib.crc32(name.encode()), seed]).standard_normal(out[name].shape)
        drawn = base * np.exp(spread * noise) if base else spread * noise
        out[name] = jnp.asarray(drawn.astype(out[name].dtype))
    for name, factor in factors.items():
        out[name] = (out[name] * factor).astype(out[name].dtype)
    return out
```

```python
from contextlib import ExitStack

import concourse.bass as bass
from concourse import mybir
from concourse.alu_op_type import AluOpType as ALU

F32 = mybir.dt.float32
BF16 = mybir.dt.bfloat16
I32 = mybir.dt.int32
ACT = mybir.ActivationFunctionType
AX = mybir.AxisListType
RMAX = bass.bass_isa.ReduceOp.max

N = 6250
E = 106250
F = 128
FE = 64
P = 125
G = 5
NG = E // (P * G)
W = 64
CH = 5
NT = N // P
NCH = NT // CH
CN = CH * P
HB = 128
NHI = (N + HB - 1) // HB
LN_EPS = 1e-5



class Chain:

    def __init__(self, eng, sem):
        self.eng, self.sem, self.base, self.n, self.start = eng, sem, 0, 0, 0

    def link(self, instruction):
        self.n += 1
        instruction.then_inc(self.sem, 1)
        self.eng.wait_ge(self.sem, self.base + self.n)

    def loop(self, first, count, body):
        start = self.n if isinstance(self.base, int) and self.base == 0 else self.base + self.n
        self.base, self.n = start, 0
        body(0, True)
        per = self.n
        with self.eng.Fori(1, count) as i:
            self.base, self.n = i * per + start, 0
            body(i, False)
            assert self.n == per
        self.base, self.n = start + per * count, 0

def gnn_kernel(nc, x, src_g, dst_g, src_rows, dst_rows, edge_attr_128, edge_attr_64_t,
               mW1, mb1, mW2, mb2, mW3, mb3, uW1, ub1, uW2, ub2, gamma, beta,
               gW, gb, lin_w, lin_b, w1, b1, w2, b2, sW1, sb1, sW2, sb2, out):
    ctx = ExitStack()
    with ctx:
        def sb(name, shape, dt=F32):
            return ctx.enter_context(nc.sbuf_tensor(name, shape, dt))

        def sem(name):
            return ctx.enter_context(nc.semaphore(name))

        def dram(name, shape):
            return nc.dram_tensor(name, shape, F32).ap()

        src_table0 = dram("src_table0", (N, F))
        dst_table0 = dram("dst_table0", (N, F))
        table1 = dram("table1", (N, F))
        table2 = dram("table2", (N, F))
        table3 = dram("table3", (N, F))
        sums = [dram(f"sums{g}", (N + P, F)) for g in range(G)]
        stats = dram("stats", (5, NHI * HB))

        X = sb("X", [P, NT, F])
        HN = sb("HN", [P, NT, F])
        HT = sb("HT", [F, N])
        ACC = sb("ACC", [F, N])
        srcI = sb("srcI", [P, NG * G], I32)
        dstI = sb("dstI", [P, NG * G], I32)
        dst_rel = sb("dst_rel", [P, NG * G])
        high = sb("high", [P, NG * G])
        low = sb("low", [P, NG * G])
        part_of = sb("part_of", [P, NG * G], I32)
        neg_min = sb("neg_min", [P, NG])
        neg_win = sb("neg_win", [P, NG])
        win_node = sb("win_node", [P, NG])
        winI = sb("winI", [1, NG], I32)
        ident = sb("ident", [F, F])
        before = sb("before", [P, P], BF16)
        iota_i = sb("iota_i", [P, F], I32)
        iota = sb("iota", [P, F])
        part_i = sb("part_i", [P, 1], I32)
        part = sb("part", [P, 1])
        spare_row = sb("spare_row", [P, 1])
        neg_half = sb("neg_half", [P, HB])
        zeros = sb("zeros", [P, CH * F])
        zeros16 = sb("zeros16", [P, HB], BF16)
        w_pq = sb("w_pq", [F, 2 * F])
        w_m2, w_m3 = sb("w_m2", [F, F]), sb("w_m3", [F, F])
        w_uh, w_ua, w_u2 = sb("w_uh", [F, F]), sb("w_ua", [F, F]), sb("w_u2", [F, F])
        w_g, w_lin = sb("w_g", [F, F]), sb("w_lin", [F, F])
        w_z1, w_z2 = sb("w_z1", [F, 2 * F]), sb("w_z2", [F, 2, F])
        w_s1, w_s2 = sb("w_s1", [F, F]), sb("w_s2", [F, F])
        c_mb1, c_mb3, c_ub1, c_sb1 = (sb(n, [F, 1]) for n in ("c_mb1", "c_mb3", "c_ub1", "c_sb1"))
        c_b1 = sb("c_b1", [F, 2])
        r_mb2, r_ub2, r_gamma, r_beta, r_gb, r_lb, r_b2, r_sb2 = (
            sb(n, [P, F]) for n in ("r_mb2", "r_ub2", "r_gamma", "r_beta", "r_gb", "r_lb", "r_b2", "r_sb2"))
        hist = sb("hist", [NHI, 4, HB])
        stat_rows = sb("stat_rows", [NT, P])
        dinv1 = sb("dinv1", [P, NT])
        dinv2 = sb("dinv2", [P, NT])
        idx = [sb(f"idx{b}", [P, G], I32) for b in range(2)]
        GA_all = sb("GA_all", [P, 2, G, F])
        GA = [GA_all[:, b] for b in range(2)]
        ER = [sb(f"ER{b}", [F, G * F]) for b in range(2)]
        DR = [ER[b][0:W, 0:G * P].bitcast(I32) for b in range(2)]
        SR = [ER[b][0:P, 0:G * P].bitcast(I32) for b in range(2)]
        R = [sb(f"R{b}", [F, G * P]) for b in range(2)]
        L = [sb(f"L{b}", [F, F]) for b in range(2)]
        OH = [sb(f"OH{b}", [P, G, W]) for b in range(2)]
        OHB = [sb(f"OHB{b}", [P, G, W], BF16) for b in range(2)]
        HHI = [sb(f"HHI{b}", [P, G, NHI], BF16) for b in range(2)]
        HLO = [sb(f"HLO{b}", [P, G, HB], BF16) for b in range(2)]
        A1 = [sb(f"A1_{b}", [F, G, F]) for b in range(2)]
        A2 = [sb(f"A2_{b}", [P, G, F]) for b in range(2)]
        A3f = [sb(f"A3_{b}", [F, G, F]) for b in range(2)]
        A3 = [A3f[b][0:P] for b in range(2)]
        SM = [sb(f"SM{b}", [P, G, P], BF16) for b in range(2)]
        SE = sb("SE", [P, G, P], BF16)
        earlier = sb("earlier", [P, G])
        to_spare = sb("to_spare", [P, G])
        move = sb("move", [P, G])
        stats6 = sb("stats6", [P, CH, 6])
        mean_var = sb("mean_var", [P, CH, 2])
        var_eps = sb("var_eps", [P, CH])
        rstd = sb("rstd", [P, CH])
        row_stage, val_stage = A2[0], A2[1]
        table_stage = sb("table_stage", [P, CH, F])
        pq_stage = GA_all[:, :, :, :].rearrange("p a g f -> p (a g f)").rearrange("p (g f) -> p g f", f=2 * F)
        t_stage, agg_stage = A1[0], A1[1]
        z_stage = ER[1][:, :].rearrange("p (g f) -> p g f", f=F)
        hid_stage = A3f
        cnt_stage = R
        sum_parts = [GA[0], GA[1], A1[0][0:P], A1[1][0:P], ER[0][0:P, :].rearrange("p (g f) -> p g f", f=F)]

        PS = ctx.enter_context(nc.psum_tensor("PS", [F, 8 * 512], F32))

        def tiles(bank, rows, inner=F):
            return PS[0:rows, bank * 512:bank * 512 + G * F].rearrange("p (g f) -> p g f", f=F)[:, :, 0:inner]

        BANK_TILES = 512 // (2 * F)
        PQ = PS[0:P, 2 * 512:2 * 512 + CH * 2 * F].rearrange("p (g f) -> p g f", f=2 * F)
        AGG = PS[:, 6 * 512:6 * 512 + W]
        HIST = PS[0:NHI, 7 * 512:7 * 512 + HB]
        TURNED = PS[0:P, 7 * 512 + HB:7 * 512 + HB + NT]

        def sems(prefix, names):
            return {n: sem(f"{prefix}_{n}") for n in names.split()}

        def slot_sems(prefix):
            return [sem(f"{prefix}{b}") for b in range(2)]

        loads, consts, zeroed = sem("loads"), sem("consts"), sem("zeroed")
        waits_passed = sem("waits_passed")
        pool_chain, dve_chain = sem("pool_chain"), sem("dve_chain")
        neg_min_ready, neg_win_ready, win_ready = sem("neg_min_ready"), sem("neg_win_ready"), sem("win_ready")
        var_ready, rstd_ready = sem("var_ready"), sem("rstd_ready")
        st = sems("st", "counted rooted stored loaded turned done")
        e0 = sems("e0", "idx onehot onehot_t hist_in hist x1_win x1 g1 x2 y2 g2 agg added")
        e1 = sems("e1", "idx onehot hist_in hist agg added")
        e2 = sems("e2", "idx onehot same pick picked rows rows_out")
        e3 = sems("e3", "idx onehot msg_in msg agg added")
        gathered = {i: slot_sems(f"e{i}_gathered") for i in (0, 1, 3)}
        attr_in = {i: slot_sems(f"e{i}_attr_in") for i in (0, 3)}
        rows_in = {i: slot_sems(f"e{i}_rows_in") for i in (0, 2)}
        window_in = {i: slot_sems(f"e{i}_window_in") for i in (0, 2)}
        scattered = [sem(f"scattered{g}") for g in range(G)]
        n0 = sems("n0", "hn row turn turned ht mm p_out q_out stored")
        n1 = sems("n1", "inp mm agg mm2 act mm3 y row turn acc stored")
        n2 = sems("n2", "acc_cp mm v hn row turn turned mm2 lin out stored")
        n3 = sems("n3", "inp sum row turn turned mm act mm2 x out stored turn2 ht acc_zero")
        n4 = sems("n4", "inp hh mm act mm2 y out stored")

        def weight_list():
            yield w_pq[:, 0:F], mW1[0:F, :]
            yield w_pq[:, F:2 * F], mW1[F:2 * F, :]
            for b in range(2):
                yield L[b][W:F, :], mW1[2 * F:2 * F + FE, :]
            yield w_m2[:, :], mW2
            yield w_m3[:, :], mW3
            yield w_uh[:, :], uW1[0:F, :]
            yield w_ua[:, :], uW1[F:2 * F, :]
            yield w_u2[:, :], uW2
            yield w_g[:, :], gW
            yield w_lin[:, :], lin_w
            yield w_z1[:, :], w1
            for h in range(2):
                yield w_z2[:, h, :], w2[h * F:(h + 1) * F, :]
            yield w_s1[:, :], sW1
            yield w_s2[:, :], sW2
            for col, v in ((c_mb1, mb1), (c_mb3, mb3), (c_ub1, ub1), (c_sb1, sb1)):
                yield col[:, :], v.rearrange("(p a) -> p a", a=1)
            for h in range(2):
                yield c_b1[:, h:h + 1], b1[h * F:(h + 1) * F].rearrange("(p a) -> p a", a=1)
            for row, v in ((r_mb2, mb2), (r_ub2, ub2), (r_gamma, gamma), (r_beta, beta), (r_gb, gb),
                           (r_lb, lin_b), (r_b2, b2), (r_sb2, sb2)):
                yield row[:, :], v.rearrange("(a f) -> a f", a=1).to_broadcast([P, F])

        n_loads = 3 + len(list(weight_list()))
        n_consts = 8

        def node_rows(t, k):
            return t[bass.ds(k * CN, CN), :].rearrange("(t p) f -> p t f", p=P)

        def chunk(buf, k):
            return buf[:, bass.ds(k * CH, CH), :]

        def chunk_t(buf, k):
            return buf[:, bass.ds(k * CN, CN)].rearrange("p (t n) -> p t n", n=P)

        def tile_col(buf, k, j):
            return buf[:, bass.ds(k * CH + j, 1)]

        def group(buf, c):
            return buf[:, bass.ds(c * G, G)]

        def over_groups(eng, body):
            body(0, True, False)
            with eng.Fori(1, NG // 2 - 1) as t:
                body(t, False, False)
            body(NG // 2 - 1, False, True)

        def over_chunks(eng, body):
            body(0, True)
            with eng.Fori(1, NCH) as k:
                body(k, False)

        def part_from_waits(eng):
            eng.sem_inc(waits_passed, 1)

        block = ctx.enter_context(nc.Block())

        @block.sync
        def _(sp):
            sp.dma_start(X[:, :, :], x.rearrange("(t p) f -> p t f", p=P)).then_inc(loads, 16)
            sp.dma_start(dstI[:, :], dst_g).then_inc(loads, 16)
            sp.dma_start(srcI[:, :], src_g).then_inc(loads, 16)
            for to, frm in weight_list():
                sp.dma_start(to, frm).then_inc(loads, 16)
            sp.wait_ge(consts, n_consts)
            for g in range(G):
                if g:
                    with sp.Fori(0, NCH) as k:
                        sp.dma_start(node_rows(sums[g], k),
                                     zeros[:, :].rearrange("p (t f) -> p t f", f=F)).then_inc(zeroed, 16)
                sp.dma_start(sums[g][N:N + P, :], zeros[:, 0:F]).then_inc(zeroed, 16)

            def nodes0(k, first):
                sp.wait_ge(n0["p_out"], k + 1)
                sp.wait_ge(n0["q_out"], k + 1)
                sp.dma_start(node_rows(src_table0, k), pq_stage[:, :, 0:F]).then_inc(n0["stored"], 16)
                sp.dma_start(node_rows(dst_table0, k), pq_stage[:, :, F:2 * F]).then_inc(n0["stored"], 16)
            over_chunks(sp, nodes0)

            def edges0(t, first, last):
                for b in range(2):
                    c = 2 * t + b
                    if not first:
                        sp.wait_ge(e0["onehot_t"], c - 1)
                        sp.wait_ge(e0["x1_win"], c - 1)
                    sp.dma_start(DR[b], dst_rows[bass.ds(c, 1), :].to_broadcast([W, G * P])).then_inc(rows_in[0][b], 16)
                    sp.dma_start(R[b][W:F, :], edge_attr_64_t[bass.ds(c * FE, FE), :]).then_inc(attr_in[0][b], 16)
            over_groups(sp, edges0)

            def store_stats(rows, n):
                for i, r in enumerate(rows):
                    sp.dma_start(stats[r:r + 1, :].rearrange("a (h l) -> (a h) l", l=HB),
                                 hist[:, i, :]).then_inc(st["stored"], 16)
                sp.wait_ge(st["stored"], 16 * n)
                r = rows[-1]
                sp.dma_start(stat_rows[:, :], stats[r:r + 1, 0:N].rearrange("a (t p) -> (a t) p", p=P)
                             ).then_inc(st["loaded"], 16)
            sp.wait_ge(st["rooted"], 1)
            store_stats((0, 1, 2, 3), 4)

            sp.wait_ge(e0["x1_win"], NG)
            def nodes1(k, first):
                if not first:
                    sp.wait_ge(n1["agg"], k)
                for i in range(2):
                    sp.dma_start(cnt_stage[i][:, :], stats[i:i + 1, bass.ds(k * CN, CN)].to_broadcast([F, CN])
                                 ).then_inc(n1["inp"], 16)
                sp.wait_ge(n1["row"], k + 1)
                sp.dma_start(node_rows(table1, k), table_stage[:, :, :]).then_inc(n1["stored"], 16)
            over_chunks(sp, nodes1)

            sp.wait_ge(st["rooted"], 2)
            store_stats((4,), 5)

            def nodes2(k, first):
                sp.wait_ge(n2["out"], k + 1)
                sp.dma_start(node_rows(table2, k), table_stage[:, :, :]).then_inc(n2["stored"], 16)
                sp.dma_start(node_rows(sums[0], k), table_stage[:, :, :]).then_inc(n2["stored"], 16)
            over_chunks(sp, nodes2)

            def edges2(t, first, last):
                for b in range(2):
                    c = 2 * t + b
                    if not first:
                        sp.wait_ge(e2["same"], c - 1)
                    sp.dma_start(SR[b], src_rows[bass.ds(c, 1), :].to_broadcast([P, G * P])).then_inc(rows_in[2][b], 16)
            over_groups(sp, edges2)
            for g in range(G):
                sp.wait_ge(scattered[g], 16 * NG)

            def nodes3(k, first):
                if not first:
                    sp.wait_ge(n3["sum"], k)
                for g in range(G):
                    sp.dma_start(sum_parts[g], node_rows(sums[g], k)).then_inc(n3["inp"], 16)
                sp.wait_ge(n3["out"], k + 1)
                sp.dma_start(node_rows(table3, k), table_stage[:, :, :]).then_inc(n3["stored"], 16)
            over_chunks(sp, nodes3)

            sp.wait_ge(n3["mm"], NCH)
            def edges3(t, first, last):
                for b in range(2):
                    c = 2 * t + b
                    if not first:
                        sp.wait_ge(e3["msg_in"], c - 1)
                    sp.dma_start(ER[b][0:P, :], edge_attr_128[bass.ds(c * P * G, P * G), :]
                                 .rearrange("(p g) f -> p (g f)", g=G)).then_inc(attr_in[3][b], 16)
            over_groups(sp, edges3)

            def nodes4(k, first):
                if not first:
                    sp.wait_ge(n4["hh"], k)
                sp.dma_start(cnt_stage[0][:, :], stats[2:3, bass.ds(k * CN, CN)].to_broadcast([F, CN])
                             ).then_inc(n4["inp"], 16)
                sp.wait_ge(n4["out"], k + 1)
                sp.dma_start(node_rows(out, k), chunk(X, k)).then_inc(n4["stored"], 16)
            over_chunks(sp, nodes4)
            sp.wait_ge(n4["stored"], 16 * NCH)

        @block.gpsimd
        def _(pool):
            ch = Chain(pool, pool_chain)
            pool.memset(zeros[:, :], 0.0).then_inc(consts, 1)
            pool.memset(zeros16[:, :], 0.0).then_inc(consts, 1)
            pool.memset(neg_half[:, :], -0.5).then_inc(consts, 1)
            pool.iota(iota_i[:, :], pattern=[[1, F]], base=0, channel_multiplier=0).then_inc(consts, 1)
            pool.iota(part_i[:, :], pattern=[[0, 1]], base=0, channel_multiplier=1).then_inc(consts, 1)
            pool.memset(ACC[:, :], 0.0).then_inc(consts, 1)
            ch.link(pool.memset(ident[:, :], 0.0))
            ch.link(pool.memset(before[:, :], 1.0))
            pool.affine_select(out=ident[:, :], in_=ident[:, :], compare_op=ALU.not_equal, fill=1.0, base=0,
                               pattern=[[-1, F]], channel_multiplier=1).then_inc(consts, 1)
            pool.affine_select(out=before[:, :], in_=before[:, :], compare_op=ALU.is_gt, fill=0.0, base=0,
                               pattern=[[-1, P]], channel_multiplier=1).then_inc(consts, 1)
            pool.wait_ge(neg_min_ready, 1)
            pool.partition_all_reduce(neg_win[:, :], neg_min[:, :], P, RMAX).then_inc(neg_win_ready, 1)

            done = [0]

            def inverse_roots(norms):
                def body(k, first):
                    for i in range(norms):
                        r = k * norms + (done[0] + i)
                        pool.wait_ge(var_ready, r + 1)
                        pool.tensor_tensor(rstd[:, :], var_eps[:, :], neg_half[:, 0:CH], ALU.pow).then_inc(rstd_ready, 1)
                over_chunks(pool, body)
                done[0] += norms * NCH

            def root_counts(n, i):
                pool.wait_ge(st["counted"], n)
                pool.tensor_tensor(hist[:, i, :], hist[:, i, :], neg_half[0:NHI, :], ALU.pow).then_inc(st["rooted"], 1)

            def gather(i, ready, table, read):
                def body(t, first, last):
                    for b in range(2):
                        c = 2 * t + b
                        pool.wait_ge(ready, c + 1)
                        if not first:
                            pool.wait_ge(read, c - 1)
                        part_from_waits(pool)
                        for g in range(G):
                            pool.indirect_dma_start(
                                out=GA[b][:, g, :], out_offset=None, in_=table,
                                in_offset=bass.IndirectOffsetOnAxis(ap=idx[b][:, g:g + 1], axis=0)
                            ).then_inc(gathered[i][b], 16)
                over_groups(pool, body)

            inverse_roots(1)
            pool.wait_ge(n0["stored"], 32 * NCH)
            gather(0, e0["idx"], src_table0, e0["x1"])
            root_counts(1, 3)
            inverse_roots(2)
            pool.wait_ge(n1["stored"], 16 * NCH)
            gather(1, e1["idx"], table1, e1["agg"])
            root_counts(2, 0)
            inverse_roots(1)
            pool.wait_ge(n2["stored"], 32 * NCH)
            pool.wait_ge(zeroed, 16 * (G + (G - 1) * NCH))

            def scatter(t, first, last):
                for b in range(2):
                    c = 2 * t + b
                    pool.wait_ge(e2["idx"], c + 1)
                    pool.wait_ge(e2["rows_out"], c + 1)
                    for g in range(G):
                        if not (first and b == 0):
                            pool.wait_ge(scattered[g], 16 * c)
                        part_from_waits(pool)
                        pool.indirect_dma_start(
                            out=sums[g], out_offset=bass.IndirectOffsetOnAxis(ap=idx[b][:, g:g + 1], axis=0),
                            in_=A3[b][:, g, :], in_offset=None, compute_op=ALU.add).then_inc(scattered[g], 16)
            over_groups(pool, scatter)
            pool.wait_ge(n2["acc_cp"], NCH)
            pool.memset(ACC[:, :], 0.0).then_inc(n3["acc_zero"], 1)
            inverse_roots(1)
            pool.wait_ge(n3["stored"], 16 * NCH)
            gather(3, e3["idx"], table3, e3["msg_in"])

        @block.scalar
        def _(act):
            fn = nc.scalar.activation
            act.wait_ge(loads, 16 * n_loads)
            act.wait_ge(win_ready, 1)

            def nodes0(k, first):
                act.wait_ge(n0["hn"], k + 1)
                if not first:
                    act.wait_ge(n0["turn"], k)
                fn(row_stage[:, :, :], chunk(HN, k), ACT.Relu).then_inc(n0["row"], 1)
                act.wait_ge(n0["turn"], k + 1)
                if not first:
                    act.wait_ge(n0["mm"], k)
                    act.wait_ge(n0["ht"], k)
                fn(t_stage[:, :, 0:P], tiles(0, F, P), ACT.Copy).then_inc(n0["turned"], 1)
                act.wait_ge(n0["mm"], k + 1)
                if not first:
                    act.wait_ge(n0["stored"], 32 * k)
                n = 2 * BANK_TILES
                fn(pq_stage[:, 0:n, :], PQ[:, 0:n, :], ACT.Copy).then_inc(n0["p_out"], 1)
            over_chunks(act, nodes0)

            def window(i, c, b, table):
                lo = act.value_load(winI[0:1, bass.ds(c, 1)], min_val=0, max_val=N - W)
                act.dma_start(L[b][0:W, :], table[bass.ds(lo, W), :]).then_inc(window_in[i][b], 16)

            act.wait_ge(n0["stored"], 32 * NCH)
            for b in range(2):
                window(0, b, b, dst_table0)

            def edges0(t, first, last):
                for b in range(2):
                    c = 2 * t + b
                    act.wait_ge(e0["x1"], c + 1)
                    if not first:
                        act.wait_ge(e0["x2"], c - 1)
                    fn(A1[b][:, :, 0:P], tiles(2 * b, F, P), ACT.Gelu_apprx_tanh, bias=c_mb1[:, :]
                       ).then_inc(e0["g1"], 1)
                    if not last:
                        window(0, c + 2, b, dst_table0)
                    act.wait_ge(e0["y2"], c + 1)
                    if not first:
                        act.wait_ge(e0["agg"], c - 1)
                    fn(A3[b][:, :, :], A2[b][:, :, :], ACT.Gelu_apprx_tanh).then_inc(e0["g2"], 1)
            over_groups(act, edges0)
            act.wait_ge(st["turned"], 1)
            fn(dinv1[:, :], TURNED, ACT.Copy).then_inc(st["done"], 1)

            def nodes1(k, first):
                act.wait_ge(n1["mm2"], k + 1)
                if not first:
                    act.wait_ge(n1["mm3"], k)
                fn(t_stage[:, :, 0:P], tiles(2, F, P), ACT.Gelu_apprx_tanh, bias=c_ub1[:, :]).then_inc(n1["act"], 1)
                act.wait_ge(n1["turn"], k + 1)
                fn(chunk_t(ACC, k), tiles(0, F, P), ACT.Copy).then_inc(n1["acc"], 1)
            over_chunks(act, nodes1)
            act.wait_ge(st["turned"], 2)
            fn(dinv2[:, :], TURNED, ACT.Copy).then_inc(st["done"], 1)

            act.wait_ge(e1["added"], NG)

            def nodes2(k, first):
                if not first:
                    act.wait_ge(n2["mm"], k)
                fn(agg_stage[:, :, 0:P], chunk_t(ACC, k), ACT.Copy).then_inc(n2["acc_cp"], 1)
                act.wait_ge(n2["hn"], k + 1)
                if not first:
                    act.wait_ge(n2["turn"], k)
                fn(row_stage[:, :, :], chunk(HN, k), ACT.Relu).then_inc(n2["row"], 1)
                act.wait_ge(n2["turn"], k + 1)
                if not first:
                    act.wait_ge(n2["mm2"], k)
                fn(t_stage[:, :, 0:P], tiles(2, F, P), ACT.Copy).then_inc(n2["turned"], 1)
            over_chunks(act, nodes2)

            act.wait_ge(n2["stored"], 32 * NCH)
            for b in range(2):
                window(2, b, b, table2)

            def rows_out(c, b, more, later):
                act.wait_ge(e2["rows"], c + 1)
                if later:
                    for g in range(G):
                        act.wait_ge(scattered[g], 16 * (c - 1))
                fn(A3[b][:, :, :], tiles(4, P), ACT.Copy).then_inc(e2["rows_out"], 1)
                if more:
                    window(2, c + 2, b, table2)

            def edges2(t, first, last):
                for b in range(2):
                    c = 2 * t + b
                    act.wait_ge(e2["pick"], c + 1)
                    if not first:
                        act.wait_ge(e2["rows"], c - 1)
                    fn(A1[b][0:W, :, 0:P], tiles(2 * b, W, P), ACT.Copy).then_inc(e2["picked"], 1)
                    if not (first and b == 0):
                        rows_out(c - 1, 1 - b, not (last and b == 1), not first)
            over_groups(act, edges2)
            rows_out(NG - 1, 1, False, True)

            def nodes3(k, first):
                act.wait_ge(n3["sum"], k + 1)
                if not first:
                    act.wait_ge(n3["turn"], k)
                fn(row_stage[:, :, :], val_stage[:, :, :], ACT.Relu).then_inc(n3["row"], 1)
                act.wait_ge(n3["turn"], k + 1)
                if not first:
                    act.wait_ge(n3["mm"], k)
                fn(z_stage[:, :, 0:P], tiles(0, F, P), ACT.Copy).then_inc(n3["turned"], 1)
                act.wait_ge(n3["mm"], k + 1)
                if not first:
                    act.wait_ge(n3["mm2"], k)
                for h in range(2):
                    fn(hid_stage[h][:, :, 0:P], tiles(2 + 2 * h, F, P), ACT.Relu, bias=c_b1[:, h:h + 1]
                       ).then_inc(n3["act"], 1)
                act.wait_ge(n3["turn2"], k + 1)
                fn(chunk_t(HT, k), tiles(6, F, P), ACT.Copy).then_inc(n3["ht"], 1)
            over_chunks(act, nodes3)

            def edges3(t, first, last):
                for b in range(2):
                    c = 2 * t + b
                    act.wait_ge(e3["msg_in"], c + 1)
                    if not first:
                        act.wait_ge(e3["agg"], c - 1)
                    fn(A3[b][:, :, :], A2[b][:, :, :], ACT.Silu).then_inc(e3["msg"], 1)
            over_groups(act, edges3)

            def nodes4(k, first):
                act.wait_ge(n4["mm"], k + 1)
                if not first:
                    act.wait_ge(n4["mm2"], k)
                fn(t_stage[:, :, 0:P], tiles(0, F, P), ACT.Silu, bias=c_sb1[:, :]).then_inc(n4["act"], 1)
            over_chunks(act, nodes4)

        @block.vector
        def _(dve):
            v = nc.vector
            ch = Chain(dve, dve_chain)
            norms = [0]

            def layer_norm(frm, to, k, per, i):
                part_from_waits(dve)
                for j in range(CH):
                    last = v.bn_stats(stats6[:, j, :], frm(j))
                ch.link(last)
                part_from_waits(dve)
                for j in range(CH):
                    last = v.bn_aggr(mean_var[:, j, :], stats6[:, j, :])
                ch.link(last)
                v.tensor_scalar(var_eps[:, :], mean_var[:, :, 1], LN_EPS, None, ALU.add).then_inc(var_ready, 1)
                dve.wait_ge(rstd_ready, k * per + (norms[0] + i + 1))
                for j in range(CH):
                    last = v.tensor_scalar(to(j), frm(j), mean_var[:, j, 0:1], rstd[:, j:j + 1],
                                           ALU.subtract, ALU.mult)
                return last

            def norm_x(k, per, i):
                return layer_norm(lambda j: X[:, bass.ds(k * CH + j, 1), :].rearrange("p a f -> p (a f)"),
                                  lambda j: HN[:, bass.ds(k * CH + j, 1), :].rearrange("p a f -> p (a f)"), k, per, i)

            def row(r):
                return r[:, None, :].to_broadcast([P, CH, F])

            def split(nodes):
                ch.link(v.tensor_scalar(part_of[:, :], nodes, HB.bit_length() - 1, None, ALU.arith_shift_right))
                ch.link(v.tensor_copy(high[:, :], part_of[:, :]))
                ch.link(v.tensor_scalar(part_of[:, :], nodes, HB - 1, None, ALU.bitwise_and))
                ch.link(v.tensor_copy(low[:, :], part_of[:, :]))

            def one_hot(to, c, values, width):
                return v.tensor_tensor(to, iota[:, None, 0:width].to_broadcast([P, G, width]),
                                       group(values, c)[:, :, None].to_broadcast([P, G, width]), ALU.is_equal)

            def histogram(s, c, b, first):
                if not first:
                    dve.wait_ge(s["hist"], c - 1)
                one_hot(HHI[b][:, :, :], c, high, NHI)
                one_hot(HLO[b][:, :, :], c, low, HB).then_inc(s["hist_in"], 1)

            def window_one_hot(s, to, c, b, read, first):
                if not first:
                    dve.wait_ge(read, c - 1)
                one_hot(to[b][:, :, :], c, dst_rel, W).then_inc(s["onehot"], 1)

            def add_window(s, c, b, none_before):
                lo = dve.value_load(winI[0:1, bass.ds(c, 1)], min_val=0, max_val=N - W)
                dve.wait_ge(s["agg"], c + 1)
                if not none_before:
                    dve.wait_ge(s["added"], c)
                v.tensor_tensor(ACC[:, bass.ds(lo, W)], ACC[:, bass.ds(lo, W)], AGG, ALU.add
                                ).then_inc(s["added"], 1)

            def source_indices(s, c, b):
                v.tensor_copy(idx[b][:, :], group(srcI, c)).then_inc(s["idx"], 1)

            dve.wait_ge(loads, 16 * n_loads)
            v.tensor_reduce(neg_min[:, :], dstI[:, :].rearrange("p (c g) -> p c g", g=G), AX.X, ALU.min, negate=True
                            ).then_inc(neg_min_ready, 1)
            dve.wait_ge(consts, n_consts)
            ch.link(v.tensor_copy(iota[:, :], iota_i[:, :]))
            ch.link(v.tensor_copy(part[:, :], part_i[:, :]))
            ch.link(v.tensor_scalar(spare_row[:, :], part[:, :], float(N), None, ALU.add))
            split(dstI[:, :])
            dve.wait_ge(neg_win_ready, 1)
            ch.link(v.tensor_scalar(neg_win[:, :], neg_win[:, :], float(W - N), None, ALU.max))
            v.tensor_scalar(winI[:, :], neg_win[0:1, :], -1.0, None, ALU.mult).then_inc(win_ready, 1)
            ch.link(v.tensor_scalar(win_node[:, :], neg_win[:, :], -1.0, part[:, :], ALU.mult, ALU.add))
            ch.link(v.tensor_tensor(dst_rel[:, :].rearrange("p (c g) -> p c g", g=G),
                                    dstI[:, :].rearrange("p (c g) -> p c g", g=G),
                                    neg_win[:, :, None].to_broadcast([P, NG, G]), ALU.add))
            dve.wait_ge(win_ready, 1)

            def tail0(k, first):
                dve.wait_ge(n0["turned"], k + 1)
                v.tensor_copy(chunk_t(HT, k), t_stage[:, :, 0:P]).then_inc(n0["ht"], 1)
                dve.wait_ge(n0["mm"], k + 1)
                if not first:
                    dve.wait_ge(n0["stored"], 32 * k)
                n = 2 * BANK_TILES
                v.tensor_copy(pq_stage[:, n:CH, :], PQ[:, n:CH, :]).then_inc(n0["q_out"], 1)

            def nodes0(k, first):
                norm_x(k, 1, 0).then_inc(n0["hn"], 1)
                tail0(k, first)
            ch.loop(0, NCH, nodes0)
            norms[0] += NCH

            dve.wait_ge(n0["stored"], 32 * NCH)
            for b in range(2):
                source_indices(e0, b, b)

            def edges0(t, first, last):
                for b in range(2):
                    c = 2 * t + b
                    dve.wait_ge(rows_in[0][b], 16 * (t + 1))
                    if not first:
                        dve.wait_ge(e0["x1_win"], c - 1)
                    v.tensor_scalar(R[b][0:W, :], DR[b], win_node[0:W, bass.ds(c, 1)], None, ALU.is_equal
                                    ).then_inc(e0["onehot_t"], 1)
                    window_one_hot(e0, OH, c, b, e0["agg"], first)
                    histogram(e0, c, b, first)
                    if not (first and b == 0):
                        add_window(e0, c - 1, 1 - b, first and b == 1)
                    if not last:
                        dve.wait_ge(gathered[0][b], 16 * G * (t + 1))
                        source_indices(e0, c + 2, b)
                    dve.wait_ge(e0["x2"], c + 1)
                    if not first:
                        dve.wait_ge(e0["g2"], c - 1)
                    v.tensor_tensor(A2[b][:, :, :], tiles(4, P), row(r_mb2), ALU.add).then_inc(e0["y2"], 1)
            over_groups(dve, edges0)
            add_window(e0, NG - 1, 1, False)

            dve.wait_ge(e0["hist"], NG + 1)
            ch.link(v.tensor_copy(hist[:, 0, :], HIST))
            ch.link(v.tensor_scalar(hist[:, 1, :], hist[:, 0, :], 1e-8, None, ALU.add))
            ch.link(v.reciprocal(hist[:, 1, :], hist[:, 1, :]))
            ch.link(v.tensor_scalar(hist[:, 2, :], hist[:, 0, :], 1.0, None, ALU.max))
            ch.link(v.reciprocal(hist[:, 2, :], hist[:, 2, :]))
            v.tensor_scalar(hist[:, 3, :], hist[:, 0, :], 1.0, None, ALU.add).then_inc(st["counted"], 1)
            split(srcI[:, :])
            dve.wait_ge(st["done"], 1)

            def nodes1(k, first):
                dve.wait_ge(n1["inp"], 32 * (k + 1))
                dve.wait_ge(n1["mm"], k + 1)
                if not first:
                    dve.wait_ge(n1["mm2"], k)
                cnt, inv = (cnt_stage[i][:, :].rearrange("p (t n) -> p t n", n=P) for i in range(2))
                agg = agg_stage[:, :, 0:P]
                ch.link(v.scalar_tensor_tensor(agg, cnt, c_mb3[:, :], tiles(0, F, P), ALU.mult, ALU.add))
                v.tensor_tensor(agg, agg, inv, ALU.mult).then_inc(n1["agg"], 1)
                dve.wait_ge(n1["mm3"], k + 1)
                y = val_stage
                v.scalar_tensor_tensor(y[:, :, :], chunk(HN, k), 0.0, tiles(4, P), ALU.max, ALU.add
                                       ).then_inc(n1["y"], 1)
                dve.wait_ge(n1["y"], k + 1)
                ch.link(v.tensor_tensor(y[:, :, :], y[:, :, :], row(r_ub2), ALU.add))
                ch.link(layer_norm(lambda j: y[:, j, :], lambda j: y[:, j, :], k, 2, 0))
                ch.link(v.tensor_tensor(y[:, :, :], y[:, :, :], row(r_gamma), ALU.mult))
                ch.link(v.tensor_tensor(y[:, :, :], y[:, :, :], row(r_beta), ALU.add))
                ch.link(v.tensor_tensor(chunk(X, k), chunk(X, k), y[:, :, :], ALU.add))
                ch.link(norm_x(k, 2, 1))
                if not first:
                    dve.wait_ge(n1["stored"], 16 * k)
                    dve.wait_ge(n1["turn"], k)
                for j in range(CH):
                    last = v.tensor_scalar(table_stage[:, j, :],
                                           HN[:, bass.ds(k * CH + j, 1), :].rearrange("p a f -> p (a f)"),
                                           0.0, tile_col(dinv1, k, j), ALU.max, ALU.mult)
                last.then_inc(n1["row"], 1)
            ch.loop(0, NCH, nodes1)
            norms[0] += 2 * NCH

            dve.wait_ge(n1["acc"], NCH)
            for b in range(2):
                source_indices(e1, b, b)

            def edges1(t, first, last):
                for b in range(2):
                    c = 2 * t + b
                    window_one_hot(e1, OH, c, b, e1["agg"], first)
                    histogram(e1, c, b, first)
                    if not (first and b == 0):
                        add_window(e1, c - 1, 1 - b, first and b == 1)
                    if not last:
                        dve.wait_ge(gathered[1][b], 16 * G * (t + 1))
                        source_indices(e1, c + 2, b)
            over_groups(dve, edges1)
            add_window(e1, NG - 1, 1, False)

            dve.wait_ge(e1["hist"], NG + 1)
            dve.wait_ge(st["stored"], 16 * 4)
            v.tensor_scalar(hist[:, 0, :], HIST, 1.0, None, ALU.add).then_inc(st["counted"], 1)
            dve.wait_ge(st["done"], 2)

            def nodes2(k, first):
                dve.wait_ge(n2["mm"], k + 1)
                if not first:
                    dve.wait_ge(n2["out"], k)
                for j in range(CH):
                    last = v.scalar_tensor_tensor(val_stage[:, j, :], tiles(0, P)[:, j, :], tile_col(dinv1, k, j),
                                                  r_gb[:, :], ALU.mult, ALU.add)
                last.then_inc(n2["v"], 1)
                dve.wait_ge(n2["v"], k + 1)
                ch.link(v.scalar_tensor_tensor(chunk(X, k), val_stage[:, :, :], 0.0, chunk(X, k), ALU.max, ALU.add))
                norm_x(k, 1, 0).then_inc(n2["hn"], 1)
                dve.wait_ge(n2["mm2"], k + 1)
                v.tensor_tensor(val_stage[:, :, :], tiles(4, P), row(r_lb), ALU.add).then_inc(n2["lin"], 1)
                dve.wait_ge(n2["lin"], k + 1)
                if not first:
                    dve.wait_ge(n2["stored"], 32 * k)
                v.tensor_tensor(table_stage[:, :, :], val_stage[:, :, :],
                                dinv2[:, bass.ds(k * CH, CH)][:, :, None].to_broadcast([P, CH, F]), ALU.mult
                                ).then_inc(n2["out"], 1)
            dve.wait_ge(n1["stored"], 16 * NCH)
            ch.loop(0, NCH, nodes2)
            norms[0] += NCH

            def edges2(t, first, last):
                for b in range(2):
                    c = 2 * t + b
                    window_one_hot(e2, OHB, c, b, e2["pick"], first)
                    dve.wait_ge(rows_in[2][b], 16 * (t + 1))
                    v.tensor_tensor(SM[b][:, :, :], SR[b].rearrange("p (g e) -> p g e", g=G),
                                    group(srcI, c)[:, :, None].to_broadcast([P, G, P]), ALU.is_equal
                                    ).then_inc(e2["same"], 1)
                    dve.wait_ge(e2["same"], c + 1)
                    ch.link(v.tensor_tensor(SE[:, :, :], SM[b][:, :, :], before[:, None, :].to_broadcast([P, G, P]),
                                            ALU.mult))
                    v.tensor_scalar(to_spare[:, :], group(srcI, c), -1.0, spare_row[:, :], ALU.mult, ALU.add)
                    ch.link(v.tensor_reduce(earlier[:, :], SE[:, :, :], AX.X, ALU.add))
                    ch.link(v.scalar_tensor_tensor(move[:, :], earlier[:, :], 0.0, to_spare[:, :], ALU.is_gt, ALU.mult))
                    if not first:
                        for g in range(G):
                            dve.wait_ge(scattered[g], 16 * (c - 1))
                    v.tensor_tensor(idx[b][:, :], group(srcI, c), move[:, :], ALU.add).then_inc(e2["idx"], 1)

            def edges2_pair(t, first):
                edges2(t, first, False)
            ch.loop(0, NG // 2, edges2_pair)

            def nodes3(k, first):
                dve.wait_ge(n3["inp"], 16 * G * (k + 1))
                s = sum_parts[0]
                for g in range(1, G):
                    ch.link(v.tensor_tensor(s, s, sum_parts[g], ALU.add))
                if not first:
                    dve.wait_ge(n3["row"], k)
                v.tensor_tensor(val_stage[:, :, :], s,
                                dinv2[:, bass.ds(k * CH, CH)][:, :, None].to_broadcast([P, CH, F]), ALU.mult
                                ).then_inc(n3["sum"], 1)
                dve.wait_ge(n3["mm2"], k + 1)
                v.tensor_tensor(chunk(HN, k), tiles(0, P), row(r_b2), ALU.add).then_inc(n3["x"], 1)
                dve.wait_ge(n3["x"], k + 1)
                ch.link(v.tensor_tensor(chunk(X, k), chunk(X, k), chunk(HN, k), ALU.add))
                ch.link(norm_x(k, 1, 0))
                if not first:
                    dve.wait_ge(n3["stored"], 16 * k)
                    dve.wait_ge(n3["turn2"], k)
                v.tensor_scalar(table_stage[:, :, :], chunk(HN, k), 0.0, None, ALU.max).then_inc(n3["out"], 1)
            dve.wait_ge(n2["stored"], 32 * NCH)
            ch.loop(0, NCH, nodes3)
            norms[0] += NCH

            dve.wait_ge(n3["acc_zero"], 1)
            for b in range(2):
                source_indices(e3, b, b)

            def edges3(t, first, last):
                for b in range(2):
                    c = 2 * t + b
                    window_one_hot(e3, OH, c, b, e3["agg"], first)
                    if not (first and b == 0):
                        add_window(e3, c - 1, 1 - b, first and b == 1)
                    dve.wait_ge(gathered[3][b], 16 * G * (t + 1))
                    if not last:
                        source_indices(e3, c + 2, b)
                    dve.wait_ge(attr_in[3][b], 16 * (t + 1))
                    if not first:
                        dve.wait_ge(e3["msg"], c - 1)
                    v.tensor_tensor(A2[b][:, :, :], GA[b], ER[b][0:P, :].rearrange("p (g f) -> p g f", f=F), ALU.add
                                    ).then_inc(e3["msg_in"], 1)
            over_groups(dve, edges3)
            add_window(e3, NG - 1, 1, False)

            dve.wait_ge(n3["ht"], NCH)
            dve.wait_ge(e3["added"], NG)

            def nodes4(k, first):
                dve.wait_ge(n4["inp"], 16 * (k + 1))
                if not first:
                    dve.wait_ge(n4["mm"], k)
                hh = agg_stage[:, :, 0:P]
                ch.link(v.tensor_tensor(hh, chunk_t(ACC, k), cnt_stage[0][:, :].rearrange("p (t n) -> p t n", n=P),
                                        ALU.mult))
                v.tensor_tensor(hh, hh, chunk_t(HT, k), ALU.add).then_inc(n4["hh"], 1)
                dve.wait_ge(n4["mm2"], k + 1)
                y = val_stage[:, :, :]
                if not first:
                    dve.wait_ge(n4["out"], k)
                v.scalar_tensor_tensor(y, chunk(HN, k), 0.0, tiles(2, P), ALU.max, ALU.add).then_inc(n4["y"], 1)
                dve.wait_ge(n4["y"], k + 1)
                ch.link(v.tensor_tensor(y, y, row(r_sb2), ALU.add))
                v.tensor_tensor(chunk(X, k), chunk(X, k), y, ALU.add).then_inc(n4["out"], 1)
            ch.loop(0, NCH, nodes4)

        @block.tensor
        def _(pe):
            mm = nc.tensor.matmul

            def wide(bank, lhsT, rhs, start, stop):
                o = tiles(bank, F, P)
                mm(o[:, 0:4, :], lhsT, rhs[:, 0:4, :], start=start, stop=stop)
                return mm(o[:, 4, :], lhsT, rhs[:, 4, :], start=start, stop=stop)

            def per_tile(bank, stage, rhs):
                for j in range(CH):
                    last = mm(tiles(bank, P)[:, j, :], stage[:, j, 0:P], rhs, start=True, stop=True)
                return last

            def turn(bank, stage):
                for j in range(CH):
                    last = mm(tiles(bank, F, P)[:, j, :], stage[:, j, :], ident[0:P, 0:P], start=True, stop=True)
                return last

            def histogram(s, c, b):
                pe.wait_ge(s["hist_in"], c + 1)
                for g in range(G):
                    last = mm(HIST, HHI[b][:, g, :], HLO[b][:, g, :], start=False, stop=False)
                last.then_inc(s["hist"], 1)

            def histogram_edge(s, start):
                last = mm(HIST, zeros16[:, 0:NHI], zeros16[:, :], start=start, stop=not start)
                if not start:
                    last.then_inc(s["hist"], 1)

            def aggregate(s, c, b, rows, none_before):
                pe.wait_ge(s["onehot"], c + 1)
                if not none_before:
                    pe.wait_ge(s["added"], c)
                for g in range(G):
                    last = mm(AGG, rows[:, g, :], OH[b][:, g, :], start=(g == 0), stop=(g == G - 1))
                last.then_inc(s["agg"], 1)

            pe.wait_ge(loads, 16 * n_loads)
            pe.wait_ge(consts, n_consts)

            def nodes0(k, first):
                pe.wait_ge(n0["row"], k + 1)
                if not first:
                    pe.wait_ge(n0["turned"], k)
                turn(0, row_stage).then_inc(n0["turn"], 1)
                pe.wait_ge(n0["turned"], k + 1)
                if not first:
                    pe.wait_ge(n0["p_out"], k)
                    pe.wait_ge(n0["q_out"], k)
                for j in range(CH):
                    last = mm(PQ[:, j, :], t_stage[:, j, 0:P], w_pq[:, :], start=True, stop=True)
                last.then_inc(n0["mm"], 1)
            over_chunks(pe, nodes0)

            pe.wait_ge(n0["ht"], NCH)
            pe.wait_ge(n0["q_out"], NCH)
            pe.wait_ge(n0["p_out"], NCH)
            histogram_edge(e0, True)

            def edges0(t, first, last):
                for b in range(2):
                    c = 2 * t + b
                    pe.wait_ge(e0["onehot_t"], c + 1)
                    pe.wait_ge(attr_in[0][b], 16 * (t + 1))
                    pe.wait_ge(window_in[0][b], 16 * (t + 1))
                    if not first:
                        pe.wait_ge(e0["g1"], c - 1)
                    wide(2 * b, L[b][:, :], R[b][:, :].rearrange("p (g e) -> p g e", g=G), True, False
                         ).then_inc(e0["x1_win"], 1)
                    histogram(e0, c, b)
                    if not (first and b == 0):
                        pe.wait_ge(e0["g2"], c)
                        aggregate(e0, c - 1, 1 - b, A3[1 - b], first and b == 1)
                    pe.wait_ge(gathered[0][b], 16 * G * (t + 1))
                    for g in range(G):
                        last_mm = mm(tiles(2 * b, F, P)[:, g, :], GA[b][:, g, :], ident[0:P, 0:P],
                                     start=False, stop=g >= 3)
                    last_mm.then_inc(e0["x1"], 1)
                    pe.wait_ge(e0["g1"], c + 1)
                    if not (first and b == 0):
                        pe.wait_ge(e0["y2"], c)
                    per_tile(4, A1[b], w_m2[:, :]).then_inc(e0["x2"], 1)
            over_groups(pe, edges0)
            pe.wait_ge(e0["g2"], NG)
            aggregate(e0, NG - 1, 1, A3[1], False)
            histogram_edge(e0, False)
            pe.wait_ge(st["loaded"], 16)
            mm(TURNED, stat_rows[:, :], ident[0:NT, 0:NT], start=True, stop=True).then_inc(st["turned"], 1)

            pe.wait_ge(e0["added"], NG)

            def nodes1(k, first):
                if not first:
                    pe.wait_ge(n1["acc"], k)
                wide(0, w_m3[:, :], chunk_t(ACC, k), True, True).then_inc(n1["mm"], 1)
                if not first:
                    pe.wait_ge(n1["act"], k)
                wide(2, w_uh[:, :], chunk_t(HT, k), True, False)
                pe.wait_ge(n1["agg"], k + 1)
                wide(2, w_ua[:, :], agg_stage[:, :, 0:P], False, True).then_inc(n1["mm2"], 1)
                pe.wait_ge(n1["act"], k + 1)
                if not first:
                    pe.wait_ge(n1["y"], k)
                per_tile(4, t_stage, w_u2[:, :]).then_inc(n1["mm3"], 1)
                pe.wait_ge(n1["row"], k + 1)
                turn(0, table_stage).then_inc(n1["turn"], 1)
            over_chunks(pe, nodes1)

            pe.wait_ge(st["done"], 1)
            histogram_edge(e1, True)

            def edges1(t, first, last):
                for b in range(2):
                    c = 2 * t + b
                    histogram(e1, c, b)
                    pe.wait_ge(gathered[1][b], 16 * G * (t + 1))
                    aggregate(e1, c, b, GA[b], first and b == 0)
            over_groups(pe, edges1)
            histogram_edge(e1, False)
            pe.wait_ge(st["loaded"], 32)
            mm(TURNED, stat_rows[:, :], ident[0:NT, 0:NT], start=True, stop=True).then_inc(st["turned"], 1)

            def nodes2(k, first):
                pe.wait_ge(n2["acc_cp"], k + 1)
                if not first:
                    pe.wait_ge(n2["v"], k)
                per_tile(0, agg_stage, w_g[:, :]).then_inc(n2["mm"], 1)
                pe.wait_ge(n2["row"], k + 1)
                if not first:
                    pe.wait_ge(n2["turned"], k)
                turn(2, row_stage).then_inc(n2["turn"], 1)
                pe.wait_ge(n2["turned"], k + 1)
                if not first:
                    pe.wait_ge(n2["lin"], k)
                per_tile(4, t_stage, w_lin[:, :]).then_inc(n2["mm2"], 1)
            over_chunks(pe, nodes2)

            def rows(c, b, t, none_before):
                pe.wait_ge(e2["picked"], c + 1)
                pe.wait_ge(window_in[2][b], 16 * (t + 1))
                if not none_before:
                    pe.wait_ge(e2["rows_out"], c)
                for g in range(G):
                    last = mm(tiles(4, P)[:, g, :], A1[b][0:W, g, 0:P], L[b][0:W, :], start=True, stop=True)
                last.then_inc(e2["rows"], 1)

            pe.wait_ge(n2["lin"], NCH)

            def edges2(t, first, last):
                for b in range(2):
                    c = 2 * t + b
                    pe.wait_ge(e2["onehot"], c + 1)
                    pe.wait_ge(e2["same"], c + 1)
                    if not first:
                        pe.wait_ge(e2["picked"], c - 1)
                    for g in range(G):
                        last_mm = mm(tiles(2 * b, W, P)[:, g, :], OHB[b][:, g, :], SM[b][:, g, :], start=True, stop=True)
                    last_mm.then_inc(e2["pick"], 1)
                    if not (first and b == 0):
                        rows(c - 1, 1 - b, t - (1 - b), first and b == 1)
            over_groups(pe, edges2)
            rows(NG - 1, 1, NG // 2 - 1, False)

            pe.wait_ge(e2["rows_out"], NG)
            pe.wait_ge(e2["picked"], NG)

            def nodes3(k, first):
                pe.wait_ge(n3["row"], k + 1)
                if not first:
                    pe.wait_ge(n3["x"], k)
                turn(0, row_stage).then_inc(n3["turn"], 1)
                pe.wait_ge(n3["turned"], k + 1)
                if not first:
                    pe.wait_ge(n3["act"], 2 * k)
                wide(2, w_z1[:, 0:F], z_stage[:, :, 0:P], True, True)
                wide(4, w_z1[:, F:2 * F], z_stage[:, :, 0:P], True, True).then_inc(n3["mm"], 1)
                pe.wait_ge(n3["act"], 2 * k + 2)
                for j in range(CH):
                    for h in range(2):
                        last = mm(tiles(0, P)[:, j, :], hid_stage[h][:, j, 0:P], w_z2[:, h, :],
                                  start=(h == 0), stop=(h == 1))
                last.then_inc(n3["mm2"], 1)
                pe.wait_ge(n3["out"], k + 1)
                if not first:
                    pe.wait_ge(n3["ht"], k)
                turn(6, table_stage).then_inc(n3["turn2"], 1)
            over_chunks(pe, nodes3)

            pe.wait_ge(n3["ht"], NCH)

            def edges3(t, first, last):
                for b in range(2):
                    c = 2 * t + b
                    pe.wait_ge(e3["msg"], c + 1)
                    aggregate(e3, c, b, A3[b], first and b == 0)
            over_groups(pe, edges3)

            pe.wait_ge(n3["x"], NCH)

            def nodes4(k, first):
                pe.wait_ge(n4["hh"], k + 1)
                if not first:
                    pe.wait_ge(n4["act"], k)
                wide(0, w_s1[:, :], agg_stage[:, :, 0:P], True, True).then_inc(n4["mm"], 1)
                pe.wait_ge(n4["act"], k + 1)
                if not first:
                    pe.wait_ge(n4["y"], k)
                per_tile(2, t_stage, w_s2[:, :]).then_inc(n4["mm2"], 1)
            over_chunks(pe, nodes4)


_PLAIN = ["L0_gnn_mW1", "L0_gnn_mb1", "L0_gnn_mW2", "L0_gnn_mb2", "L0_gnn_mW3", "L0_gnn_mb3", "L0_gnn_uW1",
          "L0_gnn_ub1", "L0_gnn_uW2", "L0_gnn_ub2", "L0_gnn_gamma", "L0_gnn_beta", "L1_gnn_W", "L1_gnn_b",
          "L2_gnn_lin_w", "L2_gnn_lin_b", "L2_gnn_w1", "L2_gnn_b1", "L2_gnn_w2", "L2_gnn_b2", "L3_gnn_W1",
          "L3_gnn_b1", "L3_gnn_W2", "L3_gnn_b2"]


def kernel(**inputs):
    import numpy as np
    import concourse.bacc as bacc
    from concourse.bass_utils import run_bass_kernel_spmd

    a = {n: np.ascontiguousarray(inputs[n]) for n in inputs}
    by_partition = {n: a[n].reshape(NG, P, G).transpose(1, 0, 2).reshape(P, NG * G) for n in ("src", "dst")}
    by_tile = {n: a[n].reshape(NG, P, G).transpose(0, 2, 1).reshape(NG, G * P) for n in ("src", "dst")}
    edge_attr_64_t = a["edge_attr_64"].reshape(NG, P, G, FE).transpose(0, 3, 2, 1).reshape(NG * FE, G * P)
    laid = [("x", a["x"]), ("src_g", by_partition["src"]), ("dst_g", by_partition["dst"]),
            ("src_rows", by_tile["src"]), ("dst_rows", by_tile["dst"]),
            ("edge_attr_128", a["edge_attr_128"]), ("edge_attr_64_t", edge_attr_64_t)]
    laid += [(n, a[n]) for n in _PLAIN]

    nc = bacc.Bacc("TRN2", target_bir_lowering=False, num_devices=1)
    arrays, args = {}, []
    for name, v in laid:
        v = np.ascontiguousarray(v)
        arrays[f"in_{name}"] = v
        args.append(nc.dram_tensor(f"in_{name}", v.shape, mybir.dt.from_np(v.dtype), kind="ExternalInput").ap())
    args.append(nc.dram_tensor("out_x", (N, F), F32, kind="ExternalOutput").ap())
    gnn_kernel(nc, *args)
    r = run_bass_kernel_spmd(nc, [arrays], core_ids=[0])
    return r.results[0]["out_x"]
```

```python
from contextlib import ExitStack

import concourse.bass as bass
from concourse import mybir
from concourse.alu_op_type import AluOpType as ALU

F32 = mybir.dt.float32
BF16 = mybir.dt.bfloat16
I32 = mybir.dt.int32
ACT = mybir.ActivationFunctionType
AX = mybir.AxisListType
RMAX = bass.bass_isa.ReduceOp.max

N = 6250
E = 106250
F = 128
FE = 64
P = 125
G = 5
NG = E // (P * G)
W = 64
CH = 5
NT = N // P
NCH = NT // CH
CN = CH * P
HB = 128
NHI = (N + HB - 1) // HB
NWIN = (N + W - 1) // W
NPAD = NWIN * W
SWEEPS = NWIN
LN_EPS = 1e-5



class Steps:

    def __init__(self, sem, **counts):
        self.sem, self.total, self.until = sem, 0, {}
        for step, count in counts.items():
            self.total += count
            self.until[step] = self.total

    def begin(self, n):
        return (n - 1) * self.total + 1

    def after(self, step, n):
        return (n - 1) * self.total + 1 + self.until[step]


class Chain:

    def __init__(self, eng, sem):
        self.eng, self.sem, self.n = eng, sem, 0

    def link(self, instruction):
        self.n += 1
        instruction.then_inc(self.sem, 1)
        self.eng.wait_ge(self.sem, self.n)


def gnn_kernel(nc, x, src_g, dst_g, src_rows, dst_rows, edge_attr_128, edge_attr_64_t,
               mW1, mb1, mW2, mb2, mW3, mb3, uW1, ub1, uW2, ub2, gamma, beta,
               gW, gb, lin_w, lin_b, w1, b1, w2, b2, sW1, sb1, sW2, sb2, out):
    ctx = ExitStack()
    with ctx:
        def sb(name, shape, dt=F32):
            return ctx.enter_context(nc.sbuf_tensor(name, shape, dt))

        def sem(name):
            return ctx.enter_context(nc.semaphore(name))

        def dram(name, shape):
            return nc.dram_tensor(name, shape, F32).ap()

        src_table0 = dram("src_table0", (N, F))
        dst_table0 = dram("dst_table0", (NPAD, F))
        table1 = dram("table1", (N, F))
        table2 = dram("table2", (NPAD, F))
        table3 = dram("table3", (N, F))
        sums = [dram(f"sums{g}", (N + P, F)) for g in range(G)]
        stats = dram("stats", (5, NHI * HB))

        X = sb("X", [P, NT, F])
        H = sb("H", [P, NT, F])
        HT = sb("HT", [F, N])
        ACC = sb("ACC", [F, NPAD])
        srcI = sb("srcI", [P, NG * G], I32)
        dstI = sb("dstI", [P, NG * G], I32)
        dst_rel = sb("dst_rel", [P, NG * G])
        high = sb("high", [P, NG * G])
        low = sb("low", [P, NG * G])
        part_of = sb("part_of", [P, NG * G], I32)
        neg_min = sb("neg_min", [P, NG])
        neg_win = sb("neg_win", [P, NG])
        win_node = sb("win_node", [P, NG])
        winI = sb("winI", [1, NG], I32)
        left = sb("left", [P, NG * G])
        left_most = sb("left_most", [P, 2])
        leftI = sb("leftI", [1, 1], I32)
        ident = sb("ident", [F, F])
        before = sb("before", [P, P], BF16)
        iota_i = sb("iota_i", [P, F], I32)
        iota = sb("iota", [P, F])
        part_i = sb("part_i", [P, 1], I32)
        part = sb("part", [P, 1])
        spare_row = sb("spare_row", [P, 1])
        neg_half = sb("neg_half", [P, HB])
        zeros = sb("zeros", [P, CH * F])
        zeros16 = sb("zeros16", [P, HB], BF16)
        ones_row = sb("ones_row", [1, P])
        sweep_i = sb("sweep_i", [P, NWIN], I32)
        sweep_win = sb("sweep_win", [P, NWIN])
        sweep_node = sb("sweep_node", [P, NWIN])
        w_pq = sb("w_pq", [F, 2 * F])
        w_m2, w_m3 = sb("w_m2", [F, F]), sb("w_m3", [F, F])
        w_uh, w_ua, w_u2 = sb("w_uh", [F, F]), sb("w_ua", [F, F]), sb("w_u2", [F, F])
        w_g, w_lin = sb("w_g", [F, F]), sb("w_lin", [F, F])
        w_z1, w_z2 = sb("w_z1", [F, 2 * F]), sb("w_z2", [F, 2, F])
        w_s1, w_s2 = sb("w_s1", [F, F]), sb("w_s2", [F, F])
        c_mb1, c_mb3, c_ub1, c_sb1 = (sb(n, [F, 1]) for n in ("c_mb1", "c_mb3", "c_ub1", "c_sb1"))
        c_b1 = sb("c_b1", [F, 2])
        r_mb2, r_gamma, r_beta, r_gb = (sb(n, [P, F]) for n in ("r_mb2", "r_gamma", "r_beta", "r_gb"))
        o_ub2, o_lb, o_b2, o_sb2 = (sb(n, [1, CH, F]) for n in ("o_ub2", "o_lb", "o_b2", "o_sb2"))
        hist = sb("hist", [NHI, 4, HB])
        stat_rows = sb("stat_rows", [NT, P])
        dinv1 = sb("dinv1", [P, NT])
        dinv2 = sb("dinv2", [P, NT])
        idx = [sb(f"idx{b}", [P, G], I32) for b in range(2)]
        GA_all = sb("GA_all", [P, 2, G, F])
        GA = [GA_all[:, b] for b in range(2)]
        ER = [sb(f"ER{b}", [F, G * F]) for b in range(2)]
        DR = [ER[b][0:W, 0:G * P].bitcast(I32) for b in range(2)]
        SR = [ER[b][0:P, 0:G * P].bitcast(I32) for b in range(2)]
        R = [sb(f"R{b}", [F, G * P]) for b in range(2)]
        L = [sb(f"L{b}", [F, F]) for b in range(2)]
        OH = [sb(f"OH{b}", [P, G, W]) for b in range(2)]
        OHB = [sb(f"OHB{b}", [P, G, W], BF16) for b in range(2)]
        HHI = [sb(f"HHI{b}", [P, G, NHI], BF16) for b in range(2)]
        HLO = [sb(f"HLO{b}", [P, G, HB], BF16) for b in range(2)]
        A1 = [sb(f"A1_{b}", [F, G, F]) for b in range(2)]
        A2 = [sb(f"A2_{b}", [P, G, F]) for b in range(2)]
        A3f = [sb(f"A3_{b}", [F, G, F]) for b in range(2)]
        A3 = [A3f[b][0:P] for b in range(2)]
        SM = [sb(f"SM{b}", [P, G, P], BF16) for b in range(2)]
        SE = sb("SE", [P, G, P], BF16)
        earlier = sb("earlier", [P, G])
        to_spare = sb("to_spare", [P, G])
        move = sb("move", [P, G])
        left_rel = sb("left_rel", [P, G])
        LN = [{"six": sb(f"ln_six{i}", [P, CH, 6]), "mv": sb(f"ln_mv{i}", [P, CH, 2]),
               "var": sb(f"ln_var{i}", [P, CH]), "root": sb(f"ln_root{i}", [P, CH]),
               "scale": sb(f"ln_scale{i}", [P, CH]), "shift": sb(f"ln_shift{i}", [P, CH])} for i in range(2)]
        row_stage, val_stage = A2[0], A2[1]
        table_stage = sb("table_stage", [P, CH, F])
        zero_rows = sb("zero_rows", [NPAD - N, F])
        pq_stage = GA_all[:, :, :, :].rearrange("p a g f -> p (a g f)").rearrange("p (g f) -> p g f", f=2 * F)
        t_stage, agg_stage = A1[0], A1[1]
        z_stage = ER[1][:, :].rearrange("p (g f) -> p g f", f=F)
        hid_stage = A3f
        cnt_stage = R
        sum_parts = [GA[0], GA[1], A1[0][0:P], A1[1][0:P], ER[0][0:P, :].rearrange("p (g f) -> p g f", f=F)]

        PS = ctx.enter_context(nc.psum_tensor("PS", [F, 8 * 512], F32))

        def tiles(bank, rows, inner=F):
            return PS[0:rows, bank * 512:bank * 512 + G * F].rearrange("p (g f) -> p g f", f=F)[:, :, 0:inner]

        IN_BANK = 512 // F
        BANK_TILES = 512 // (2 * F)
        PQ = PS[0:P, 2 * 512:2 * 512 + CH * 2 * F].rearrange("p (g f) -> p g f", f=2 * F)
        AGG = PS[:, 6 * 512:6 * 512 + W]
        HIST = PS[0:NHI, 7 * 512:7 * 512 + HB]
        TURNED = PS[0:P, 7 * 512 + HB:7 * 512 + HB + NT]

        def sems(prefix, names):
            return {n: sem(f"{prefix}_{n}") for n in names.split()}

        def slot_sems(prefix):
            return [sem(f"{prefix}{b}") for b in range(2)]

        idx_in, x_in, first_in, loads = sem("idx_in"), sem("x_in"), sem("first_in"), sem("loads")
        consts, zeroed, pads_zeroed = sem("consts"), sem("zeroed"), sem("pads_zeroed")
        waits_passed = sem("waits_passed")
        pool_chain, dve_chain = sem("pool_chain"), sem("dve_chain")
        neg_min_ready, neg_win_ready, win_ready = sem("neg_min_ready"), sem("neg_win_ready"), sem("win_ready")
        most_ready, most_everywhere, left_ready = sem("most_ready"), sem("most_everywhere"), sem("left_ready")
        st = sems("st", "counted rooted stored loaded turned done")
        e0 = sems("e0", "idx onehot onehot_t hist_in hist x1_win x1 g1 x2 y2 g2 agg added")
        e1 = sems("e1", "idx onehot hist_in hist agg added")
        e2 = sems("e2", "idx onehot same first_of pick picked rows rows_out earlier move")
        e3 = sems("e3", "idx onehot msg_in msg agg added")
        acc_done = [sem(f"acc_done{i}") for i in range(4)]
        gathered, attr_in, rows_in, window_in = (slot_sems(n) for n in ("gathered", "attr_in", "rows_in", "window_in"))
        PASS = NG // 2
        scattered = [sem(f"scattered{g}") for g in range(G)]
        x0 = Steps(sem("general0"), rel=1, masks=2, loaded=16 * (3 + G), masks_t=1, x1=1, g1=1, x2=1, y2=1, g2=1,
                   agg=1, added=1)
        x1 = Steps(sem("general1"), rel=1, masks=2, gathered=16 * G, agg=1, added=1)
        x2 = Steps(sem("general2"), loaded=16 * 2, rel=1, masks=2, first_of=2, earlier=1, move=1, idx=1, pick=1,
                   picked=1, rows=1, rows_out=1, sent=16 * G)
        x3 = Steps(sem("general3"), rel=1, masks=2, loaded=16 * (1 + G), msg_in=1, msg=1, agg=1, added=1)
        ln = sems("ln", "six mv var root scale shift applied")

        def after_norms(phases, s):
            return {**s, "before": phases * NCH}
        n0 = after_norms(0, sems("n0", "kept beta turn turned ht mm p_out q_out stored"))
        n1a = sems("n1a", "inp mm agg1 agg mm2 act mm3 y")
        n1b = after_norms(1, sems("n1b", "scaled x"))
        n1c = after_norms(2, sems("n1c", "turn acc stored"))
        n2 = after_norms(3, sems("n2", "acc_cp mm v x turn turned mm2 out stored"))
        n3 = after_norms(4, sems("n3", "inp s1 s2 s3 s4 sum row turn turned mm act mm2 x h_added stored turn2 ht acc_zero"))
        n4 = sems("n4", "inp hh1 hh mm act mm2 out stored")

        def first_weights():
            yield w_pq[:, 0:F], mW1[0:F, :]
            yield w_pq[:, F:2 * F], mW1[F:2 * F, :]
            yield r_beta[:, :], beta.rearrange("(a f) -> a f", a=1).to_broadcast([P, F])

        def weights():
            for b in range(2):
                yield L[b][W:F, :], mW1[2 * F:2 * F + FE, :]
            yield w_m2[:, :], mW2
            yield w_m3[:, :], mW3
            yield w_uh[:, :], uW1[0:F, :]
            yield w_ua[:, :], uW1[F:2 * F, :]
            yield w_u2[:, :], uW2
            yield w_g[:, :], gW
            yield w_lin[:, :], lin_w
            yield w_z1[:, :], w1
            for h in range(2):
                yield w_z2[:, h, :], w2[h * F:(h + 1) * F, :]
            yield w_s1[:, :], sW1
            yield w_s2[:, :], sW2
            for col, v in ((c_mb1, mb1), (c_mb3, mb3), (c_ub1, ub1), (c_sb1, sb1)):
                yield col[:, :], v.rearrange("(p a) -> p a", a=1)
            for h in range(2):
                yield c_b1[:, h:h + 1], b1[h * F:(h + 1) * F].rearrange("(p a) -> p a", a=1)
            for row, v in ((r_mb2, mb2), (r_gamma, gamma), (r_gb, gb)):
                yield row[:, :], v.rearrange("(a f) -> a f", a=1).to_broadcast([P, F])
            for row, v in ((o_ub2, ub2), (o_lb, lin_b), (o_b2, b2), (o_sb2, sb2)):
                yield row[:, :, :], v.rearrange("(a t f) -> a t f", a=1, t=1).to_broadcast([1, CH, F])

        N_LOADS = 16 * len(list(weights()))
        N_CONSTS = 11

        def node_rows(t, k):
            return t[bass.ds(k * CN, CN), :].rearrange("(t p) f -> p t f", p=P)

        def chunk(buf, k):
            return buf[:, bass.ds(k * CH, CH), :]

        def tile_of(buf, k, j):
            return buf[:, bass.ds(k * CH + j, 1), :].rearrange("p a f -> p (a f)")

        def chunk_t(buf, k):
            return buf[:, bass.ds(k * CN, CN)].rearrange("p (t n) -> p t n", n=P)

        def chunk_cols(buf, k):
            return buf[:, bass.ds(k * CH, CH)][:, :, None].to_broadcast([P, CH, F])

        def group(buf, c):
            return buf[:, bass.ds(c * G, G)]

        def over_groups(eng, body):
            body(0, True, False)
            with eng.Fori(1, NG // 2 - 1) as t:
                body(t, False, False)
            body(NG // 2 - 1, False, True)

        def over_chunks(eng, *stages):
            most = max(lag for lag, _ in stages)

            def a_round(i, outside):
                for lag, stage in stages:
                    if not outside:
                        stage(i - lag, False)
                    elif 0 <= i - lag < NCH:
                        stage(i - lag, i == lag)
            for i in range(most + 1):
                a_round(i, True)
            with eng.Fori(most + 1, NCH) as i:
                a_round(i, False)
            for i in range(NCH, NCH + most):
                a_round(i, True)

        def part_from_waits(eng):
            eng.sem_inc(waits_passed, 1)

        def general_path(eng, body):
            eng.wait_ge(left_ready, 1)
            any_left = eng.value_load(leftI[0:1, 0:1], min_val=0, max_val=1)
            with eng.If(any_left > 0):
                with eng.Fori(0, SWEEPS) as s:
                    with eng.Fori(0, NG) as c:
                        body(s, c, s * NG + c + 1)

        block = ctx.enter_context(nc.Block())

        @block.sync
        def _(sp):
            sp.dma_start(dstI[:, :], dst_g).then_inc(idx_in, 16)
            sp.dma_start(srcI[:, :], src_g).then_inc(idx_in, 16)
            with sp.Fori(0, NCH) as k:
                sp.dma_start(chunk(X, k), node_rows(x, k)).then_inc(x_in, 16)
            for to, frm in first_weights():
                sp.dma_start(to, frm).then_inc(first_in, 16)
            for to, frm in weights():
                sp.dma_start(to, frm).then_inc(loads, 16)

            def nodes0(k, first):
                sp.wait_ge(n0["p_out"], k + 1)
                sp.wait_ge(n0["q_out"], k + 1)
                sp.dma_start(node_rows(src_table0, k), pq_stage[:, :, 0:F]).then_inc(n0["stored"], 16)
                sp.dma_start(node_rows(dst_table0, k), pq_stage[:, :, F:2 * F]).then_inc(n0["stored"], 16)
            over_chunks(sp, (0, nodes0))

            def load0(c, b, rows_sem, attr_sem):
                sp.dma_start(DR[b], dst_rows[bass.ds(c, 1), :].to_broadcast([W, G * P])).then_inc(rows_sem, 16)
                sp.dma_start(R[b][W:F, :], edge_attr_64_t[bass.ds(c * FE, FE), :]).then_inc(attr_sem, 16)

            def edges0(t, first, last):
                for b in range(2):
                    c = 2 * t + b
                    if not first:
                        sp.wait_ge(e0["onehot_t"], c - 1)
                        sp.wait_ge(e0["x1_win"], c - 1)
                    load0(c, b, rows_in[b], attr_in[b])
            over_groups(sp, edges0)

            def general0(s, c, n):
                sp.wait_ge(x0.sem, x0.after("masks", n))
                load0(c, 0, x0.sem, x0.sem)
            general_path(sp, general0)

            def store_stats(rows, n):
                for i, r in enumerate(rows):
                    sp.dma_start(stats[r:r + 1, :].rearrange("a (h l) -> (a h) l", l=HB),
                                 hist[:, i, :]).then_inc(st["stored"], 16)
                sp.wait_ge(st["stored"], 16 * n)
                r = rows[-1]
                sp.dma_start(stat_rows[:, :], stats[r:r + 1, 0:N].rearrange("a (t p) -> (a t) p", p=P)
                             ).then_inc(st["loaded"], 16)
            sp.wait_ge(st["rooted"], 1)
            store_stats((0, 1, 2, 3), 4)

            sp.wait_ge(acc_done[0], 1)

            def counts1(k, first):
                if not first:
                    sp.wait_ge(n1a["agg"], k)
                for i in range(2):
                    sp.dma_start(cnt_stage[i][:, :], stats[i:i + 1, bass.ds(k * CN, CN)].to_broadcast([F, CN])
                                 ).then_inc(n1a["inp"], 16)
            over_chunks(sp, (0, counts1))

            def table1_out(k, first):
                sp.wait_ge(ln["applied"], n1c["before"] + k + 1)
                sp.dma_start(node_rows(table1, k), table_stage[:, :, :]).then_inc(n1c["stored"], 16)
            over_chunks(sp, (0, table1_out))

            for g in range(G):
                if g:
                    with sp.Fori(0, NCH) as k:
                        sp.dma_start(node_rows(sums[g], k),
                                     zeros[:, :].rearrange("p (t f) -> p t f", f=F)).then_inc(zeroed, 16)
                sp.dma_start(sums[g][N:N + P, :], zeros[:, 0:F]).then_inc(zeroed, 16)
            sp.wait_ge(st["rooted"], 2)
            store_stats((4,), 5)

            def nodes2(k, first):
                sp.wait_ge(n2["out"], k + 1)
                sp.dma_start(node_rows(table2, k), table_stage[:, :, :]).then_inc(n2["stored"], 16)
                sp.dma_start(node_rows(sums[0], k), table_stage[:, :, :]).then_inc(n2["stored"], 16)
            over_chunks(sp, (0, nodes2))

            def load2(c, b, rows_sem):
                sp.dma_start(SR[b], src_rows[bass.ds(c, 1), :].to_broadcast([P, G * P])).then_inc(rows_sem, 16)

            def edges2(t, first, last):
                for b in range(2):
                    c = 2 * t + b
                    if not first:
                        sp.wait_ge(e2["same"], c - 1)
                    load2(c, b, rows_in[b])
            over_groups(sp, edges2)

            def general2(s, c, n):
                sp.wait_ge(x2.sem, x2.begin(n))
                load2(c, 0, x2.sem)
            general_path(sp, general2)
            sp.wait_ge(acc_done[2], 1)

            def sums3(k, first):
                if not first:
                    sp.wait_ge(n3["sum"], k)
                for g in range(G):
                    sp.dma_start(sum_parts[g], node_rows(sums[g], k)).then_inc(n3["inp"], 16)

            def table3_out(k, first):
                sp.wait_ge(ln["applied"], n3["before"] + k + 1)
                sp.dma_start(node_rows(table3, k), table_stage[:, :, :]).then_inc(n3["stored"], 16)
            over_chunks(sp, (0, sums3), (2, table3_out))

            sp.wait_ge(n3["mm"], NCH)

            def load3(c, b, attr_sem):
                sp.dma_start(ER[b][0:P, :], edge_attr_128[bass.ds(c * P * G, P * G), :]
                             .rearrange("(p g) f -> p (g f)", g=G)).then_inc(attr_sem, 16)

            def edges3(t, first, last):
                for b in range(2):
                    c = 2 * t + b
                    if not first:
                        sp.wait_ge(e3["msg_in"], c - 1)
                    load3(c, b, attr_in[b])
            over_groups(sp, edges3)

            def general3(s, c, n):
                sp.wait_ge(x3.sem, x3.after("masks", n))
                load3(c, 0, x3.sem)
            general_path(sp, general3)

            def counts4(k, first):
                if not first:
                    sp.wait_ge(n4["hh1"], k)
                sp.dma_start(cnt_stage[0][:, :], stats[2:3, bass.ds(k * CN, CN)].to_broadcast([F, CN])
                             ).then_inc(n4["inp"], 16)

            def result(k, first):
                sp.wait_ge(n4["out"], k + 1)
                sp.dma_start(node_rows(out, k), chunk(X, k)).then_inc(n4["stored"], 16)
            over_chunks(sp, (0, counts4), (2, result))
            sp.wait_ge(n4["stored"], 16 * NCH)
            sp.wait_ge(pads_zeroed, 16)

        @block.gpsimd
        def _(pool):
            ch = Chain(pool, pool_chain)
            pool.iota(iota_i[:, :], pattern=[[1, F]], base=0, channel_multiplier=0).then_inc(consts, 1)
            pool.iota(part_i[:, :], pattern=[[0, 1]], base=0, channel_multiplier=1).then_inc(consts, 1)
            pool.iota(sweep_i[:, :], pattern=[[W, NWIN]], base=0, channel_multiplier=0).then_inc(consts, 1)
            pool.memset(neg_half[:, :], -0.5).then_inc(consts, 1)
            ch.link(pool.memset(ident[:, :], 0.0))
            ch.link(pool.memset(before[:, :], 1.0))
            pool.affine_select(out=ident[:, :], in_=ident[:, :], compare_op=ALU.not_equal, fill=1.0, base=0,
                               pattern=[[-1, F]], channel_multiplier=1).then_inc(consts, 1)
            pool.affine_select(out=before[:, :], in_=before[:, :], compare_op=ALU.is_gt, fill=0.0, base=0,
                               pattern=[[-1, P]], channel_multiplier=1).then_inc(consts, 1)
            pool.memset(ones_row[:, :], 1.0).then_inc(consts, 1)
            pool.memset(zeros16[:, :], 0.0).then_inc(consts, 1)
            pool.memset(zeros[:, :], 0.0).then_inc(consts, 1)
            pool.memset(ACC[:, :], 0.0).then_inc(consts, 1)
            pool.memset(zero_rows[:, :], 0.0).then_inc(consts, 1)
            pool.wait_ge(neg_min_ready, 1)
            pool.partition_all_reduce(neg_win[:, :], neg_min[:, :], P, RMAX).then_inc(neg_win_ready, 1)
            pool.wait_ge(most_ready, 1)
            pool.partition_all_reduce(left_most[:, 1:2], left_most[:, 0:1], P, RMAX).then_inc(most_everywhere, 1)

            def inverse_root(s, i):
                def stage(k, first):
                    pool.wait_ge(ln["var"], s["before"] + k + 1)
                    if not first:
                        pool.wait_ge(ln["applied"], s["before"] + k)
                    pool.tensor_tensor(LN[i]["root"][:, :], LN[i]["var"][:, :], neg_half[:, 0:CH], ALU.pow
                                       ).then_inc(ln["root"], 1)
                return stage

            def root_counts(n, i):
                pool.wait_ge(st["counted"], n)
                pool.tensor_tensor(hist[:, i, :], hist[:, i, :], neg_half[0:NHI, :], ALU.pow).then_inc(st["rooted"], 1)

            def gather_group(b, table, done):
                for g in range(G):
                    pool.indirect_dma_start(out=GA[b][:, g, :], out_offset=None, in_=table,
                                            in_offset=bass.IndirectOffsetOnAxis(ap=idx[b][:, g:g + 1], axis=0)
                                            ).then_inc(done, 16)

            def gather(ready, table, read):
                def body(t, first, last):
                    for b in range(2):
                        c = 2 * t + b
                        pool.wait_ge(ready, c + 1)
                        if not first:
                            pool.wait_ge(read, c - 1)
                        part_from_waits(pool)
                        gather_group(b, table, gathered[b])
                over_groups(pool, body)

            def gather_general(xs, table):
                def body(s, c, n):
                    pool.wait_ge(xs.sem, xs.after("masks", n))
                    part_from_waits(pool)
                    gather_group(0, table, xs.sem)
                general_path(pool, body)

            def keep0(k, first):
                pool.wait_ge(ln["applied"], n0["before"] + k + 1)
                pool.tensor_copy(chunk(H, k), row_stage[:, :, :]).then_inc(n0["kept"], 1)
                pool.wait_ge(first_in, 48)
                pool.tensor_tensor(chunk(X, k), chunk(X, k), r_beta[:, None, :].to_broadcast([P, CH, F]), ALU.add
                                   ).then_inc(n0["beta"], 1)
            over_chunks(pool, (0, inverse_root(n0, 0)), (1, keep0))

            pool.wait_ge(n0["stored"], 32 * NCH)
            gather(e0["idx"], src_table0, e0["x1"])
            gather_general(x0, src_table0)
            root_counts(1, 3)

            over_chunks(pool, (0, inverse_root(n1b, 0)))
            over_chunks(pool, (0, inverse_root(n1c, 1)))

            pool.wait_ge(n1c["stored"], 16 * NCH)
            gather(e1["idx"], table1, e1["agg"])
            gather_general(x1, table1)
            root_counts(2, 0)

            over_chunks(pool, (0, inverse_root(n2, 0)))
            pool.wait_ge(n2["acc_cp"], NCH)
            pool.wait_ge(n2["stored"], 32 * NCH)
            pool.wait_ge(zeroed, 16 * (G + (G - 1) * NCH))

            def scatter_tile(b, g, done):
                pool.indirect_dma_start(
                    out=sums[g], out_offset=bass.IndirectOffsetOnAxis(ap=idx[b][:, g:g + 1], axis=0),
                    in_=A3[b][:, g, :], in_offset=None, compute_op=ALU.add).then_inc(done, 16)

            def scatter(t, first, last):
                for b in range(2):
                    c = 2 * t + b
                    pool.wait_ge(e2["idx"], c + 1)
                    pool.wait_ge(e2["rows_out"], c + 1)
                    for g in range(G):
                        if not (first and b == 0):
                            pool.wait_ge(scattered[g], 16 * c)
                    part_from_waits(pool)
                    for g in range(G):
                        scatter_tile(b, g, scattered[g])
            over_groups(pool, scatter)
            for g in range(G):
                pool.wait_ge(scattered[g], 16 * NG)
            pool.sem_inc(x2.sem, 1)

            def scatter_general(s, c, n):
                pool.wait_ge(x2.sem, x2.after("rows_out", n))
                part_from_waits(pool)
                for g in range(G):
                    scatter_tile(0, g, x2.sem)
                pool.wait_ge(x2.sem, x2.after("sent", n))
            general_path(pool, scatter_general)
            pool.sem_inc(acc_done[2], 1)

            pool.memset(ACC[:, :], 0.0).then_inc(n3["acc_zero"], 1)

            def add_h(k, first):
                pool.wait_ge(ln["applied"], n3["before"] + k + 1)
                pool.tensor_tensor(chunk(X, k), chunk(X, k), table_stage[:, :, :], ALU.add).then_inc(n3["h_added"], 1)
            over_chunks(pool, (0, inverse_root(n3, 0)), (1, add_h))

            pool.wait_ge(n3["stored"], 16 * NCH)
            gather(e3["idx"], table3, e3["msg_in"])
            gather_general(x3, table3)

        @block.scalar
        def _(act):
            fn = nc.scalar.activation

            def normalize(s, i, frm, to, func, free, k):
                act.wait_ge(ln["shift"], s["before"] + k + 1)
                free(k)
                for j in range(CH):
                    last = fn(to(j), frm(j), func, scale=LN[i]["scale"][:, j:j + 1], bias=LN[i]["shift"][:, j:j + 1])
                last.then_inc(ln["applied"], 1)

            def turned0(k, first):
                act.wait_ge(n0["turn"], k + 1)
                if not first:
                    act.wait_ge(n0["mm"], k)
                    act.wait_ge(n0["ht"], k)
                fn(t_stage[:, :, 0:P], tiles(0, F, P), ACT.Copy).then_inc(n0["turned"], 1)

            def apply0(k, first):
                def free(k):
                    if not first:
                        act.wait_ge(n0["turn"], k)
                        act.wait_ge(n0["kept"], k)
                normalize(n0, 0, lambda j: tile_of(X, k, j), lambda j: row_stage[:, j, :], ACT.Relu, free, k)

            def pq_out0(k, first):
                act.wait_ge(n0["mm"], k + 1)
                if not first:
                    act.wait_ge(n0["stored"], 32 * k)
                n = 2 * BANK_TILES
                fn(pq_stage[:, 0:n, :], PQ[:, 0:n, :], ACT.Copy).then_inc(n0["p_out"], 1)
            over_chunks(act, (1, turned0), (0, apply0), (1, pq_out0))

            def window(sem_in, lo, b, table):
                act.dma_start(L[b][0:W, :], table[bass.ds(lo, W), :]).then_inc(sem_in, 16)

            def group_window(c, b, table):
                lo = act.value_load(winI[0:1, bass.ds(c, 1)], min_val=0, max_val=N - W)
                window(window_in[b], lo, b, table)

            act.wait_ge(consts, N_CONSTS)
            act.dma_start(dst_table0[N:NPAD, :], zero_rows[:, :]).then_inc(pads_zeroed, 16)
            act.dma_start(table2[N:NPAD, :], zero_rows[:, :]).then_inc(pads_zeroed, 16)
            act.wait_ge(pads_zeroed, 32)
            act.wait_ge(loads, N_LOADS)
            act.wait_ge(win_ready, 1)
            act.wait_ge(n0["stored"], 32 * NCH)
            for b in range(2):
                group_window(b, b, dst_table0)

            def edges0(t, first, last):
                for b in range(2):
                    c = 2 * t + b
                    act.wait_ge(e0["x1"], c + 1)
                    if not first:
                        act.wait_ge(e0["x2"], c - 1)
                    fn(A1[b][:, :, 0:P], tiles(2 * b, F, P), ACT.Gelu_apprx_tanh, bias=c_mb1[:, :]
                       ).then_inc(e0["g1"], 1)
                    if not last:
                        group_window(c + 2, b, dst_table0)
                    act.wait_ge(e0["y2"], c + 1)
                    if not first:
                        act.wait_ge(e0["agg"], c - 1)
                    fn(A3[b][:, :, :], A2[b][:, :, :], ACT.Gelu_apprx_tanh).then_inc(e0["g2"], 1)
            over_groups(act, edges0)

            def general0(s, c, n):
                act.wait_ge(x0.sem, x0.after("masks", n))
                window(x0.sem, s * W, 0, dst_table0)
                act.wait_ge(x0.sem, x0.after("x1", n))
                fn(A1[0][:, :, 0:P], tiles(0, F, P), ACT.Gelu_apprx_tanh, bias=c_mb1[:, :]).then_inc(x0.sem, 1)
                act.wait_ge(x0.sem, x0.after("y2", n))
                fn(A3[0][:, :, :], A2[0][:, :, :], ACT.Gelu_apprx_tanh).then_inc(x0.sem, 1)
            general_path(act, general0)
            act.wait_ge(st["turned"], 1)
            fn(dinv1[:, :], TURNED, ACT.Copy).then_inc(st["done"], 1)

            def act1(k, first):
                act.wait_ge(n1a["mm2"], k + 1)
                if not first:
                    act.wait_ge(n1a["mm3"], k)
                fn(t_stage[:, :, 0:P], tiles(2, F, P), ACT.Gelu_apprx_tanh, bias=c_ub1[:, :]).then_inc(n1a["act"], 1)
            over_chunks(act, (0, act1))

            def apply1(k, first):
                def free(k):
                    if not first:
                        act.wait_ge(n1b["x"], k)
                normalize(n1b, 0, lambda j: tile_of(H, k, j), lambda j: val_stage[:, j, :], ACT.Identity, free, k)
            over_chunks(act, (0, apply1))

            def apply_table1(k, first):
                def free(k):
                    if not first:
                        act.wait_ge(n1c["turn"], k)
                        act.wait_ge(n1c["stored"], 16 * k)
                normalize(n1c, 1, lambda j: tile_of(X, k, j), lambda j: table_stage[:, j, :], ACT.Relu, free, k)

            def self_loop1(k, first):
                act.wait_ge(n1c["turn"], k + 1)
                fn(chunk_t(ACC, k), tiles(6, F, P), ACT.Copy).then_inc(n1c["acc"], 1)
            over_chunks(act, (0, apply_table1), (1, self_loop1))

            act.wait_ge(st["turned"], 2)
            fn(dinv2[:, :], TURNED, ACT.Copy).then_inc(st["done"], 1)

            act.wait_ge(acc_done[1], 1)

            def acc_copy2(k, first):
                if not first:
                    act.wait_ge(n2["mm"], k)
                fn(agg_stage[:, :, 0:P], chunk_t(ACC, k), ACT.Copy).then_inc(n2["acc_cp"], 1)

            def apply2(k, first):
                def free(k):
                    if not first:
                        act.wait_ge(n2["turn"], k)
                normalize(n2, 0, lambda j: tile_of(X, k, j), lambda j: row_stage[:, j, :], ACT.Relu, free, k)

            def turned2(k, first):
                act.wait_ge(n2["turn"], k + 1)
                if not first:
                    act.wait_ge(n2["mm2"], k)
                fn(t_stage[:, :, 0:P], tiles(2, F, P), ACT.Copy).then_inc(n2["turned"], 1)
            over_chunks(act, (0, acc_copy2), (1, apply2), (1, turned2))

            act.wait_ge(n2["stored"], 32 * NCH)
            for b in range(2):
                group_window(b, b, table2)

            def picked(c, b, later):
                act.wait_ge(e2["pick"], c + 1)
                if later:
                    act.wait_ge(e2["rows"], c - 1)
                fn(A1[b][0:W, :, 0:P], tiles(2 * b, W, P), ACT.Copy).then_inc(e2["picked"], 1)
            picked(0, 0, False)

            def edges2(t, first, last):
                for b in range(2):
                    c = 2 * t + b
                    act.wait_ge(e2["rows"], c + 1)
                    if not first:
                        for g in range(G):
                            act.wait_ge(scattered[g], 16 * (c - 1))
                    fn(A3[b][:, :, :], tiles(4, P), ACT.Copy).then_inc(e2["rows_out"], 1)
                    if not last:
                        group_window(c + 2, b, table2)
                    if not (last and b == 1):
                        picked(c + 1, 1 - b, not (first and b == 0))
            over_groups(act, edges2)

            def general2(s, c, n):
                act.wait_ge(x2.sem, x2.begin(n))
                window(x2.sem, s * W, 0, table2)
                act.wait_ge(x2.sem, x2.after("pick", n))
                fn(A1[0][0:W, :, 0:P], tiles(0, W, P), ACT.Copy).then_inc(x2.sem, 1)
                act.wait_ge(x2.sem, x2.after("rows", n))
                fn(A3[0][:, :, :], tiles(4, P), ACT.Copy).then_inc(x2.sem, 1)
            general_path(act, general2)

            def row3(k, first):
                act.wait_ge(n3["sum"], k + 1)
                if not first:
                    act.wait_ge(n3["turn"], k)
                fn(row_stage[:, :, :], val_stage[:, :, :], ACT.Relu).then_inc(n3["row"], 1)

            def turned3(k, first):
                act.wait_ge(n3["turn"], k + 1)
                if not first:
                    act.wait_ge(n3["mm"], k)
                fn(z_stage[:, :, 0:P], tiles(0, F, P), ACT.Copy).then_inc(n3["turned"], 1)

            def hidden3(k, first):
                act.wait_ge(n3["mm"], k + 1)
                if not first:
                    act.wait_ge(n3["mm2"], k)
                for h in range(2):
                    fn(hid_stage[h][:, :, 0:P], tiles(2 + 2 * h, F, P), ACT.Relu, bias=c_b1[:, h:h + 1]
                       ).then_inc(n3["act"], 1)

            def apply3(k, first):
                def free(k):
                    if not first:
                        act.wait_ge(n3["stored"], 16 * k)
                        act.wait_ge(n3["turn2"], k)
                        act.wait_ge(n3["h_added"], k)
                normalize(n3, 0, lambda j: tile_of(X, k, j), lambda j: table_stage[:, j, :], ACT.Relu, free, k)

            def ht3(k, first):
                act.wait_ge(n3["turn2"], k + 1)
                fn(chunk_t(HT, k), tiles(6, F, P), ACT.Copy).then_inc(n3["ht"], 1)
            over_chunks(act, (1, turned3), (0, row3), (1, hidden3), (2, apply3), (2, ht3))

            def edges3(t, first, last):
                for b in range(2):
                    c = 2 * t + b
                    act.wait_ge(e3["msg_in"], c + 1)
                    if not first:
                        act.wait_ge(e3["agg"], c - 1)
                    fn(A3[b][:, :, :], A2[b][:, :, :], ACT.Silu).then_inc(e3["msg"], 1)
            over_groups(act, edges3)

            def general3(s, c, n):
                act.wait_ge(x3.sem, x3.after("msg_in", n))
                fn(A3[0][:, :, :], A2[0][:, :, :], ACT.Silu).then_inc(x3.sem, 1)
            general_path(act, general3)

            def act4(k, first):
                act.wait_ge(n4["mm"], k + 1)
                if not first:
                    act.wait_ge(n4["mm2"], k)
                fn(t_stage[:, :, 0:P], tiles(0, F, P), ACT.Silu, bias=c_sb1[:, :]).then_inc(n4["act"], 1)
            over_chunks(act, (0, act4))

        @block.vector
        def _(dve):
            v = nc.vector
            ch = Chain(dve, dve_chain)

            def statistics(s, i, frm, k, first):
                buf = LN[i]
                for j in range(CH):
                    last = v.bn_stats(buf["six"][:, j, :], frm(j))
                last.then_inc(ln["six"], 1)
                dve.wait_ge(ln["six"], s["before"] + k + 1)
                part_from_waits(dve)
                for j in range(CH):
                    last = v.bn_aggr(buf["mv"][:, j, :], buf["six"][:, j, :])
                last.then_inc(ln["mv"], 1)
                dve.wait_ge(ln["mv"], s["before"] + k + 1)
                v.tensor_scalar(buf["var"][:, :], buf["mv"][:, :, 1], LN_EPS, None, ALU.add).then_inc(ln["var"], 1)

            def scale_shift(s, i, times=None):
                buf = LN[i]

                def stage(k, first):
                    dve.wait_ge(ln["root"], s["before"] + k + 1)
                    if not first:
                        dve.wait_ge(ln["applied"], s["before"] + k)
                    if times is None:
                        v.tensor_copy(buf["scale"][:, :], buf["root"][:, :]).then_inc(ln["scale"], 1)
                    else:
                        v.tensor_tensor(buf["scale"][:, :], buf["root"][:, :], times[:, bass.ds(k * CH, CH)], ALU.mult
                                        ).then_inc(ln["scale"], 1)
                    dve.wait_ge(ln["scale"], s["before"] + k + 1)
                    v.scalar_tensor_tensor(buf["shift"][:, :], buf["mv"][:, :, 0], -1.0, buf["scale"][:, :],
                                           ALU.mult, ALU.mult).then_inc(ln["shift"], 1)
                return stage

            def ready_for_statistics(s, first, k):
                if not first:
                    dve.wait_ge(ln["shift"], s["before"] + k)
                part_from_waits(dve)

            def split(nodes):
                ch.link(v.tensor_scalar(part_of[:, :], nodes, HB.bit_length() - 1, None, ALU.arith_shift_right))
                ch.link(v.tensor_copy(high[:, :], part_of[:, :]))
                ch.link(v.tensor_scalar(part_of[:, :], nodes, HB - 1, None, ALU.bitwise_and))
                ch.link(v.tensor_copy(low[:, :], part_of[:, :]))

            def one_hot(to, values, width):
                return v.tensor_tensor(to, iota[:, None, 0:width].to_broadcast([P, G, width]),
                                       values[:, :, None].to_broadcast([P, G, width]), ALU.is_equal)

            def histogram(s, c, b, later):
                if later:
                    dve.wait_ge(s["hist"], c - 1)
                one_hot(HHI[b][:, :, :], group(high, c), NHI)
                one_hot(HLO[b][:, :, :], group(low, c), HB).then_inc(s["hist_in"], 1)

            def window_one_hot(s, to, c, b, read, later):
                if later:
                    dve.wait_ge(read, c - 1)
                one_hot(to[b][:, :, :], group(dst_rel, c), W).then_inc(s["onehot"], 1)

            def add_window(s, c, none_before):
                lo = dve.value_load(winI[0:1, bass.ds(c, 1)], min_val=0, max_val=N - W)
                dve.wait_ge(s["agg"], c + 1)
                if not none_before:
                    dve.wait_ge(s["added"], c)
                v.tensor_tensor(ACC[:, bass.ds(lo, W)], ACC[:, bass.ds(lo, W)], AGG, ALU.add).then_inc(s["added"], 1)

            def source_indices(ready, c, b):
                v.tensor_copy(idx[b][:, :], group(srcI, c)).then_inc(ready, 1)

            def general_masks(xs, to, s, c, n):
                dve.wait_ge(xs.sem, xs.begin(n) if xs is not x2 else xs.after("loaded", n))
                v.tensor_scalar(left_rel[:, :], group(left, c), sweep_win[:, bass.ds(s, 1)], None, ALU.subtract
                                ).then_inc(xs.sem, 1)
                dve.wait_ge(xs.sem, xs.after("rel", n))
                one_hot(to[0][:, :, :], left_rel, W).then_inc(xs.sem, 1)

            def general_add(xs, s, n):
                dve.wait_ge(xs.sem, xs.after("agg", n))
                v.tensor_tensor(ACC[:, bass.ds(s * W, W)], ACC[:, bass.ds(s * W, W)], AGG, ALU.add
                                ).then_inc(xs.sem, 1)

            def finish_edges(i, s, xs, body):
                dve.wait_ge(s["added"], NG)
                dve.sem_inc(xs.sem, 1)
                general_path(dve, body)
                dve.sem_inc(acc_done[i], 1)

            dve.wait_ge(idx_in, 32)
            v.tensor_reduce(neg_min[:, :], dstI[:, :].rearrange("p (c g) -> p c g", g=G), AX.X, ALU.min, negate=True
                            ).then_inc(neg_min_ready, 1)
            dve.wait_ge(consts, N_CONSTS)
            ch.link(v.tensor_copy(iota[:, :], iota_i[:, :]))
            ch.link(v.tensor_copy(part[:, :], part_i[:, :]))
            ch.link(v.tensor_copy(sweep_win[:, :], sweep_i[:, :]))
            ch.link(v.tensor_scalar(sweep_node[:, :], sweep_win[:, :], part[:, :], None, ALU.add))
            ch.link(v.tensor_scalar(spare_row[:, :], part[:, :], float(N), None, ALU.add))
            split(dstI[:, :])
            dve.wait_ge(neg_win_ready, 1)
            ch.link(v.tensor_scalar(neg_win[:, :], neg_win[:, :], float(W - N), None, ALU.max))
            v.tensor_scalar(winI[:, :], neg_win[0:1, :], -1.0, None, ALU.mult).then_inc(win_ready, 1)
            ch.link(v.tensor_scalar(win_node[:, :], neg_win[:, :], -1.0, part[:, :], ALU.mult, ALU.add))
            ch.link(v.tensor_tensor(dst_rel[:, :].rearrange("p (c g) -> p c g", g=G),
                                    dstI[:, :].rearrange("p (c g) -> p c g", g=G),
                                    neg_win[:, :, None].to_broadcast([P, NG, G]), ALU.add))
            v.tensor_reduce(left_most[:, 0:1], dst_rel[:, :], AX.X, ALU.max).then_inc(most_ready, 1)
            ch.link(v.tensor_scalar(left[:, :], dst_rel[:, :], float(W), None, ALU.is_ge))
            ch.link(v.scalar_tensor_tensor(left[:, :], dstI[:, :], 1.0, left[:, :], ALU.add, ALU.mult))
            ch.link(v.tensor_scalar(left[:, :], left[:, :], -1.0, None, ALU.add))
            dve.wait_ge(most_everywhere, 1)
            v.tensor_scalar(leftI[:, :], left_most[0:1, 1:2], float(W), None, ALU.is_ge).then_inc(left_ready, 1)
            dve.wait_ge(win_ready, 1)
            dve.wait_ge(x_in, 16 * NCH)

            def statistics0(k, first):
                ready_for_statistics(n0, first, k)
                statistics(n0, 0, lambda j: tile_of(X, k, j), k, first)

            def tail0(k, first):
                dve.wait_ge(n0["turned"], k + 1)
                v.tensor_copy(chunk_t(HT, k), t_stage[:, :, 0:P]).then_inc(n0["ht"], 1)
                dve.wait_ge(n0["mm"], k + 1)
                if not first:
                    dve.wait_ge(n0["stored"], 32 * k)
                n = 2 * BANK_TILES
                v.tensor_copy(pq_stage[:, n:CH, :], PQ[:, n:CH, :]).then_inc(n0["q_out"], 1)
            over_chunks(dve, (1, scale_shift(n0, 0)), (0, statistics0), (2, tail0))

            def one_hot_turned(c, b, t, first):
                dve.wait_ge(rows_in[b], 16 * (t + 1))
                if not first:
                    dve.wait_ge(e0["x1_win"], c - 1)
                v.tensor_scalar(R[b][0:W, :], DR[b], win_node[0:W, bass.ds(c, 1)], None, ALU.is_equal
                                ).then_inc(e0["onehot_t"], 1)

            dve.wait_ge(loads, N_LOADS)
            dve.wait_ge(n0["stored"], 32 * NCH)
            dve.wait_ge(n0["kept"], NCH)
            for b in range(2):
                source_indices(e0["idx"], b, b)
            for b in range(2):
                one_hot_turned(b, b, 0, True)
                histogram(e0, b, b, False)

            def mlp_bias(b):
                return v.tensor_tensor(A2[b][:, :, :], tiles(4, P), r_mb2[:, None, :].to_broadcast([P, G, F]), ALU.add)

            def edges0(t, first, last):
                for b in range(2):
                    c = 2 * t + b
                    if not last:
                        dve.wait_ge(gathered[b], 16 * G * (t + 1))
                        source_indices(e0["idx"], c + 2, b)
                    window_one_hot(e0, OH, c, b, e0["agg"], not first)
                    dve.wait_ge(e0["x2"], c + 1)
                    if not first:
                        dve.wait_ge(e0["g2"], c - 1)
                    mlp_bias(b).then_inc(e0["y2"], 1)
                    if not (first and b == 0):
                        add_window(e0, c - 1, first and b == 1)
                    if not last:
                        one_hot_turned(c + 2, b, t + 1, False)
                        histogram(e0, c + 2, b, True)
            over_groups(dve, edges0)
            add_window(e0, NG - 1, False)

            def general0(s, c, n):
                general_masks(x0, OH, s, c, n)
                source_indices(x0.sem, c, 0)
                dve.wait_ge(x0.sem, x0.after("loaded", n))
                v.tensor_scalar(R[0][0:W, :], DR[0], sweep_node[0:W, bass.ds(s, 1)], None, ALU.is_equal
                                ).then_inc(x0.sem, 1)
                dve.wait_ge(x0.sem, x0.after("x2", n))
                mlp_bias(0).then_inc(x0.sem, 1)
                general_add(x0, s, n)
            finish_edges(0, e0, x0, general0)

            dve.wait_ge(e0["hist"], NG + 1)
            ch.link(v.tensor_copy(hist[:, 0, :], HIST))
            ch.link(v.tensor_scalar(hist[:, 1, :], hist[:, 0, :], 1e-8, None, ALU.add))
            ch.link(v.reciprocal(hist[:, 1, :], hist[:, 1, :]))
            ch.link(v.tensor_scalar(hist[:, 2, :], hist[:, 0, :], 1.0, None, ALU.max))
            ch.link(v.reciprocal(hist[:, 2, :], hist[:, 2, :]))
            v.tensor_scalar(hist[:, 3, :], hist[:, 0, :], 1.0, None, ALU.add).then_inc(st["counted"], 1)
            split(srcI[:, :])

            def agg1(k, first):
                dve.wait_ge(n1a["inp"], 32 * (k + 1))
                dve.wait_ge(n1a["mm"], k + 1)
                if not first:
                    dve.wait_ge(n1a["mm2"], k)
                cnt, inv = (cnt_stage[i][:, :].rearrange("p (t n) -> p t n", n=P) for i in range(2))
                agg = agg_stage[:, :, 0:P]
                v.scalar_tensor_tensor(agg, cnt, c_mb3[:, :], tiles(0, F, P), ALU.mult, ALU.add
                                       ).then_inc(n1a["agg1"], 1)
                dve.wait_ge(n1a["agg1"], k + 1)
                v.tensor_tensor(agg, agg, inv, ALU.mult).then_inc(n1a["agg"], 1)

            def residual1(k, first):
                dve.wait_ge(n1a["mm3"], k + 1)
                v.tensor_tensor(chunk(H, k), chunk(H, k), tiles(4, P), ALU.add).then_inc(n1a["y"], 1)
            dve.wait_ge(n0["beta"], NCH)
            over_chunks(dve, (0, agg1), (1, residual1))

            dve.wait_ge(n1a["y"], NCH)
            dve.wait_ge(ln["shift"], n0["before"] + NCH)

            def statistics1(k, first):
                ready_for_statistics(n1b, first, k)
                statistics(n1b, 0, lambda j: tile_of(H, k, j), k, first)

            def x1_sum(k, first):
                dve.wait_ge(ln["applied"], n1b["before"] + k + 1)
                y = val_stage[:, :, :]
                v.tensor_tensor(y, y, r_gamma[:, None, :].to_broadcast([P, CH, F]), ALU.mult).then_inc(n1b["scaled"], 1)
                dve.wait_ge(n1b["scaled"], k + 1)
                v.tensor_tensor(chunk(X, k), chunk(X, k), y, ALU.add).then_inc(n1b["x"], 1)
            over_chunks(dve, (1, scale_shift(n1b, 0)), (0, statistics1), (2, x1_sum))

            dve.wait_ge(st["done"], 1)
            dve.wait_ge(n1b["x"], NCH)

            def statistics1c(k, first):
                ready_for_statistics(n1c, first, k)
                statistics(n1c, 1, lambda j: tile_of(X, k, j), k, first)
            over_chunks(dve, (1, scale_shift(n1c, 1, dinv1)), (0, statistics1c))

            dve.wait_ge(n1c["acc"], NCH)
            for b in range(2):
                source_indices(e1["idx"], b, b)

            def edges1(t, first, last):
                for b in range(2):
                    c = 2 * t + b
                    window_one_hot(e1, OH, c, b, e1["agg"], not first)
                    histogram(e1, c, b, not first)
                    if not (first and b == 0):
                        add_window(e1, c - 1, first and b == 1)
                    if not last:
                        dve.wait_ge(gathered[b], 16 * G * (PASS + t + 1))
                        source_indices(e1["idx"], c + 2, b)
            over_groups(dve, edges1)
            add_window(e1, NG - 1, False)

            def general1(s, c, n):
                general_masks(x1, OH, s, c, n)
                source_indices(x1.sem, c, 0)
                general_add(x1, s, n)
            finish_edges(1, e1, x1, general1)

            dve.wait_ge(e1["hist"], NG + 1)
            dve.wait_ge(st["stored"], 16 * 4)
            v.tensor_scalar(hist[:, 0, :], HIST, 1.0, None, ALU.add).then_inc(st["counted"], 1)

            def x2_sum(k, first):
                dve.wait_ge(n2["mm"], k + 1)
                if not first:
                    dve.wait_ge(n2["x"], k)
                for j in range(CH):
                    last = v.scalar_tensor_tensor(val_stage[:, j, :], tiles(0, P)[:, j, :],
                                                  dinv1[:, bass.ds(k * CH + j, 1)], r_gb[:, :], ALU.mult, ALU.add)
                last.then_inc(n2["v"], 1)
                dve.wait_ge(n2["v"], k + 1)
                v.scalar_tensor_tensor(chunk(X, k), val_stage[:, :, :], 0.0, chunk(X, k), ALU.max, ALU.add
                                       ).then_inc(n2["x"], 1)
                dve.wait_ge(n2["x"], k + 1)
                ready_for_statistics(n2, first, k)
                statistics(n2, 0, lambda j: tile_of(X, k, j), k, first)

            def table2_rows(k, first):
                dve.wait_ge(n2["mm2"], k + 1)
                if not first:
                    dve.wait_ge(n2["stored"], 32 * k)
                v.tensor_tensor(table_stage[:, :, :], tiles(4, P), chunk_cols(dinv2, k), ALU.mult
                                ).then_inc(n2["out"], 1)
            dve.wait_ge(n1c["stored"], 16 * NCH)
            dve.wait_ge(ln["shift"], n1c["before"] + NCH)
            dve.wait_ge(st["done"], 2)
            over_chunks(dve, (1, scale_shift(n2, 0)), (0, x2_sum), (2, table2_rows))

            def same_source(c, b, t, later):
                window_one_hot(e2, OHB, c, b, e2["pick"], later)
                dve.wait_ge(rows_in[b], 16 * (PASS + t + 1))
                v.tensor_tensor(SM[b][:, :, :], SR[b].rearrange("p (g e) -> p g e", g=G),
                                group(srcI, c)[:, :, None].to_broadcast([P, G, P]), ALU.is_equal
                                ).then_inc(e2["same"], 1)

            def sum_rows(done, c, b):
                v.tensor_tensor(SE[:, :, :], SM[b][:, :, :], before[:, None, :].to_broadcast([P, G, P]), ALU.mult
                                ).then_inc(done("first_of")[0], 1)
                v.tensor_scalar(to_spare[:, :], group(srcI, c), -1.0, spare_row[:, :], ALU.mult, ALU.add
                                ).then_inc(done("first_of")[0], 1)
                dve.wait_ge(*done("first_of"))
                v.tensor_reduce(earlier[:, :], SE[:, :, :], AX.X, ALU.add).then_inc(done("earlier")[0], 1)
                dve.wait_ge(*done("earlier"))
                v.scalar_tensor_tensor(move[:, :], earlier[:, :], 0.0, to_spare[:, :], ALU.is_gt, ALU.mult
                                       ).then_inc(done("move")[0], 1)
                dve.wait_ge(*done("move"))

            def sum_indices(ready, c, b):
                v.tensor_tensor(idx[b][:, :], group(srcI, c), move[:, :], ALU.add).then_inc(ready, 1)

            def done_by(n):
                return lambda step: (e2[step], 2 * n if step == "first_of" else n)
            same_source(0, 0, 0, False)

            def edges2(t, first, last):
                for b in range(2):
                    c = 2 * t + b
                    if not (last and b == 1):
                        same_source(c + 1, 1 - b, t + b, not (first and b == 0))
                    if not (first and b == 0):
                        dve.wait_ge(e2["idx"], c)
                    dve.wait_ge(e2["same"], c + 1)
                    sum_rows(done_by(c + 1), c, b)
                    if not first:
                        for g in range(G):
                            dve.wait_ge(scattered[g], 16 * (c - 1))
                    sum_indices(e2["idx"], c, b)
            over_groups(dve, edges2)

            def general2(s, c, n):
                general_masks(x2, OHB, s, c, n)
                v.tensor_tensor(SM[0][:, :, :], SR[0].rearrange("p (g e) -> p g e", g=G),
                                group(srcI, c)[:, :, None].to_broadcast([P, G, P]), ALU.is_equal
                                ).then_inc(x2.sem, 1)
                dve.wait_ge(x2.sem, x2.after("masks", n))
                sum_rows(lambda step: (x2.sem, x2.after(step, n)), c, 0)
                sum_indices(x2.sem, c, 0)
            general_path(dve, general2)

            def sum3(k, first):
                dve.wait_ge(n3["inp"], 16 * G * (k + 1))
                s = sum_parts[0]
                for g in range(1, G):
                    v.tensor_tensor(s, s, sum_parts[g], ALU.add).then_inc(n3[f"s{g}"], 1)
                    dve.wait_ge(n3[f"s{g}"], k + 1)
                if not first:
                    dve.wait_ge(n3["row"], k)
                v.tensor_tensor(val_stage[:, :, :], s, chunk_cols(dinv2, k), ALU.mult).then_inc(n3["sum"], 1)

            def x3_sum(k, first):
                dve.wait_ge(n3["mm2"], k + 1)
                v.tensor_tensor(chunk(X, k), chunk(X, k), tiles(0, P), ALU.add).then_inc(n3["x"], 1)
                dve.wait_ge(n3["x"], k + 1)
                ready_for_statistics(n3, first, k)
                statistics(n3, 0, lambda j: tile_of(X, k, j), k, first)
            over_chunks(dve, (2, scale_shift(n3, 0)), (0, sum3), (1, x3_sum))

            dve.wait_ge(n3["acc_zero"], 1)
            for b in range(2):
                source_indices(e3["idx"], b, b)

            def message_in(b):
                return v.tensor_tensor(A2[b][:, :, :], GA[b], ER[b][0:P, :].rearrange("p (g f) -> p g f", f=F), ALU.add)

            def edges3(t, first, last):
                for b in range(2):
                    c = 2 * t + b
                    window_one_hot(e3, OH, c, b, e3["agg"], not first)
                    if not (first and b == 0):
                        add_window(e3, c - 1, first and b == 1)
                    dve.wait_ge(gathered[b], 16 * G * (2 * PASS + t + 1))
                    if not last:
                        source_indices(e3["idx"], c + 2, b)
                    dve.wait_ge(attr_in[b], 16 * (PASS + t + 1))
                    if not first:
                        dve.wait_ge(e3["msg"], c - 1)
                    message_in(b).then_inc(e3["msg_in"], 1)
            over_groups(dve, edges3)
            add_window(e3, NG - 1, False)

            def general3(s, c, n):
                general_masks(x3, OH, s, c, n)
                source_indices(x3.sem, c, 0)
                dve.wait_ge(x3.sem, x3.after("loaded", n))
                message_in(0).then_inc(x3.sem, 1)
                general_add(x3, s, n)
            finish_edges(3, e3, x3, general3)

            def hh4(k, first):
                dve.wait_ge(n4["inp"], 16 * (k + 1))
                if not first:
                    dve.wait_ge(n4["mm"], k)
                hh = agg_stage[:, :, 0:P]
                v.tensor_tensor(hh, chunk_t(ACC, k), cnt_stage[0][:, :].rearrange("p (t n) -> p t n", n=P), ALU.mult
                                ).then_inc(n4["hh1"], 1)
                dve.wait_ge(n4["hh1"], k + 1)
                v.tensor_tensor(hh, hh, chunk_t(HT, k), ALU.add).then_inc(n4["hh"], 1)

            def x4_sum(k, first):
                dve.wait_ge(n4["mm2"], k + 1)
                v.tensor_tensor(chunk(X, k), chunk(X, k), tiles(2, P), ALU.add).then_inc(n4["out"], 1)
            dve.wait_ge(n3["ht"], NCH)
            dve.wait_ge(n3["h_added"], NCH)
            over_chunks(dve, (0, hh4), (1, x4_sum))

        @block.tensor
        def _(pe):
            mm = nc.tensor.matmul

            def wide(bank, lhsT, rhs, start, stop):
                o, n = tiles(bank, F, P), IN_BANK
                mm(o[:, 0:n, :], lhsT, rhs[:, 0:n, :], start=start, stop=stop)
                return mm(o[:, n:CH, :], lhsT, rhs[:, n:CH, :], start=start, stop=stop)

            def bias(bank, row):
                o, n = tiles(bank, P), IN_BANK
                mm(o[:, 0:n, :], ones_row[:, :], row[:, 0:n, :], start=True, stop=False)
                mm(o[:, n:CH, :], ones_row[:, :], row[:, n:CH, :], start=True, stop=False)

            def closes(j):
                return j == IN_BANK - 1 or j == CH - 1

            def per_tile(bank, stage, rhs, on_bias=False):
                for j in range(CH):
                    last = mm(tiles(bank, P)[:, j, :], stage[:, j, 0:P], rhs, start=not on_bias,
                              stop=not on_bias or closes(j))
                return last

            def turn(bank, stage):
                for j in range(CH):
                    last = mm(tiles(bank, F, P)[:, j, :], stage[:, j, :], ident[0:P, 0:P], start=True, stop=True)
                return last

            def histogram(s, c, b):
                pe.wait_ge(s["hist_in"], c + 1)
                for g in range(G):
                    last = mm(HIST, HHI[b][:, g, :], HLO[b][:, g, :], start=False, stop=False)
                last.then_inc(s["hist"], 1)

            def histogram_edge(s, start):
                last = mm(HIST, zeros16[:, 0:NHI], zeros16[:, :], start=start, stop=not start)
                if not start:
                    last.then_inc(s["hist"], 1)

            def aggregate(rows, b):
                for g in range(G):
                    last = mm(AGG, rows[:, g, :], OH[b][:, g, :], start=(g == 0), stop=(g == G - 1))
                return last

            def group_aggregate(s, c, b, rows, none_before):
                pe.wait_ge(s["onehot"], c + 1)
                if not none_before:
                    pe.wait_ge(s["added"], c)
                aggregate(rows, b).then_inc(s["agg"], 1)

            pe.wait_ge(consts, N_CONSTS)
            pe.wait_ge(first_in, 48)

            def turn0(k, first):
                pe.wait_ge(ln["applied"], n0["before"] + k + 1)
                if not first:
                    pe.wait_ge(n0["turned"], k)
                turn(0, row_stage).then_inc(n0["turn"], 1)

            def tables0(k, first):
                pe.wait_ge(n0["turned"], k + 1)
                if not first:
                    pe.wait_ge(n0["p_out"], k)
                    pe.wait_ge(n0["q_out"], k)
                for j in range(CH):
                    last = mm(PQ[:, j, :], t_stage[:, j, 0:P], w_pq[:, :], start=True, stop=True)
                last.then_inc(n0["mm"], 1)
            over_chunks(pe, (1, tables0), (0, turn0))

            pe.wait_ge(loads, N_LOADS)
            pe.wait_ge(n0["q_out"], NCH)
            pe.wait_ge(n0["p_out"], NCH)
            histogram_edge(e0, True)

            def x1_window(b):
                return wide(2 * b, L[b][:, :], R[b][:, :].rearrange("p (g e) -> p g e", g=G), True, False)

            def x1_sources(b):
                for g in range(G):
                    last = mm(tiles(2 * b, F, P)[:, g, :], GA[b][:, g, :], ident[0:P, 0:P], start=False, stop=closes(g))
                return last

            def ahead(c, b, t, later):
                pe.wait_ge(e0["onehot_t"], c + 1)
                pe.wait_ge(attr_in[b], 16 * (t + 1))
                pe.wait_ge(window_in[b], 16 * (t + 1))
                if later:
                    pe.wait_ge(e0["g1"], c - 1)
                x1_window(b).then_inc(e0["x1_win"], 1)
                histogram(e0, c, b)
            ahead(0, 0, 0, False)

            def edges0(t, first, last):
                for b in range(2):
                    c = 2 * t + b
                    pe.wait_ge(gathered[b], 16 * G * (t + 1))
                    x1_sources(b).then_inc(e0["x1"], 1)
                    if not (last and b == 1):
                        ahead(c + 1, 1 - b, t + b, not (first and b == 0))
                    pe.wait_ge(e0["g1"], c + 1)
                    if not (first and b == 0):
                        pe.wait_ge(e0["y2"], c)
                    per_tile(4, A1[b], w_m2[:, :]).then_inc(e0["x2"], 1)
                    if not (first and b == 0):
                        pe.wait_ge(e0["g2"], c)
                        group_aggregate(e0, c - 1, 1 - b, A3[1 - b], first and b == 1)
            over_groups(pe, edges0)
            pe.wait_ge(e0["g2"], NG)
            group_aggregate(e0, NG - 1, 1, A3[1], False)
            histogram_edge(e0, False)

            def general0(s, c, n):
                pe.wait_ge(x0.sem, x0.after("masks_t", n))
                x1_window(0)
                x1_sources(0).then_inc(x0.sem, 1)
                pe.wait_ge(x0.sem, x0.after("g1", n))
                per_tile(4, A1[0], w_m2[:, :]).then_inc(x0.sem, 1)
                pe.wait_ge(x0.sem, x0.after("g2", n))
                aggregate(A3[0], 0).then_inc(x0.sem, 1)
            general_path(pe, general0)
            pe.wait_ge(st["loaded"], 16)
            mm(TURNED, stat_rows[:, :], ident[0:NT, 0:NT], start=True, stop=True).then_inc(st["turned"], 1)

            pe.wait_ge(acc_done[0], 1)

            def messages1(k, first):
                if not first:
                    pe.wait_ge(n1a["agg"], k)
                wide(0, w_m3[:, :], chunk_t(ACC, k), True, True).then_inc(n1a["mm"], 1)

            def update1(k, first):
                if not first:
                    pe.wait_ge(n1a["act"], k)
                wide(2, w_uh[:, :], chunk_t(HT, k), True, False)
                if not first:
                    pe.wait_ge(n1a["y"], k)
                bias(4, o_ub2)
                pe.wait_ge(n1a["agg"], k + 1)
                wide(2, w_ua[:, :], agg_stage[:, :, 0:P], False, True).then_inc(n1a["mm2"], 1)

            def output1(k, first):
                pe.wait_ge(n1a["act"], k + 1)
                per_tile(4, t_stage, w_u2[:, :], on_bias=True).then_inc(n1a["mm3"], 1)
            over_chunks(pe, (1, update1), (0, messages1), (1, output1))

            def turn1(k, first):
                pe.wait_ge(ln["applied"], n1c["before"] + k + 1)
                if not first:
                    pe.wait_ge(n1c["acc"], k)
                turn(6, table_stage).then_inc(n1c["turn"], 1)
            pe.wait_ge(st["done"], 1)
            over_chunks(pe, (0, turn1))

            pe.wait_ge(n1c["acc"], NCH)
            histogram_edge(e1, True)

            def edges1(t, first, last):
                for b in range(2):
                    c = 2 * t + b
                    histogram(e1, c, b)
                    pe.wait_ge(gathered[b], 16 * G * (PASS + t + 1))
                    group_aggregate(e1, c, b, GA[b], first and b == 0)
            over_groups(pe, edges1)
            histogram_edge(e1, False)

            def general1(s, c, n):
                pe.wait_ge(x1.sem, x1.after("gathered", n))
                aggregate(GA[0], 0).then_inc(x1.sem, 1)
            general_path(pe, general1)
            pe.wait_ge(st["loaded"], 32)
            mm(TURNED, stat_rows[:, :], ident[0:NT, 0:NT], start=True, stop=True).then_inc(st["turned"], 1)

            def product2(k, first):
                pe.wait_ge(n2["acc_cp"], k + 1)
                if not first:
                    pe.wait_ge(n2["v"], k)
                per_tile(0, agg_stage, w_g[:, :]).then_inc(n2["mm"], 1)

            def turn2(k, first):
                pe.wait_ge(ln["applied"], n2["before"] + k + 1)
                if not first:
                    pe.wait_ge(n2["turned"], k)
                turn(2, row_stage).then_inc(n2["turn"], 1)
                if not first:
                    pe.wait_ge(n2["out"], k)
                bias(4, o_lb)

            def linear2(k, first):
                pe.wait_ge(n2["turned"], k + 1)
                per_tile(4, t_stage, w_lin[:, :], on_bias=True).then_inc(n2["mm2"], 1)
            over_chunks(pe, (0, product2), (1, turn2), (1, linear2))

            def pick_tiles(b):
                for g in range(G):
                    last = mm(tiles(2 * b, W, P)[:, g, :], OHB[b][:, g, :], SM[b][:, g, :], start=True, stop=True)
                return last

            def row_tiles(b):
                for g in range(G):
                    last = mm(tiles(4, P)[:, g, :], A1[b][0:W, g, 0:P], L[b][0:W, :], start=True, stop=True)
                return last

            def pick(c, b, later):
                pe.wait_ge(e2["onehot"], c + 1)
                pe.wait_ge(e2["same"], c + 1)
                if later:
                    pe.wait_ge(e2["picked"], c - 1)
                pick_tiles(b).then_inc(e2["pick"], 1)
            pe.wait_ge(n2["out"], NCH)
            pick(0, 0, False)

            def edges2(t, first, last):
                for b in range(2):
                    c = 2 * t + b
                    if not (last and b == 1):
                        pick(c + 1, 1 - b, not (first and b == 0))
                    pe.wait_ge(e2["picked"], c + 1)
                    pe.wait_ge(window_in[b], 16 * (PASS + t + 1))
                    if not (first and b == 0):
                        pe.wait_ge(e2["rows_out"], c)
                    row_tiles(b).then_inc(e2["rows"], 1)
            over_groups(pe, edges2)

            def general2(s, c, n):
                pe.wait_ge(x2.sem, x2.after("idx", n))
                pick_tiles(0).then_inc(x2.sem, 1)
                pe.wait_ge(x2.sem, x2.after("picked", n))
                row_tiles(0).then_inc(x2.sem, 1)
            general_path(pe, general2)

            pe.wait_ge(e2["rows_out"], NG)

            def turn3(k, first):
                pe.wait_ge(n3["row"], k + 1)
                if not first:
                    pe.wait_ge(n3["x"], k)
                turn(0, row_stage).then_inc(n3["turn"], 1)

            def hidden3(k, first):
                pe.wait_ge(n3["turned"], k + 1)
                if not first:
                    pe.wait_ge(n3["act"], 2 * k)
                wide(2, w_z1[:, 0:F], z_stage[:, :, 0:P], True, True)
                wide(4, w_z1[:, F:2 * F], z_stage[:, :, 0:P], True, True).then_inc(n3["mm"], 1)
                bias(0, o_b2)

            def output3(k, first):
                pe.wait_ge(n3["act"], 2 * k + 2)
                for j in range(CH):
                    for h in range(2):
                        last = mm(tiles(0, P)[:, j, :], hid_stage[h][:, j, 0:P], w_z2[:, h, :],
                                  start=False, stop=h == 1 and closes(j))
                last.then_inc(n3["mm2"], 1)

            def turn_table3(k, first):
                pe.wait_ge(ln["applied"], n3["before"] + k + 1)
                if not first:
                    pe.wait_ge(n3["ht"], k)
                turn(6, table_stage).then_inc(n3["turn2"], 1)
            over_chunks(pe, (0, turn3), (0, hidden3), (0, output3), (1, turn_table3))

            pe.wait_ge(n3["ht"], NCH)

            def edges3(t, first, last):
                for b in range(2):
                    c = 2 * t + b
                    pe.wait_ge(e3["msg"], c + 1)
                    group_aggregate(e3, c, b, A3[b], first and b == 0)
            over_groups(pe, edges3)

            def general3(s, c, n):
                pe.wait_ge(x3.sem, x3.after("msg", n))
                aggregate(A3[0], 0).then_inc(x3.sem, 1)
            general_path(pe, general3)

            def hidden4(k, first):
                pe.wait_ge(n4["hh"], k + 1)
                if not first:
                    pe.wait_ge(n4["act"], k)
                wide(0, w_s1[:, :], agg_stage[:, :, 0:P], True, True).then_inc(n4["mm"], 1)

            def output4(k, first):
                if not first:
                    pe.wait_ge(n4["out"], k)
                bias(2, o_sb2)
                pe.wait_ge(n4["act"], k + 1)
                per_tile(2, t_stage, w_s2[:, :], on_bias=True).then_inc(n4["mm2"], 1)
            over_chunks(pe, (0, hidden4), (1, output4))


_PLAIN = ["L0_gnn_mW1", "L0_gnn_mb1", "L0_gnn_mW2", "L0_gnn_mb2", "L0_gnn_mW3", "L0_gnn_mb3", "L0_gnn_uW1",
          "L0_gnn_ub1", "L0_gnn_uW2", "L0_gnn_ub2", "L0_gnn_gamma", "L0_gnn_beta", "L1_gnn_W", "L1_gnn_b",
          "L2_gnn_lin_w", "L2_gnn_lin_b", "L2_gnn_w1", "L2_gnn_b1", "L2_gnn_w2", "L2_gnn_b2", "L3_gnn_W1",
          "L3_gnn_b1", "L3_gnn_W2", "L3_gnn_b2"]


def kernel(**inputs):
    import numpy as np
    import concourse.bacc as bacc
    from concourse.bass_utils import run_bass_kernel_spmd

    a = {n: np.ascontiguousarray(inputs[n]) for n in inputs}
    by_partition = {n: a[n].reshape(NG, P, G).transpose(1, 0, 2).reshape(P, NG * G) for n in ("src", "dst")}
    by_tile = {n: a[n].reshape(NG, P, G).transpose(0, 2, 1).reshape(NG, G * P) for n in ("src", "dst")}
    edge_attr_64_t = a["edge_attr_64"].reshape(NG, P, G, FE).transpose(0, 3, 2, 1).reshape(NG * FE, G * P)
    laid = [("x", a["x"]), ("src_g", by_partition["src"]), ("dst_g", by_partition["dst"]),
            ("src_rows", by_tile["src"]), ("dst_rows", by_tile["dst"]),
            ("edge_attr_128", a["edge_attr_128"]), ("edge_attr_64_t", edge_attr_64_t)]
    laid += [(n, a[n]) for n in _PLAIN]

    nc = bacc.Bacc("TRN2", target_bir_lowering=False, num_devices=1)
    arrays, args = {}, []
    for name, v in laid:
        v = np.ascontiguousarray(v)
        arrays[f"in_{name}"] = v
        args.append(nc.dram_tensor(f"in_{name}", v.shape, mybir.dt.from_np(v.dtype), kind="ExternalInput").ap())
    args.append(nc.dram_tensor("out_x", (N, F), F32, kind="ExternalOutput").ap())
    gnn_kernel(nc, *args)
    r = run_bass_kernel_spmd(nc, [arrays], core_ids=[0])
    return r.results[0]["out_x"]
```

```python
from contextlib import ExitStack

import concourse.bass as bass
from concourse import mybir
from concourse.alu_op_type import AluOpType as ALU

F32 = mybir.dt.float32
BF16 = mybir.dt.bfloat16
I32 = mybir.dt.int32
ACT = mybir.ActivationFunctionType
AX = mybir.AxisListType
RMAX = bass.bass_isa.ReduceOp.max

N = 6250
E = 106250
F = 128
FE = 64
P = 125
G = 5
NG = E // (P * G)
W = 64
CH = 5
NT = N // P
NCH = NT // CH
CN = CH * P
HB = 128
NHI = (N + HB - 1) // HB
NWIN = (N + W - 1) // W
NPAD = NWIN * W
SWEEPS = NWIN
LN_EPS = 1e-5



class Steps:

    def __init__(self, sem, **counts):
        self.sem, self.total, self.until = sem, 0, {}
        for step, count in counts.items():
            self.total += count
            self.until[step] = self.total

    def begin(self, n):
        return (n - 1) * self.total + 1

    def after(self, step, n):
        return (n - 1) * self.total + 1 + self.until[step]


class Chain:

    def __init__(self, eng, sem):
        self.eng, self.sem, self.n = eng, sem, 0

    def link(self, instruction):
        self.n += 1
        instruction.then_inc(self.sem, 1)
        self.eng.wait_ge(self.sem, self.n)


def gnn_kernel(nc, x, src_g, dst_g, src_rows, dst_rows, edge_attr_128, edge_attr_64_t,
               mW1, mb1, mW2, mb2, mW3, mb3, uW1, ub1, uW2, ub2, gamma, beta,
               gW, gb, lin_w, lin_b, w1, b1, w2, b2, sW1, sb1, sW2, sb2, out):
    ctx = ExitStack()
    with ctx:
        def sb(name, shape, dt=F32):
            return ctx.enter_context(nc.sbuf_tensor(name, shape, dt))

        def sem(name):
            return ctx.enter_context(nc.semaphore(name))

        def dram(name, shape):
            return nc.dram_tensor(name, shape, F32).ap()

        src_table0 = dram("src_table0", (N, F))
        dst_table0 = dram("dst_table0", (NPAD, F))
        table1 = dram("table1", (N, F))
        table2 = dram("table2", (NPAD, F))
        table3 = dram("table3", (N, F))
        sums = [dram(f"sums{g}", (N + P, F)) for g in range(G)]
        stats = dram("stats", (5, NHI * HB))

        X = sb("X", [P, NT, F])
        H = sb("H", [P, NT, F])
        HT = sb("HT", [F, N])
        ACC = sb("ACC", [F, NPAD])
        srcI = sb("srcI", [P, NG * G], I32)
        dstI = sb("dstI", [P, NG * G], I32)
        dst_rel = sb("dst_rel", [P, NG * G])
        high = sb("high", [P, NG * G])
        low = sb("low", [P, NG * G])
        part_of = sb("part_of", [P, NG * G], I32)
        neg_min = sb("neg_min", [P, NG])
        neg_win = sb("neg_win", [P, NG])
        win_node = sb("win_node", [P, NG])
        winI = sb("winI", [1, NG], I32)
        left = sb("left", [P, NG * G])
        left_most = sb("left_most", [P, 2])
        leftI = sb("leftI", [1, 1], I32)
        ident = sb("ident", [F, F])
        before = sb("before", [P, P], BF16)
        iota_i = sb("iota_i", [P, F], I32)
        iota = sb("iota", [P, F])
        part_i = sb("part_i", [P, 1], I32)
        part = sb("part", [P, 1])
        spare_row = sb("spare_row", [P, 1])
        neg_half = sb("neg_half", [P, HB])
        zeros = sb("zeros", [P, CH * F])
        zeros16 = sb("zeros16", [P, HB], BF16)
        ones_row = sb("ones_row", [1, P])
        sweep_i = sb("sweep_i", [P, NWIN], I32)
        sweep_win = sb("sweep_win", [P, NWIN])
        sweep_node = sb("sweep_node", [P, NWIN])
        w_pq = sb("w_pq", [F, 2 * F])
        w_m2, w_m3 = sb("w_m2", [F, F]), sb("w_m3", [F, F])
        w_uh, w_ua, w_u2 = sb("w_uh", [F, F]), sb("w_ua", [F, F]), sb("w_u2", [F, F])
        w_g, w_lin = sb("w_g", [F, F]), sb("w_lin", [F, F])
        w_z1, w_z2 = sb("w_z1", [F, 2 * F]), sb("w_z2", [F, 2, F])
        w_s1, w_s2 = sb("w_s1", [F, F]), sb("w_s2", [F, F])
        c_mb1, c_mb3, c_ub1, c_sb1 = (sb(n, [F, 1]) for n in ("c_mb1", "c_mb3", "c_ub1", "c_sb1"))
        c_b1 = sb("c_b1", [F, 2])
        r_mb2, r_ub2, r_gamma, r_beta, r_gb, r_b2, r_sb2 = (
            sb(n, [P, F]) for n in ("r_mb2", "r_ub2", "r_gamma", "r_beta", "r_gb", "r_b2", "r_sb2"))
        o_lb = sb("o_lb", [1, CH, F])
        hist = sb("hist", [NHI, 4, HB])
        stat_rows = sb("stat_rows", [NT, P])
        dinv1 = sb("dinv1", [P, NT])
        dinv2 = sb("dinv2", [P, NT])
        idx = [sb(f"idx{b}", [P, G], I32) for b in range(2)]
        GA_all = sb("GA_all", [P, 2, G, F])
        GA = [GA_all[:, b] for b in range(2)]
        ER = [sb(f"ER{b}", [F, G * F]) for b in range(2)]
        DR = [ER[b][0:W, 0:G * P].bitcast(I32) for b in range(2)]
        SR = [ER[b][0:P, 0:G * P].bitcast(I32) for b in range(2)]
        R = [sb(f"R{b}", [F, G * P]) for b in range(2)]
        L = [sb(f"L{b}", [F, F]) for b in range(2)]
        OH = [sb(f"OH{b}", [P, G, W]) for b in range(2)]
        OHB = [sb(f"OHB{b}", [P, G, W], BF16) for b in range(2)]
        HHI = [sb(f"HHI{b}", [P, G, NHI], BF16) for b in range(2)]
        HLO = [sb(f"HLO{b}", [P, G, HB], BF16) for b in range(2)]
        A1 = [sb(f"A1_{b}", [F, G, F]) for b in range(2)]
        A2 = [sb(f"A2_{b}", [P, G, F]) for b in range(2)]
        A3f = [sb(f"A3_{b}", [F, G, F]) for b in range(2)]
        A3 = [A3f[b][0:P] for b in range(2)]
        SM = [sb(f"SM{b}", [P, G, P], BF16) for b in range(2)]
        SE = sb("SE", [P, G, P], BF16)
        earlier = sb("earlier", [P, G])
        to_spare = sb("to_spare", [P, G])
        move = sb("move", [P, G])
        left_rel = sb("left_rel", [P, G])
        LN = [{"six": sb(f"ln_six{i}", [P, CH, 6]), "mv": sb(f"ln_mv{i}", [P, CH, 2]),
               "var": sb(f"ln_var{i}", [P, CH]), "root": sb(f"ln_root{i}", [P, CH]),
               "scale": sb(f"ln_scale{i}", [P, CH]), "shift": sb(f"ln_shift{i}", [P, CH])} for i in range(4)]
        rows = A2
        out0 = [(GA[b], ER[b][0:P, :].rearrange("p (g f) -> p g f", f=F)) for b in range(2)]
        val_stage = A3[0]
        acc_stage = [ER[b][:, :].rearrange("p (g f) -> p g f", f=F) for b in range(2)]
        table_stage = sb("table_stage", [P, CH, F])
        zero_rows = sb("zero_rows", [NPAD - N, F])
        t_stage, agg_stage = A1[0], A1[1]
        z_stage = ER[1][:, :].rearrange("p (g f) -> p g f", f=F)
        hid_stage = A3f
        counts = [(R[b][:, :], ER[b][:, 0:CN]) for b in range(2)]
        sum_parts = [GA[0], GA[1], A1[0][0:P], A1[1][0:P], ER[0][0:P, :].rearrange("p (g f) -> p g f", f=F)]

        PS = ctx.enter_context(nc.psum_tensor("PS", [F, 8 * 512], F32))

        def tiles(bank, rows, inner=F):
            return PS[0:rows, bank * 512:bank * 512 + G * F].rearrange("p (g f) -> p g f", f=F)[:, :, 0:inner]

        IN_BANK = 512 // F
        BANK_TILES = 512 // (2 * F)
        PQ = PS[0:P, 2 * 512:2 * 512 + CH * 2 * F].rearrange("p (g f) -> p g f", f=2 * F)
        AGG = PS[:, 6 * 512:6 * 512 + W]
        HIST = PS[0:NHI, 7 * 512:7 * 512 + HB]
        TURNED = PS[0:P, 7 * 512 + HB:7 * 512 + HB + NT]

        def sems(prefix, names):
            return {n: sem(f"{prefix}_{n}") for n in names.split()}

        def slot_sems(prefix):
            return [sem(f"{prefix}{b}") for b in range(2)]

        idx_in, x_in, first_in, loads = sem("idx_in"), sem("x_in"), sem("first_in"), sem("loads")
        consts, zeroed, pads_zeroed = sem("consts"), sem("zeroed"), sem("pads_zeroed")
        waits_passed = sem("waits_passed")
        pool_chain, dve_chain = sem("pool_chain"), sem("dve_chain")
        neg_min_ready, neg_win_ready, win_ready = sem("neg_min_ready"), sem("neg_win_ready"), sem("win_ready")
        most_ready, most_everywhere, left_ready = sem("most_ready"), sem("most_everywhere"), sem("left_ready")
        st = sems("st", "counted stored loaded turned copied done")
        tables_stored, counts_in = slot_sems("tables_stored"), slot_sems("counts_in")
        parts_in = [sem(f"parts_in{i}") for i in range(3)]
        beta_added = sem("beta_added")
        e0 = sems("e0", "idx onehot onehot_t hist_in hist x1_win x1 g1 x2 y2 g2 agg added")
        e1 = sems("e1", "idx onehot hist_in hist agg added")
        e2 = sems("e2", "idx onehot same first_of pick picked rows rows_out earlier move")
        e3 = sems("e3", "idx onehot msg_in msg agg added")
        acc_done = [sem(f"acc_done{i}") for i in range(4)]
        gathered, attr_in, rows_in, window_in = (slot_sems(n) for n in ("gathered", "attr_in", "rows_in", "window_in"))
        PASS = NG // 2
        scattered = [sem(f"scattered{g}") for g in range(G)]
        x0 = Steps(sem("general0"), rel=1, masks=2, loaded=16 * 3 + 1, masks_t=1, x1=1, g1=1, x2=1, y2=1, g2=1,
                   agg=1, added=1)
        x1 = Steps(sem("general1"), rel=1, masks=2, loaded=1, agg=1, added=1)
        x2 = Steps(sem("general2"), loaded=16 * 2, rel=1, masks=2, first_of=2, earlier=1, move=1, idx=1, pick=1,
                   picked=1, rows=1, rows_out=1, sent=1)
        general_gathered, general_sent = sem("general_gathered"), sem("general_sent")
        x3 = Steps(sem("general3"), rel=1, masks=2, loaded=16 + 1, msg_in=1, msg=1, agg=1, added=1)
        LN_STEPS = "six mv var root scale shift applied"
        ln, ln_c = sems("ln", LN_STEPS), sems("ln_c", LN_STEPS)

        def after_norms(phases, s, steps=ln, bufs=0):
            return {**s, "ln": steps, "before": phases * NCH, "bufs": bufs}
        n0 = after_norms(0, sems("n0", "kept turn turned ht mm p_out q_out"))
        n1a = sems("n1a", "mm agg1 agg mm2 act mm3 y")
        n1b = after_norms(1, sems("n1b", "scaled x"))
        n1c = after_norms(0, sems("n1c", "turn acc stored"), ln_c, 2)
        n2 = after_norms(2, sems("n2", "acc_cp rooted b_added mm v x turn turned mm2 out stored"))
        n3 = after_norms(3, sems("n3", "pair s1 s2 s3 sum turn turned mm act mm2 x h_added stored turn2 ht acc_zero"))
        n4 = sems("n4", "b_added hh1 hh mm act mm2 out stored")

        def first_weights():
            yield w_pq[:, 0:F], mW1[0:F, :]
            yield w_pq[:, F:2 * F], mW1[F:2 * F, :]
            for row, v in ((r_beta, beta), (r_ub2, ub2)):
                yield row[:, :], v.rearrange("(a f) -> a f", a=1).to_broadcast([P, F])

        def weights():
            for b in range(2):
                yield L[b][W:F, :], mW1[2 * F:2 * F + FE, :]
            yield w_m2[:, :], mW2
            yield w_m3[:, :], mW3
            yield w_uh[:, :], uW1[0:F, :]
            yield w_ua[:, :], uW1[F:2 * F, :]
            yield w_u2[:, :], uW2
            yield w_g[:, :], gW
            yield w_lin[:, :], lin_w
            yield w_z1[:, :], w1
            for h in range(2):
                yield w_z2[:, h, :], w2[h * F:(h + 1) * F, :]
            yield w_s1[:, :], sW1
            yield w_s2[:, :], sW2
            for col, v in ((c_mb1, mb1), (c_mb3, mb3), (c_ub1, ub1), (c_sb1, sb1)):
                yield col[:, :], v.rearrange("(p a) -> p a", a=1)
            for h in range(2):
                yield c_b1[:, h:h + 1], b1[h * F:(h + 1) * F].rearrange("(p a) -> p a", a=1)
            for row, v in ((r_mb2, mb2), (r_gamma, gamma), (r_gb, gb), (r_b2, b2), (r_sb2, sb2)):
                yield row[:, :], v.rearrange("(a f) -> a f", a=1).to_broadcast([P, F])
            for row, v in ((o_lb, lin_b),):
                yield row[:, :, :], v.rearrange("(a t f) -> a t f", a=1, t=1).to_broadcast([1, CH, F])

        N_FIRST = 16 * len(list(first_weights()))
        N_LOADS = 16 * len(list(weights()))
        N_CONSTS = 11

        def node_rows(t, k):
            return t[bass.ds(k * CN, CN), :].rearrange("(t p) f -> p t f", p=P)

        def chunk(buf, k):
            return buf[:, bass.ds(k * CH, CH), :]

        def tile_of(buf, k, j):
            return buf[:, bass.ds(k * CH + j, 1), :].rearrange("p a f -> p (a f)")

        def chunk_t(buf, k):
            return buf[:, bass.ds(k * CN, CN)].rearrange("p (t n) -> p t n", n=P)

        def chunk_cols(buf, k):
            return buf[:, bass.ds(k * CH, CH)][:, :, None].to_broadcast([P, CH, F])

        def group(buf, c):
            return buf[:, bass.ds(c * G, G)]

        def over_groups(eng, body):
            body(0, True, False)
            with eng.Fori(1, NG // 2 - 1) as t:
                body(t, False, False)
            body(NG // 2 - 1, False, True)

        EARLY = NG // 4

        def over_groups_counting(eng, body, counts_done):
            body(0, True, False, True)
            with eng.Fori(1, EARLY) as t:
                body(t, False, False, True)
            counts_done()
            with eng.Fori(EARLY, NG // 2 - 1) as t:
                body(t, False, False, False)
            body(NG // 2 - 1, False, True, False)

        def over_chunks(eng, *stages):
            most = max(lag for lag, _ in stages)
            start = most + 2 + most % 2

            def a_round(i):
                for lag, stage in stages:
                    if 0 <= i - lag < NCH:
                        stage(i - lag, (i - lag) % 2, lambda n, k=i - lag: k >= n)
            for i in range(start):
                a_round(i)
            with eng.Fori(start // 2, NCH // 2) as h:
                for half in range(2):
                    for lag, stage in stages:
                        stage(2 * h + (half - lag), (half - lag) % 2, lambda n: True)
            for i in range(NCH, NCH + most):
                a_round(i)

        def slot_count(k, b, per):
            return (k - b) * (8 * per) + 16 * per

        def part_from_waits(eng):
            eng.sem_inc(waits_passed, 1)

        def tables_are_stored(eng):
            for b in range(2):
                eng.wait_ge(tables_stored[b], 16 * NCH)

        def general_path(eng, body, steps=None):
            eng.wait_ge(left_ready, 1)
            any_left = eng.value_load(leftI[0:1, 0:1], min_val=0, max_val=1)
            with eng.If(any_left > 0):
                with eng.Fori(0, SWEEPS) as s:
                    with eng.Fori(0, NG) as c:
                        body(s, c, s * NG + c + 1)
                if steps:
                    eng.wait_ge(steps.sem, steps.begin(SWEEPS * NG + 1))

        block = ctx.enter_context(nc.Block())

        @block.sync
        def _(sp):
            sp.dma_start(dstI[:, :], dst_g).then_inc(idx_in, 16)
            sp.dma_start(srcI[:, :], src_g).then_inc(idx_in, 16)
            with sp.Fori(0, NCH) as k:
                sp.dma_start(chunk(X, k), node_rows(x, k)).then_inc(x_in, 16)
            for to, frm in first_weights():
                sp.dma_start(to, frm).then_inc(first_in, 16)
            for to, frm in weights():
                sp.dma_start(to, frm).then_inc(loads, 16)

            def nodes0(k, b, had):
                sp.wait_ge(n0["p_out"], k + 1)
                sp.wait_ge(n0["q_out"], k + 1)
                sp.dma_start(node_rows(src_table0, k), out0[b][0]).then_inc(tables_stored[b], 16)
                sp.dma_start(node_rows(dst_table0, k), out0[b][1]).then_inc(tables_stored[b], 16)
            over_chunks(sp, (0, nodes0))
            tables_are_stored(sp)

            def load0(c, b, rows_sem, attr_sem):
                sp.dma_start(DR[b], dst_rows[bass.ds(c, 1), :].to_broadcast([W, G * P])).then_inc(rows_sem, 16)
                sp.dma_start(R[b][W:F, :], edge_attr_64_t[bass.ds(c * FE, FE), :]).then_inc(attr_sem, 16)

            def edges0(t, first, last):
                for b in range(2):
                    c = 2 * t + b
                    if not first:
                        sp.wait_ge(e0["onehot_t"], c - 1)
                        sp.wait_ge(e0["x1_win"], c - 1)
                    load0(c, b, rows_in[b], attr_in[b])
            over_groups(sp, edges0)

            def general0(s, c, n):
                sp.wait_ge(x0.sem, x0.after("masks", n))
                load0(c, 0, x0.sem, x0.sem)
            general_path(sp, general0)

            def store_stats(rows, n):
                for i, r in enumerate(rows):
                    sp.dma_start(stats[r:r + 1, :].rearrange("a (h l) -> (a h) l", l=HB),
                                 hist[:, i, :]).then_inc(st["stored"], 16)
                sp.wait_ge(st["stored"], 16 * n)
                r = rows[-1]
                sp.dma_start(stat_rows[:, :], stats[r:r + 1, 0:N].rearrange("a (t p) -> (a t) p", p=P)
                             ).then_inc(st["loaded"], 16)
            sp.wait_ge(st["counted"], 1)
            store_stats((0, 1, 2, 3), 4)

            sp.wait_ge(acc_done[0], 1)

            def counts1(k, b, had):
                if had(2):
                    sp.wait_ge(n1a["agg"], k - 1)
                for i in range(2):
                    sp.dma_start(counts[b][i], stats[i:i + 1, bass.ds(k * CN, CN)].to_broadcast([F, CN])
                                 ).then_inc(counts_in[b], 16)
            over_chunks(sp, (0, counts1))

            def table1_out(k, b, had):
                sp.wait_ge(ln_c["applied"], k + 1)
                sp.dma_start(node_rows(table1, k), table_stage[:, :, :]).then_inc(n1c["stored"], 16)
            over_chunks(sp, (0, table1_out))

            for g in range(G):
                if g:
                    with sp.Fori(0, NCH) as k:
                        sp.dma_start(node_rows(sums[g], k),
                                     zeros[:, :].rearrange("p (t f) -> p t f", f=F)).then_inc(zeroed, 16)
                sp.dma_start(sums[g][N:N + P, :], zeros[:, 0:F]).then_inc(zeroed, 16)
            sp.wait_ge(st["counted"], 2)
            store_stats((4,), 5)

            def nodes2(k, b, had):
                sp.wait_ge(n2["out"], k + 1)
                sp.dma_start(node_rows(table2, k), table_stage[:, :, :]).then_inc(n2["stored"], 16)
                sp.dma_start(node_rows(sums[0], k), table_stage[:, :, :]).then_inc(n2["stored"], 16)
            over_chunks(sp, (0, nodes2))

            def load2(c, b, rows_sem):
                sp.dma_start(SR[b], src_rows[bass.ds(c, 1), :].to_broadcast([P, G * P])).then_inc(rows_sem, 16)

            def edges2(t, first, last):
                for b in range(2):
                    c = 2 * t + b
                    if not first:
                        sp.wait_ge(e2["same"], c - 1)
                    load2(c, b, rows_in[b])
            over_groups(sp, edges2)

            def general2(s, c, n):
                sp.wait_ge(x2.sem, x2.begin(n))
                load2(c, 0, x2.sem)
            general_path(sp, general2)
            sp.wait_ge(acc_done[2], 1)

            def sums3(k, b, had):
                for i, parts in enumerate(((0, 1), (4,), (2, 3))):
                    if had(1):
                        sp.wait_ge(n3[("s1", "s2", "s3")[i]], k)
                    for g in parts:
                        sp.dma_start(sum_parts[g], node_rows(sums[g], k)).then_inc(parts_in[i], 16)
            over_chunks(sp, (0, sums3))

            sp.wait_ge(n3["mm"], NCH)

            def load3(c, b, attr_sem):
                sp.dma_start(ER[b][0:P, :], edge_attr_128[bass.ds(c * P * G, P * G), :]
                             .rearrange("(p g) f -> p (g f)", g=G)).then_inc(attr_sem, 16)

            def edges3(t, first, last):
                for b in range(2):
                    c = 2 * t + b
                    if not first:
                        sp.wait_ge(e3["msg_in"], c - 1)
                    load3(c, b, attr_in[b])
            over_groups(sp, edges3)

            def general3(s, c, n):
                sp.wait_ge(x3.sem, x3.after("masks", n))
                load3(c, 0, x3.sem)
            general_path(sp, general3)

            def counts4(k, b, had):
                if had(2):
                    sp.wait_ge(n4["hh1"], k - 1)
                sp.dma_start(counts[b][0], stats[2:3, bass.ds(k * CN, CN)].to_broadcast([F, CN])
                             ).then_inc(counts_in[b], 16)

            def result(k, b, had):
                sp.wait_ge(n4["out"], k + 1)
                sp.dma_start(node_rows(out, k), chunk(X, k)).then_inc(n4["stored"], 16)
            over_chunks(sp, (0, counts4), (4, result))
            sp.wait_ge(n4["stored"], 16 * NCH)
            sp.wait_ge(pads_zeroed, 16)

        @block.gpsimd
        def _(pool):
            ch = Chain(pool, pool_chain)
            pool.iota(iota_i[:, :], pattern=[[1, F]], base=0, channel_multiplier=0).then_inc(consts, 1)
            pool.iota(part_i[:, :], pattern=[[0, 1]], base=0, channel_multiplier=1).then_inc(consts, 1)
            pool.iota(sweep_i[:, :], pattern=[[W, NWIN]], base=0, channel_multiplier=0).then_inc(consts, 1)
            pool.memset(neg_half[:, :], -0.5).then_inc(consts, 1)
            ch.link(pool.memset(ident[:, :], 0.0))
            ch.link(pool.memset(before[:, :], 1.0))
            pool.affine_select(out=ident[:, :], in_=ident[:, :], compare_op=ALU.not_equal, fill=1.0, base=0,
                               pattern=[[-1, F]], channel_multiplier=1).then_inc(consts, 1)
            pool.affine_select(out=before[:, :], in_=before[:, :], compare_op=ALU.is_gt, fill=0.0, base=0,
                               pattern=[[-1, P]], channel_multiplier=1).then_inc(consts, 1)
            pool.memset(ones_row[:, :], 1.0).then_inc(consts, 1)
            pool.memset(zeros16[:, :], 0.0).then_inc(consts, 1)
            pool.memset(zeros[:, :], 0.0).then_inc(consts, 1)
            pool.memset(ACC[:, :], 0.0).then_inc(consts, 1)
            pool.memset(zero_rows[:, :], 0.0).then_inc(consts, 1)
            pool.wait_ge(neg_min_ready, 1)
            pool.partition_all_reduce(neg_win[:, :], neg_min[:, :], P, RMAX).then_inc(neg_win_ready, 1)
            pool.wait_ge(most_ready, 1)
            pool.partition_all_reduce(left_most[:, 1:2], left_most[:, 0:1], P, RMAX).then_inc(most_everywhere, 1)

            def inverse_root(s):
                def stage(k, b, had):
                    pool.wait_ge(s["ln"]["var"], s["before"] + k + 1)
                    buf = LN[s["bufs"] + b]
                    pool.tensor_tensor(buf["root"][:, :], buf["var"][:, :], neg_half[:, 0:CH], ALU.pow
                                       ).then_inc(s["ln"]["root"], 1)
                return stage

            def add_row(k, row, done):
                pool.tensor_tensor(chunk(X, k), chunk(X, k), row[:, None, :].to_broadcast([P, CH, F]), ALU.add
                                   ).then_inc(done, 1)

            def gather_group(b, table, done):
                for g in range(G):
                    pool.indirect_dma_start(out=GA[b][:, g, :], out_offset=None, in_=table,
                                            in_offset=bass.IndirectOffsetOnAxis(ap=idx[b][:, g:g + 1], axis=0)
                                            ).then_inc(done, 16)

            def gather(ready, table, read):
                def body(t, first, last):
                    for b in range(2):
                        c = 2 * t + b
                        pool.wait_ge(ready, c + 1)
                        if not first:
                            pool.wait_ge(read, c - 1)
                        part_from_waits(pool)
                        gather_group(b, table, gathered[b])
                over_groups(pool, body)

            def all_landed(moved):
                pool.wait_ge(moved, 16 * G)
                pool.inc_swdge_sem([moved], [16 * G], mode="sub")

            def gather_general(xs, table):
                def body(s, c, n):
                    pool.wait_ge(xs.sem, xs.after("masks", n))
                    part_from_waits(pool)
                    gather_group(0, table, general_gathered)
                    all_landed(general_gathered)
                    pool.sem_inc(xs.sem, 1)
                general_path(pool, body)

            def keep0(k, b, had):
                pool.wait_ge(ln["applied"], n0["before"] + k + 1)
                pool.tensor_tensor(chunk(H, k), rows[b][:, :, :], r_ub2[:, None, :].to_broadcast([P, CH, F]), ALU.add
                                   ).then_inc(n0["kept"], 1)
            pool.wait_ge(first_in, N_FIRST)
            over_chunks(pool, (0, inverse_root(n0)), (1, keep0))

            tables_are_stored(pool)
            gather(e0["idx"], src_table0, e0["x1"])
            gather_general(x0, src_table0)

            pool.wait_ge(st["copied"], 1)
            pool.tensor_tensor(dinv1[:, :], dinv1[:, :], neg_half[:, 0:NT], ALU.pow).then_inc(st["done"], 1)

            def scaled1(k, b, had):
                pool.wait_ge(ln["applied"], n1b["before"] + k + 1)
                pool.tensor_tensor(rows[b][:, :, :], rows[b][:, :, :], r_gamma[:, None, :].to_broadcast([P, CH, F]),
                                   ALU.mult).then_inc(n1b["scaled"], 1)
            over_chunks(pool, (0, inverse_root(n1b)), (1, scaled1), (2, inverse_root(n1c)))

            pool.wait_ge(n1c["stored"], 16 * NCH)
            gather(e1["idx"], table1, e1["agg"])
            gather_general(x1, table1)

            def root_counts2(k, b, had):
                d = dinv2[:, bass.ds(k * CH, CH)]
                pool.tensor_tensor(d, d, neg_half[:, 0:CH], ALU.pow).then_inc(n2["rooted"], 1)

            def bias2(k, b, had):
                pool.wait_ge(ln["applied"], n2["before"] + k + 1)
                add_row(k, r_b2, n2["b_added"])
            pool.wait_ge(st["copied"], 2)
            over_chunks(pool, (0, inverse_root(n2)), (0, root_counts2), (1, bias2))
            pool.wait_ge(n2["acc_cp"], NCH)
            pool.wait_ge(n2["stored"], 32 * NCH)
            pool.wait_ge(zeroed, 16 * (G + (G - 1) * NCH))

            def scatter_tile(b, g, done):
                pool.indirect_dma_start(
                    out=sums[g], out_offset=bass.IndirectOffsetOnAxis(ap=idx[b][:, g:g + 1], axis=0),
                    in_=A3[b][:, g, :], in_offset=None, compute_op=ALU.add).then_inc(done, 16)

            def scatter(t, first, last):
                for b in range(2):
                    c = 2 * t + b
                    pool.wait_ge(e2["idx"], c + 1)
                    pool.wait_ge(e2["rows_out"], c + 1)
                    for g in range(G):
                        if not (first and b == 0):
                            pool.wait_ge(scattered[g], 16 * c)
                        part_from_waits(pool)
                        scatter_tile(b, g, scattered[g])
            over_groups(pool, scatter)
            for g in range(G):
                pool.wait_ge(scattered[g], 16 * NG)
            pool.sem_inc(x2.sem, 1)

            def scatter_general(s, c, n):
                pool.wait_ge(x2.sem, x2.after("rows_out", n))
                part_from_waits(pool)
                for g in range(G):
                    scatter_tile(0, g, general_sent)
                all_landed(general_sent)
                pool.sem_inc(x2.sem, 1)
            general_path(pool, scatter_general)
            pool.sem_inc(acc_done[2], 1)

            pool.memset(ACC[:, :], 0.0).then_inc(n3["acc_zero"], 1)

            def pair3(k, b, had):
                pool.wait_ge(parts_in[2], 32 * (k + 1))
                pool.tensor_tensor(sum_parts[2], sum_parts[2], sum_parts[3], ALU.add).then_inc(n3["pair"], 1)

            def add_h(k, b, had):
                pool.wait_ge(ln["applied"], n3["before"] + k + 1)
                pool.tensor_tensor(chunk(X, k), chunk(X, k), table_stage[:, :, :], ALU.add).then_inc(n3["h_added"], 1)
            over_chunks(pool, (0, pair3), (2, inverse_root(n3)), (4, add_h))

            pool.wait_ge(n3["stored"], 16 * NCH)
            gather(e3["idx"], table3, e3["msg_in"])
            gather_general(x3, table3)

            def bias4(k, b, had):
                add_row(k, r_sb2, n4["b_added"])
            pool.wait_ge(n3["h_added"], NCH)
            over_chunks(pool, (0, bias4))

        @block.scalar
        def _(act):
            fn = nc.scalar.activation

            def normalize(s, frm, to, func, k, b):
                buf = LN[s["bufs"] + b]
                act.wait_ge(s["ln"]["shift"], s["before"] + k + 1)
                for j in range(CH):
                    last = fn(to(j), frm(j), func, scale=buf["scale"][:, j:j + 1], bias=buf["shift"][:, j:j + 1])
                last.then_inc(s["ln"]["applied"], 1)

            def turned0(k, b, had):
                act.wait_ge(n0["turn"], k + 1)
                if had(2):
                    act.wait_ge(n0["mm"], k - 1)
                    act.wait_ge(n0["ht"], k - 1)
                fn(A1[b][:, :, 0:P], tiles(0, F, P), ACT.Copy).then_inc(n0["turned"], 1)

            def apply0(k, b, had):
                if had(2):
                    act.wait_ge(n0["turn"], k - 1)
                    act.wait_ge(n0["kept"], k - 1)
                normalize(n0, lambda j: tile_of(X, k, j), lambda j: rows[b][:, j, :], ACT.Relu, k, b)

            def pq_out0(k, b, had):
                act.wait_ge(n0["mm"], k + 1)
                if had(2):
                    act.wait_ge(tables_stored[b], slot_count(k, b, 2) - 32)
                n = 2 * BANK_TILES
                fn(out0[b][0][:, 0:n, :], PQ[:, 0:n, 0:F], ACT.Copy)
                fn(out0[b][1][:, 0:n, :], PQ[:, 0:n, F:2 * F], ACT.Copy).then_inc(n0["p_out"], 1)
            over_chunks(act, (0, apply0), (1, turned0), (2, pq_out0))

            def window(sem_in, lo, b, table):
                act.dma_start(L[b][0:W, :], table[bass.ds(lo, W), :]).then_inc(sem_in, 16)

            def group_window(c, b, table):
                lo = act.value_load(winI[0:1, bass.ds(c, 1)], min_val=0, max_val=N - W)
                window(window_in[b], lo, b, table)

            act.wait_ge(consts, N_CONSTS)
            act.dma_start(dst_table0[N:NPAD, :], zero_rows[:, :]).then_inc(pads_zeroed, 16)
            act.dma_start(table2[N:NPAD, :], zero_rows[:, :]).then_inc(pads_zeroed, 16)
            act.wait_ge(pads_zeroed, 32)
            act.wait_ge(loads, N_LOADS)
            act.wait_ge(win_ready, 1)
            tables_are_stored(act)
            for b in range(2):
                group_window(b, b, dst_table0)

            def edges0(t, first, last):
                for b in range(2):
                    c = 2 * t + b
                    act.wait_ge(e0["x1"], c + 1)
                    if not first:
                        act.wait_ge(e0["x2"], c - 1)
                    fn(A1[b][:, :, 0:P], tiles(2 * b, F, P), ACT.Gelu_apprx_tanh, bias=c_mb1[:, :]
                       ).then_inc(e0["g1"], 1)
                    if not last:
                        group_window(c + 2, b, dst_table0)
                    act.wait_ge(e0["y2"], c + 1)
                    if not first:
                        act.wait_ge(e0["agg"], c - 1)
                    fn(A3[b][:, :, :], A2[b][:, :, :], ACT.Gelu_apprx_tanh).then_inc(e0["g2"], 1)
            over_groups(act, edges0)

            def general0(s, c, n):
                act.wait_ge(x0.sem, x0.after("masks", n))
                window(x0.sem, s * W, 0, dst_table0)
                act.wait_ge(x0.sem, x0.after("x1", n))
                fn(A1[0][:, :, 0:P], tiles(0, F, P), ACT.Gelu_apprx_tanh, bias=c_mb1[:, :]).then_inc(x0.sem, 1)
                act.wait_ge(x0.sem, x0.after("y2", n))
                fn(A3[0][:, :, :], A2[0][:, :, :], ACT.Gelu_apprx_tanh).then_inc(x0.sem, 1)
            general_path(act, general0)
            act.wait_ge(st["turned"], 1)
            fn(dinv1[:, :], TURNED, ACT.Copy).then_inc(st["copied"], 1)

            def act1(k, b, had):
                act.wait_ge(n1a["mm2"], k + 1)
                if had(1):
                    act.wait_ge(n1a["mm3"], k)
                fn(t_stage[:, :, 0:P], tiles(2, F, P), ACT.Gelu_apprx_tanh, bias=c_ub1[:, :]).then_inc(n1a["act"], 1)
            over_chunks(act, (0, act1))

            def apply1(k, b, had):
                if had(2):
                    act.wait_ge(n1b["x"], k - 1)
                normalize(n1b, lambda j: tile_of(H, k, j), lambda j: rows[b][:, j, :], ACT.Identity, k, b)

            def apply_table1(k, b, had):
                if had(1):
                    act.wait_ge(n1c["turn"], k)
                    act.wait_ge(n1c["stored"], 16 * k)
                normalize(n1c, lambda j: tile_of(X, k, j), lambda j: table_stage[:, j, :], ACT.Relu, k, b)

            def self_loop1(k, b, had):
                act.wait_ge(n1c["turn"], k + 1)
                fn(chunk_t(ACC, k), tiles(6, F, P), ACT.Copy).then_inc(n1c["acc"], 1)
            over_chunks(act, (0, apply1), (2, apply_table1), (3, self_loop1))

            act.wait_ge(st["turned"], 2)
            fn(dinv2[:, :], TURNED, ACT.Copy).then_inc(st["copied"], 1)

            act.wait_ge(acc_done[1], 1)

            def acc_copy2(k, b, had):
                if had(2):
                    act.wait_ge(n2["mm"], k - 1)
                fn(acc_stage[b][:, :, 0:P], chunk_t(ACC, k), ACT.Copy).then_inc(n2["acc_cp"], 1)

            def apply2(k, b, had):
                if had(2):
                    act.wait_ge(n2["turn"], k - 1)
                normalize(n2, lambda j: tile_of(X, k, j), lambda j: rows[b][:, j, :], ACT.Relu, k, b)

            def turned2(k, b, had):
                act.wait_ge(n2["turn"], k + 1)
                if had(2):
                    act.wait_ge(n2["mm2"], k - 1)
                fn(A1[b][:, :, 0:P], tiles(2, F, P), ACT.Copy).then_inc(n2["turned"], 1)
            over_chunks(act, (0, acc_copy2), (3, apply2), (3, turned2))

            act.wait_ge(n2["stored"], 32 * NCH)
            for b in range(2):
                group_window(b, b, table2)

            def picked(c, b, later):
                act.wait_ge(e2["pick"], c + 1)
                if later:
                    act.wait_ge(e2["rows"], c - 1)
                fn(A1[b][0:W, :, 0:P], tiles(2 * b, W, P), ACT.Copy).then_inc(e2["picked"], 1)
            picked(0, 0, False)

            def edges2(t, first, last):
                for b in range(2):
                    c = 2 * t + b
                    act.wait_ge(e2["rows"], c + 1)
                    if not first:
                        for g in range(G):
                            act.wait_ge(scattered[g], 16 * (c - 1))
                    fn(A3[b][:, :, :], tiles(4, P), ACT.Copy).then_inc(e2["rows_out"], 1)
                    if not last:
                        group_window(c + 2, b, table2)
                    if not (last and b == 1):
                        picked(c + 1, 1 - b, not (first and b == 0))
            over_groups(act, edges2)

            def general2(s, c, n):
                act.wait_ge(x2.sem, x2.begin(n))
                window(x2.sem, s * W, 0, table2)
                act.wait_ge(x2.sem, x2.after("pick", n))
                fn(A1[0][0:W, :, 0:P], tiles(0, W, P), ACT.Copy).then_inc(x2.sem, 1)
                act.wait_ge(x2.sem, x2.after("rows", n))
                fn(A3[0][:, :, :], tiles(4, P), ACT.Copy).then_inc(x2.sem, 1)
            general_path(act, general2)

            def turned3(k, b, had):
                act.wait_ge(n3["turn"], k + 1)
                if had(1):
                    act.wait_ge(n3["mm"], k)
                fn(z_stage[:, :, 0:P], tiles(6, F, P), ACT.Relu).then_inc(n3["turned"], 1)

            def hidden3(k, b, had):
                act.wait_ge(n3["mm"], k + 1)
                if had(1):
                    act.wait_ge(n3["mm2"], k)
                for h in range(2):
                    fn(hid_stage[h][:, :, 0:P], tiles(2 + 2 * h, F, P), ACT.Relu, bias=c_b1[:, h:h + 1]
                       ).then_inc(n3["act"], 1)

            def apply3(k, b, had):
                if had(1):
                    act.wait_ge(n3["stored"], 16 * k)
                    act.wait_ge(n3["turn2"], k)
                    act.wait_ge(n3["h_added"], k)
                normalize(n3, lambda j: tile_of(X, k, j), lambda j: table_stage[:, j, :], ACT.Relu, k, b)

            def ht3(k, b, had):
                act.wait_ge(n3["turn2"], k + 1)
                fn(chunk_t(HT, k), tiles(6, F, P), ACT.Copy).then_inc(n3["ht"], 1)

            def table3_out(k, b, had):
                act.wait_ge(ln["applied"], n3["before"] + k + 1)
                act.dma_start(node_rows(table3, k), table_stage[:, :, :]).then_inc(n3["stored"], 16)
            over_chunks(act, (0, turned3), (3, apply3), (0, hidden3), (3, table3_out), (3, ht3))

            def edges3(t, first, last):
                for b in range(2):
                    c = 2 * t + b
                    act.wait_ge(e3["msg_in"], c + 1)
                    if not first:
                        act.wait_ge(e3["agg"], c - 1)
                    fn(A3[b][:, :, :], A2[b][:, :, :], ACT.Silu).then_inc(e3["msg"], 1)
            over_groups(act, edges3)

            def general3(s, c, n):
                act.wait_ge(x3.sem, x3.after("msg_in", n))
                fn(A3[0][:, :, :], A2[0][:, :, :], ACT.Silu).then_inc(x3.sem, 1)
            general_path(act, general3)

            def act4(k, b, had):
                act.wait_ge(n4["mm"], k + 1)
                if had(1):
                    act.wait_ge(n4["mm2"], k)
                fn(t_stage[:, :, 0:P], tiles(0, F, P), ACT.Silu, bias=c_sb1[:, :]).then_inc(n4["act"], 1)
            over_chunks(act, (0, act4))

        @block.vector
        def _(dve):
            v = nc.vector
            ch = Chain(dve, dve_chain)

            def statistics(s, frm, k, b, had):
                buf, steps, n = LN[s["bufs"] + b], s["ln"], s["before"] + k
                if had(2):
                    dve.wait_ge(steps["shift"], n - 1)
                part_from_waits(dve)
                for j in range(CH):
                    last = v.bn_stats(buf["six"][:, j, :], frm(j))
                last.then_inc(steps["six"], 1)
                dve.wait_ge(steps["six"], n + 1)
                part_from_waits(dve)
                for j in range(CH):
                    last = v.bn_aggr(buf["mv"][:, j, :], buf["six"][:, j, :])
                last.then_inc(steps["mv"], 1)
                dve.wait_ge(steps["mv"], n + 1)
                v.tensor_scalar(buf["var"][:, :], buf["mv"][:, :, 1], LN_EPS, None, ALU.add).then_inc(steps["var"], 1)

            def scale_shift(s, times=None):
                def stage(k, b, had):
                    buf, steps, n = LN[s["bufs"] + b], s["ln"], s["before"] + k
                    dve.wait_ge(steps["root"], n + 1)
                    if had(2):
                        dve.wait_ge(steps["applied"], n - 1)
                    if times is None:
                        v.tensor_copy(buf["scale"][:, :], buf["root"][:, :]).then_inc(steps["scale"], 1)
                    else:
                        v.tensor_tensor(buf["scale"][:, :], buf["root"][:, :], times[:, bass.ds(k * CH, CH)], ALU.mult
                                        ).then_inc(steps["scale"], 1)
                    dve.wait_ge(steps["scale"], n + 1)
                    v.scalar_tensor_tensor(buf["shift"][:, :], buf["mv"][:, :, 0], -1.0, buf["scale"][:, :],
                                           ALU.mult, ALU.mult).then_inc(steps["shift"], 1)
                return stage

            def split(nodes):
                ch.link(v.tensor_scalar(part_of[:, :], nodes, HB.bit_length() - 1, None, ALU.arith_shift_right))
                ch.link(v.tensor_copy(high[:, :], part_of[:, :]))
                ch.link(v.tensor_scalar(part_of[:, :], nodes, HB - 1, None, ALU.bitwise_and))
                ch.link(v.tensor_copy(low[:, :], part_of[:, :]))

            def one_hot(to, values, width):
                return v.tensor_tensor(to, iota[:, None, 0:width].to_broadcast([P, G, width]),
                                       values[:, :, None].to_broadcast([P, G, width]), ALU.is_equal)

            def histogram(s, c, b, later):
                if later:
                    dve.wait_ge(s["hist"], c - 1)
                one_hot(HHI[b][:, :, :], group(high, c), NHI)
                one_hot(HLO[b][:, :, :], group(low, c), HB).then_inc(s["hist_in"], 1)

            def window_one_hot(s, to, c, b, read, later):
                if later:
                    dve.wait_ge(read, c - 1)
                one_hot(to[b][:, :, :], group(dst_rel, c), W).then_inc(s["onehot"], 1)

            def add_window(s, c, none_before):
                lo = dve.value_load(winI[0:1, bass.ds(c, 1)], min_val=0, max_val=N - W)
                dve.wait_ge(s["agg"], c + 1)
                if not none_before:
                    dve.wait_ge(s["added"], c)
                v.tensor_tensor(ACC[:, bass.ds(lo, W)], ACC[:, bass.ds(lo, W)], AGG, ALU.add).then_inc(s["added"], 1)

            def source_indices(ready, c, b):
                v.tensor_copy(idx[b][:, :], group(srcI, c)).then_inc(ready, 1)

            def general_masks(xs, to, s, c, n):
                dve.wait_ge(xs.sem, xs.begin(n) if xs is not x2 else xs.after("loaded", n))
                v.tensor_scalar(left_rel[:, :], group(left, c), sweep_win[:, bass.ds(s, 1)], None, ALU.subtract
                                ).then_inc(xs.sem, 1)
                dve.wait_ge(xs.sem, xs.after("rel", n))
                one_hot(to[0][:, :, :], left_rel, W).then_inc(xs.sem, 1)

            def general_add(xs, s, n):
                dve.wait_ge(xs.sem, xs.after("agg", n))
                v.tensor_tensor(ACC[:, bass.ds(s * W, W)], ACC[:, bass.ds(s * W, W)], AGG, ALU.add
                                ).then_inc(xs.sem, 1)

            def finish_edges(i, s, xs, body):
                dve.wait_ge(s["added"], NG)
                dve.sem_inc(xs.sem, 1)
                general_path(dve, body, xs)
                dve.sem_inc(acc_done[i], 1)

            dve.wait_ge(idx_in, 32)
            v.tensor_reduce(neg_min[:, :], dstI[:, :].rearrange("p (c g) -> p c g", g=G), AX.X, ALU.min, negate=True
                            ).then_inc(neg_min_ready, 1)
            dve.wait_ge(consts, N_CONSTS)
            ch.link(v.tensor_copy(iota[:, :], iota_i[:, :]))
            ch.link(v.tensor_copy(part[:, :], part_i[:, :]))
            ch.link(v.tensor_copy(sweep_win[:, :], sweep_i[:, :]))
            ch.link(v.tensor_scalar(sweep_node[:, :], sweep_win[:, :], part[:, :], None, ALU.add))
            ch.link(v.tensor_scalar(spare_row[:, :], part[:, :], float(N), None, ALU.add))
            split(dstI[:, :])
            dve.wait_ge(neg_win_ready, 1)
            ch.link(v.tensor_scalar(neg_win[:, :], neg_win[:, :], float(W - N), None, ALU.max))
            v.tensor_scalar(winI[:, :], neg_win[0:1, :], -1.0, None, ALU.mult).then_inc(win_ready, 1)
            ch.link(v.tensor_scalar(win_node[:, :], neg_win[:, :], -1.0, part[:, :], ALU.mult, ALU.add))
            ch.link(v.tensor_tensor(dst_rel[:, :].rearrange("p (c g) -> p c g", g=G),
                                    dstI[:, :].rearrange("p (c g) -> p c g", g=G),
                                    neg_win[:, :, None].to_broadcast([P, NG, G]), ALU.add))
            v.tensor_reduce(left_most[:, 0:1], dst_rel[:, :], AX.X, ALU.max).then_inc(most_ready, 1)
            ch.link(v.tensor_scalar(left[:, :], dst_rel[:, :], float(W), None, ALU.is_ge))
            ch.link(v.scalar_tensor_tensor(left[:, :], dstI[:, :], 1.0, left[:, :], ALU.add, ALU.mult))
            ch.link(v.tensor_scalar(left[:, :], left[:, :], -1.0, None, ALU.add))
            dve.wait_ge(most_everywhere, 1)
            v.tensor_scalar(leftI[:, :], left_most[0:1, 1:2], float(W), None, ALU.is_ge).then_inc(left_ready, 1)
            dve.wait_ge(win_ready, 1)
            dve.wait_ge(x_in, 16 * NCH)

            def statistics0(k, b, had):
                statistics(n0, lambda j: tile_of(X, k, j), k, b, had)

            def tail0(k, b, had):
                dve.wait_ge(n0["turned"], k + 1)
                v.tensor_copy(chunk_t(HT, k), A1[b][:, :, 0:P]).then_inc(n0["ht"], 1)
                dve.wait_ge(n0["mm"], k + 1)
                if had(2):
                    dve.wait_ge(tables_stored[b], slot_count(k, b, 2) - 32)
                n = 2 * BANK_TILES
                v.tensor_copy(out0[b][0][:, n:CH, :], PQ[:, n:CH, 0:F])
                v.tensor_copy(out0[b][1][:, n:CH, :], PQ[:, n:CH, F:2 * F]).then_inc(n0["q_out"], 1)
            over_chunks(dve, (1, scale_shift(n0)), (0, statistics0), (3, tail0))

            def one_hot_turned(c, b, t, first):
                dve.wait_ge(rows_in[b], 16 * (t + 1))
                if not first:
                    dve.wait_ge(e0["x1_win"], c - 1)
                v.tensor_scalar(R[b][0:W, :], DR[b], win_node[0:W, bass.ds(c, 1)], None, ALU.is_equal
                                ).then_inc(e0["onehot_t"], 1)

            dve.wait_ge(loads, N_LOADS)
            tables_are_stored(dve)
            dve.wait_ge(n0["kept"], NCH)
            for b in range(2):
                source_indices(e0["idx"], b, b)
            v.tensor_tensor(X[:, :, :], X[:, :, :], r_beta[:, None, :].to_broadcast([P, NT, F]), ALU.add
                            ).then_inc(beta_added, 1)
            for b in range(2):
                one_hot_turned(b, b, 0, True)
                histogram(e0, b, b, False)

            def mlp_bias(b):
                return v.tensor_tensor(A2[b][:, :, :], tiles(4, P), r_mb2[:, None, :].to_broadcast([P, G, F]), ALU.add)

            def edges0(t, first, last):
                for b in range(2):
                    c = 2 * t + b
                    if not last:
                        dve.wait_ge(gathered[b], 16 * G * (t + 1))
                        source_indices(e0["idx"], c + 2, b)
                    window_one_hot(e0, OH, c, b, e0["agg"], not first)
                    dve.wait_ge(e0["x2"], c + 1)
                    if not first:
                        dve.wait_ge(e0["g2"], c - 1)
                    mlp_bias(b).then_inc(e0["y2"], 1)
                    if not (first and b == 0):
                        add_window(e0, c - 1, first and b == 1)
                    if not last:
                        one_hot_turned(c + 2, b, t + 1, False)
                        histogram(e0, c + 2, b, True)

            def counts_by_destination():
                dve.wait_ge(e0["hist"], NG + 1)
                ch.link(v.tensor_copy(hist[:, 0, :], HIST))
                ch.link(v.tensor_scalar(hist[:, 1, :], hist[:, 0, :], 1e-8, None, ALU.add))
                ch.link(v.reciprocal(hist[:, 1, :], hist[:, 1, :]))
                ch.link(v.tensor_scalar(hist[:, 2, :], hist[:, 0, :], 1.0, None, ALU.max))
                ch.link(v.reciprocal(hist[:, 2, :], hist[:, 2, :]))
                v.tensor_scalar(hist[:, 3, :], hist[:, 0, :], 1.0, None, ALU.add).then_inc(st["counted"], 1)
            over_groups(dve, edges0)
            counts_by_destination()
            add_window(e0, NG - 1, False)

            def general0(s, c, n):
                general_masks(x0, OH, s, c, n)
                source_indices(x0.sem, c, 0)
                dve.wait_ge(x0.sem, x0.after("loaded", n))
                v.tensor_scalar(R[0][0:W, :], DR[0], sweep_node[0:W, bass.ds(s, 1)], None, ALU.is_equal
                                ).then_inc(x0.sem, 1)
                dve.wait_ge(x0.sem, x0.after("x2", n))
                mlp_bias(0).then_inc(x0.sem, 1)
                general_add(x0, s, n)
            finish_edges(0, e0, x0, general0)


            split(srcI[:, :])

            def agg1(k, b, had):
                dve.wait_ge(counts_in[b], slot_count(k, b, 2))
                dve.wait_ge(n1a["mm"], k + 1)
                if had(1):
                    dve.wait_ge(n1a["mm2"], k)
                cnt, inv = (c.rearrange("p (t n) -> p t n", n=P) for c in counts[b])
                agg = agg_stage[:, :, 0:P]
                v.scalar_tensor_tensor(agg, cnt, c_mb3[:, :], tiles(0, F, P), ALU.mult, ALU.add
                                       ).then_inc(n1a["agg1"], 1)
                dve.wait_ge(n1a["agg1"], k + 1)
                v.tensor_tensor(agg, agg, inv, ALU.mult).then_inc(n1a["agg"], 1)

            def residual1(k, b, had):
                dve.wait_ge(n1a["mm3"], k + 1)
                v.tensor_tensor(chunk(H, k), chunk(H, k), tiles(4, P), ALU.add).then_inc(n1a["y"], 1)
            over_chunks(dve, (0, agg1), (1, residual1))

            dve.wait_ge(n1a["y"], NCH)
            dve.wait_ge(beta_added, 1)
            dve.wait_ge(st["done"], 1)

            def statistics1(k, b, had):
                statistics(n1b, lambda j: tile_of(H, k, j), k, b, had)

            def x1_sum(k, b, had):
                dve.wait_ge(n1b["scaled"], k + 1)
                v.tensor_tensor(chunk(X, k), chunk(X, k), rows[b][:, :, :], ALU.add).then_inc(n1b["x"], 1)
                dve.wait_ge(n1b["x"], k + 1)
                statistics(n1c, lambda j: tile_of(X, k, j), k, b, had)
            over_chunks(dve, (1, scale_shift(n1b)), (0, statistics1), (3, scale_shift(n1c, dinv1)), (2, x1_sum))

            dve.wait_ge(n1c["acc"], NCH)
            for b in range(2):
                source_indices(e1["idx"], b, b)

            def edges1(t, first, last, early):
                for b in range(2):
                    c = 2 * t + b
                    window_one_hot(e1, OH, c, b, e1["agg"], not first)
                    for r in range(2 * early):
                        histogram(e1, 2 * c + r, r, not (first and b == 0))
                    if not (first and b == 0):
                        add_window(e1, c - 1, first and b == 1)
                    if not last:
                        dve.wait_ge(gathered[b], 16 * G * (PASS + t + 1))
                        source_indices(e1["idx"], c + 2, b)

            def counts_by_source():
                for r in range(NG - 4 * EARLY):
                    histogram(e1, 4 * EARLY + r, r, True)
                dve.wait_ge(e1["hist"], NG + 1)
                dve.wait_ge(st["stored"], 16 * 4)
                v.tensor_scalar(hist[:, 0, :], HIST, 1.0, None, ALU.add).then_inc(st["counted"], 1)
            over_groups_counting(dve, edges1, counts_by_source)
            add_window(e1, NG - 1, False)

            def general1(s, c, n):
                general_masks(x1, OH, s, c, n)
                source_indices(x1.sem, c, 0)
                general_add(x1, s, n)
            finish_edges(1, e1, x1, general1)

            def x2_sum(k, b, had):
                dve.wait_ge(n2["mm"], k + 1)
                if had(1):
                    dve.wait_ge(n2["x"], k)
                for j in range(CH):
                    last = v.scalar_tensor_tensor(val_stage[:, j, :], tiles(0, P)[:, j, :],
                                                  dinv1[:, bass.ds(k * CH + j, 1)], r_gb[:, :], ALU.mult, ALU.add)
                last.then_inc(n2["v"], 1)
                dve.wait_ge(n2["v"], k + 1)
                v.scalar_tensor_tensor(chunk(X, k), val_stage[:, :, :], 0.0, chunk(X, k), ALU.max, ALU.add
                                       ).then_inc(n2["x"], 1)
                dve.wait_ge(n2["x"], k + 1)
                statistics(n2, lambda j: tile_of(X, k, j), k, b, had)

            def table2_rows(k, b, had):
                dve.wait_ge(n2["mm2"], k + 1)
                dve.wait_ge(n2["rooted"], k + 1)
                if had(1):
                    dve.wait_ge(n2["stored"], 32 * k)
                v.tensor_tensor(table_stage[:, :, :], tiles(4, P), chunk_cols(dinv2, k), ALU.mult
                                ).then_inc(n2["out"], 1)
            dve.wait_ge(n1c["stored"], 16 * NCH)
            over_chunks(dve, (3, table2_rows), (1, scale_shift(n2)), (0, x2_sum))

            def same_source(c, b, t, later):
                window_one_hot(e2, OHB, c, b, e2["pick"], later)
                dve.wait_ge(rows_in[b], 16 * (PASS + t + 1))
                v.tensor_tensor(SM[b][:, :, :], SR[b].rearrange("p (g e) -> p g e", g=G),
                                group(srcI, c)[:, :, None].to_broadcast([P, G, P]), ALU.is_equal
                                ).then_inc(e2["same"], 1)

            def sum_rows(done, c, b):
                v.tensor_tensor(SE[:, :, :], SM[b][:, :, :], before[:, None, :].to_broadcast([P, G, P]), ALU.mult
                                ).then_inc(done("first_of")[0], 1)
                v.tensor_scalar(to_spare[:, :], group(srcI, c), -1.0, spare_row[:, :], ALU.mult, ALU.add
                                ).then_inc(done("first_of")[0], 1)
                dve.wait_ge(*done("first_of"))
                v.tensor_reduce(earlier[:, :], SE[:, :, :], AX.X, ALU.add).then_inc(done("earlier")[0], 1)
                dve.wait_ge(*done("earlier"))
                v.scalar_tensor_tensor(move[:, :], earlier[:, :], 0.0, to_spare[:, :], ALU.is_gt, ALU.mult
                                       ).then_inc(done("move")[0], 1)
                dve.wait_ge(*done("move"))

            def sum_indices(ready, c, b):
                v.tensor_tensor(idx[b][:, :], group(srcI, c), move[:, :], ALU.add).then_inc(ready, 1)

            def done_by(n):
                return lambda step: (e2[step], 2 * n if step == "first_of" else n)
            same_source(0, 0, 0, False)

            def edges2(t, first, last):
                for b in range(2):
                    c = 2 * t + b
                    if not (last and b == 1):
                        same_source(c + 1, 1 - b, t + b, not (first and b == 0))
                    if not (first and b == 0):
                        dve.wait_ge(e2["idx"], c)
                    dve.wait_ge(e2["same"], c + 1)
                    sum_rows(done_by(c + 1), c, b)
                    if not first:
                        for g in range(G):
                            dve.wait_ge(scattered[g], 16 * (c - 1))
                    sum_indices(e2["idx"], c, b)
            over_groups(dve, edges2)

            def general2(s, c, n):
                general_masks(x2, OHB, s, c, n)
                v.tensor_tensor(SM[0][:, :, :], SR[0].rearrange("p (g e) -> p g e", g=G),
                                group(srcI, c)[:, :, None].to_broadcast([P, G, P]), ALU.is_equal
                                ).then_inc(x2.sem, 1)
                dve.wait_ge(x2.sem, x2.after("masks", n))
                sum_rows(lambda step: (x2.sem, x2.after(step, n)), c, 0)
                sum_indices(x2.sem, c, 0)
            general_path(dve, general2)

            def sum3(k, b, had):
                s = rows[b][:, :, :]
                dve.wait_ge(parts_in[0], 32 * (k + 1))
                if had(2):
                    dve.wait_ge(n3["turn"], k - 1)
                v.tensor_tensor(s, sum_parts[0], sum_parts[1], ALU.add).then_inc(n3["s1"], 1)
                dve.wait_ge(n3["s1"], k + 1)
                dve.wait_ge(parts_in[1], 16 * (k + 1))
                v.tensor_tensor(s, s, sum_parts[4], ALU.add).then_inc(n3["s2"], 1)
                dve.wait_ge(n3["s2"], k + 1)
                dve.wait_ge(n3["pair"], k + 1)
                v.tensor_tensor(s, s, sum_parts[2], ALU.add).then_inc(n3["s3"], 1)
                dve.wait_ge(n3["s3"], k + 1)
                v.tensor_tensor(s, s, chunk_cols(dinv2, k), ALU.mult).then_inc(n3["sum"], 1)

            def x3_sum(k, b, had):
                dve.wait_ge(n3["mm2"], k + 1)
                v.tensor_tensor(chunk(X, k), chunk(X, k), tiles(0, P), ALU.add).then_inc(n3["x"], 1)
                dve.wait_ge(n3["x"], k + 1)
                statistics(n3, lambda j: tile_of(X, k, j), k, b, had)
            dve.wait_ge(n2["b_added"], NCH)
            over_chunks(dve, (3, scale_shift(n3)), (2, x3_sum), (0, sum3))

            dve.wait_ge(n3["acc_zero"], 1)
            for b in range(2):
                source_indices(e3["idx"], b, b)

            def message_in(b):
                return v.tensor_tensor(A2[b][:, :, :], GA[b], ER[b][0:P, :].rearrange("p (g f) -> p g f", f=F), ALU.add)

            def edges3(t, first, last):
                for b in range(2):
                    c = 2 * t + b
                    window_one_hot(e3, OH, c, b, e3["agg"], not first)
                    if not (first and b == 0):
                        add_window(e3, c - 1, first and b == 1)
                    dve.wait_ge(gathered[b], 16 * G * (2 * PASS + t + 1))
                    if not last:
                        source_indices(e3["idx"], c + 2, b)
                    dve.wait_ge(attr_in[b], 16 * (PASS + t + 1))
                    if not first:
                        dve.wait_ge(e3["msg"], c - 1)
                    message_in(b).then_inc(e3["msg_in"], 1)
            over_groups(dve, edges3)
            add_window(e3, NG - 1, False)

            def general3(s, c, n):
                general_masks(x3, OH, s, c, n)
                source_indices(x3.sem, c, 0)
                dve.wait_ge(x3.sem, x3.after("loaded", n))
                message_in(0).then_inc(x3.sem, 1)
                general_add(x3, s, n)
            finish_edges(3, e3, x3, general3)

            def hh4(k, b, had):
                dve.wait_ge(counts_in[b], slot_count(k, b, 1) + 16 * NCH)
                if had(1):
                    dve.wait_ge(n4["mm"], k)
                hh = agg_stage[:, :, 0:P]
                v.tensor_tensor(hh, chunk_t(ACC, k), counts[b][0].rearrange("p (t n) -> p t n", n=P), ALU.mult
                                ).then_inc(n4["hh1"], 1)
                dve.wait_ge(n4["hh1"], k + 1)
                v.tensor_tensor(hh, hh, chunk_t(HT, k), ALU.add).then_inc(n4["hh"], 1)

            def x4_sum(k, b, had):
                dve.wait_ge(n4["mm2"], k + 1)
                dve.wait_ge(n4["b_added"], k + 1)
                v.tensor_tensor(chunk(X, k), chunk(X, k), tiles(2, P), ALU.add).then_inc(n4["out"], 1)
            dve.wait_ge(n3["ht"], NCH)
            dve.wait_ge(n3["h_added"], NCH)
            over_chunks(dve, (0, hh4), (2, x4_sum))

        @block.tensor
        def _(pe):
            mm = nc.tensor.matmul

            def wide(bank, lhsT, rhs, start, stop):
                o, n = tiles(bank, F, P), IN_BANK
                mm(o[:, 0:n, :], lhsT, rhs[:, 0:n, :], start=start, stop=stop)
                return mm(o[:, n:CH, :], lhsT, rhs[:, n:CH, :], start=start, stop=stop)

            def bias(bank, row):
                o, n = tiles(bank, P), IN_BANK
                mm(o[:, 0:n, :], ones_row[:, :], row[:, 0:n, :], start=True, stop=False)
                mm(o[:, n:CH, :], ones_row[:, :], row[:, n:CH, :], start=True, stop=False)

            def closes(j):
                return j == IN_BANK - 1 or j == CH - 1

            def per_tile(bank, stage, rhs, on_bias=False):
                for j in range(CH):
                    last = mm(tiles(bank, P)[:, j, :], stage[:, j, 0:P], rhs, start=not on_bias,
                              stop=not on_bias or closes(j))
                return last

            def turn(bank, stage):
                for j in range(CH):
                    last = mm(tiles(bank, F, P)[:, j, :], stage[:, j, :], ident[0:P, 0:P], start=True, stop=True)
                return last

            def histogram(s, c, b):
                pe.wait_ge(s["hist_in"], c + 1)
                for g in range(G):
                    last = mm(HIST, HHI[b][:, g, :], HLO[b][:, g, :], start=False, stop=False)
                last.then_inc(s["hist"], 1)

            def histogram_edge(s, start):
                last = mm(HIST, zeros16[:, 0:NHI], zeros16[:, :], start=start, stop=not start)
                if not start:
                    last.then_inc(s["hist"], 1)

            def histogram_end(s):
                for r in range(NG - 4 * EARLY):
                    histogram(s, 4 * EARLY + r, r)
                histogram_edge(s, False)

            def aggregate(rows, b):
                for g in range(G):
                    last = mm(AGG, rows[:, g, :], OH[b][:, g, :], start=(g == 0), stop=(g == G - 1))
                return last

            def group_aggregate(s, c, b, rows, none_before):
                pe.wait_ge(s["onehot"], c + 1)
                if not none_before:
                    pe.wait_ge(s["added"], c)
                aggregate(rows, b).then_inc(s["agg"], 1)

            pe.wait_ge(consts, N_CONSTS)
            pe.wait_ge(first_in, N_FIRST)

            def turn0(k, b, had):
                pe.wait_ge(ln["applied"], n0["before"] + k + 1)
                if had(1):
                    pe.wait_ge(n0["turned"], k)
                turn(0, rows[b]).then_inc(n0["turn"], 1)

            def tables0(k, b, had):
                pe.wait_ge(n0["turned"], k + 1)
                if had(1):
                    pe.wait_ge(n0["p_out"], k)
                    pe.wait_ge(n0["q_out"], k)
                for j in range(CH):
                    last = mm(PQ[:, j, :], A1[b][:, j, 0:P], w_pq[:, :], start=True, stop=True)
                last.then_inc(n0["mm"], 1)
            over_chunks(pe, (0, turn0), (1, tables0))

            pe.wait_ge(loads, N_LOADS)
            pe.wait_ge(n0["q_out"], NCH)
            pe.wait_ge(n0["p_out"], NCH)
            histogram_edge(e0, True)

            def x1_window(b):
                return wide(2 * b, L[b][:, :], R[b][:, :].rearrange("p (g e) -> p g e", g=G), True, False)

            def x1_sources(b):
                for g in range(G):
                    last = mm(tiles(2 * b, F, P)[:, g, :], GA[b][:, g, :], ident[0:P, 0:P], start=False, stop=closes(g))
                return last

            def ahead(c, b, t, later):
                pe.wait_ge(e0["onehot_t"], c + 1)
                pe.wait_ge(attr_in[b], 16 * (t + 1))
                pe.wait_ge(window_in[b], 16 * (t + 1))
                if later:
                    pe.wait_ge(e0["g1"], c - 1)
                x1_window(b).then_inc(e0["x1_win"], 1)
                histogram(e0, c, b)
            ahead(0, 0, 0, False)

            def edges0(t, first, last):
                for b in range(2):
                    c = 2 * t + b
                    pe.wait_ge(gathered[b], 16 * G * (t + 1))
                    x1_sources(b).then_inc(e0["x1"], 1)
                    if not (last and b == 1):
                        ahead(c + 1, 1 - b, t + b, not (first and b == 0))
                    pe.wait_ge(e0["g1"], c + 1)
                    if not (first and b == 0):
                        pe.wait_ge(e0["y2"], c)
                    per_tile(4, A1[b], w_m2[:, :]).then_inc(e0["x2"], 1)
                    if not (first and b == 0):
                        pe.wait_ge(e0["g2"], c)
                        group_aggregate(e0, c - 1, 1 - b, A3[1 - b], first and b == 1)
            over_groups(pe, edges0)
            histogram_edge(e0, False)
            pe.wait_ge(e0["g2"], NG)
            group_aggregate(e0, NG - 1, 1, A3[1], False)

            def general0(s, c, n):
                pe.wait_ge(x0.sem, x0.after("masks_t", n))
                x1_window(0)
                x1_sources(0).then_inc(x0.sem, 1)
                pe.wait_ge(x0.sem, x0.after("g1", n))
                per_tile(4, A1[0], w_m2[:, :]).then_inc(x0.sem, 1)
                pe.wait_ge(x0.sem, x0.after("g2", n))
                aggregate(A3[0], 0).then_inc(x0.sem, 1)
            general_path(pe, general0)
            pe.wait_ge(st["loaded"], 16)
            mm(TURNED, stat_rows[:, :], ident[0:NT, 0:NT], start=True, stop=True).then_inc(st["turned"], 1)

            pe.wait_ge(acc_done[0], 1)

            def messages1(k, b, had):
                if had(1):
                    pe.wait_ge(n1a["agg"], k)
                wide(0, w_m3[:, :], chunk_t(ACC, k), True, True).then_inc(n1a["mm"], 1)

            def update1(k, b, had):
                if had(1):
                    pe.wait_ge(n1a["act"], k)
                wide(2, w_uh[:, :], chunk_t(HT, k), True, False)
                pe.wait_ge(n1a["agg"], k + 1)
                wide(2, w_ua[:, :], agg_stage[:, :, 0:P], False, True).then_inc(n1a["mm2"], 1)

            def output1(k, b, had):
                pe.wait_ge(n1a["act"], k + 1)
                if had(1):
                    pe.wait_ge(n1a["y"], k)
                per_tile(4, t_stage, w_u2[:, :]).then_inc(n1a["mm3"], 1)
            over_chunks(pe, (1, update1), (0, messages1), (1, output1))

            def turn1(k, b, had):
                pe.wait_ge(ln_c["applied"], k + 1)
                if had(1):
                    pe.wait_ge(n1c["acc"], k)
                turn(6, table_stage).then_inc(n1c["turn"], 1)
            pe.wait_ge(st["copied"], 1)
            over_chunks(pe, (0, turn1))

            pe.wait_ge(n1c["acc"], NCH)
            histogram_edge(e1, True)

            def edges1(t, first, last, early):
                for b in range(2):
                    c = 2 * t + b
                    for r in range(2 * early):
                        histogram(e1, 2 * c + r, r)
                    pe.wait_ge(gathered[b], 16 * G * (PASS + t + 1))
                    group_aggregate(e1, c, b, GA[b], first and b == 0)
            over_groups_counting(pe, edges1, lambda: histogram_end(e1))

            def general1(s, c, n):
                pe.wait_ge(x1.sem, x1.after("loaded", n))
                aggregate(GA[0], 0).then_inc(x1.sem, 1)
            general_path(pe, general1)
            pe.wait_ge(st["loaded"], 32)
            mm(TURNED, stat_rows[:, :], ident[0:NT, 0:NT], start=True, stop=True).then_inc(st["turned"], 1)

            def product2(k, b, had):
                pe.wait_ge(n2["acc_cp"], k + 1)
                if had(1):
                    pe.wait_ge(n2["v"], k)
                per_tile(0, acc_stage[b], w_g[:, :]).then_inc(n2["mm"], 1)

            def turn2(k, b, had):
                pe.wait_ge(ln["applied"], n2["before"] + k + 1)
                if had(1):
                    pe.wait_ge(n2["turned"], k)
                turn(2, rows[b]).then_inc(n2["turn"], 1)
                if had(1):
                    pe.wait_ge(n2["out"], k)
                bias(4, o_lb)

            def linear2(k, b, had):
                pe.wait_ge(n2["turned"], k + 1)
                per_tile(4, A1[b], w_lin[:, :], on_bias=True).then_inc(n2["mm2"], 1)
            over_chunks(pe, (0, product2), (2, turn2), (2, linear2))

            def pick_tiles(b):
                for g in range(G):
                    last = mm(tiles(2 * b, W, P)[:, g, :], OHB[b][:, g, :], SM[b][:, g, :], start=True, stop=True)
                return last

            def row_tiles(b):
                for g in range(G):
                    last = mm(tiles(4, P)[:, g, :], A1[b][0:W, g, 0:P], L[b][0:W, :], start=True, stop=True)
                return last

            def pick(c, b, later):
                pe.wait_ge(e2["onehot"], c + 1)
                pe.wait_ge(e2["same"], c + 1)
                if later:
                    pe.wait_ge(e2["picked"], c - 1)
                pick_tiles(b).then_inc(e2["pick"], 1)
            pe.wait_ge(n2["out"], NCH)
            pick(0, 0, False)

            def edges2(t, first, last):
                for b in range(2):
                    c = 2 * t + b
                    if not (last and b == 1):
                        pick(c + 1, 1 - b, not (first and b == 0))
                    pe.wait_ge(e2["picked"], c + 1)
                    pe.wait_ge(window_in[b], 16 * (PASS + t + 1))
                    if not (first and b == 0):
                        pe.wait_ge(e2["rows_out"], c)
                    row_tiles(b).then_inc(e2["rows"], 1)
            over_groups(pe, edges2)

            def general2(s, c, n):
                pe.wait_ge(x2.sem, x2.after("idx", n))
                pick_tiles(0).then_inc(x2.sem, 1)
                pe.wait_ge(x2.sem, x2.after("picked", n))
                row_tiles(0).then_inc(x2.sem, 1)
            general_path(pe, general2)

            pe.wait_ge(e2["rows_out"], NG)

            def free3(k, b, had):
                if had(4):
                    pe.wait_ge(n3["ht"], k - 3)

            def turn3(k, b, had):
                pe.wait_ge(n3["sum"], k + 1)
                turn(6, rows[b]).then_inc(n3["turn"], 1)

            def output3(k, b, had):
                pe.wait_ge(n3["act"], 2 * k + 2)
                if had(1):
                    pe.wait_ge(n3["x"], k)
                for j in range(CH):
                    for h in range(2):
                        last = mm(tiles(0, P)[:, j, :], hid_stage[h][:, j, 0:P], w_z2[:, h, :],
                                  start=h == 0, stop=h == 1)
                last.then_inc(n3["mm2"], 1)

            def hidden3(k, b, had):
                pe.wait_ge(n3["turned"], k + 1)
                if had(1):
                    pe.wait_ge(n3["act"], 2 * k)
                wide(2, w_z1[:, 0:F], z_stage[:, :, 0:P], True, True)
                wide(4, w_z1[:, F:2 * F], z_stage[:, :, 0:P], True, True).then_inc(n3["mm"], 1)

            def turn_table3(k, b, had):
                pe.wait_ge(ln["applied"], n3["before"] + k + 1)
                if had(1):
                    pe.wait_ge(n3["ht"], k)
                turn(6, table_stage).then_inc(n3["turn2"], 1)
            over_chunks(pe, (1, output3), (0, free3), (0, turn3), (0, hidden3), (3, turn_table3))

            pe.wait_ge(n3["ht"], NCH)

            def edges3(t, first, last):
                for b in range(2):
                    c = 2 * t + b
                    pe.wait_ge(e3["msg"], c + 1)
                    group_aggregate(e3, c, b, A3[b], first and b == 0)
            over_groups(pe, edges3)

            def general3(s, c, n):
                pe.wait_ge(x3.sem, x3.after("msg", n))
                aggregate(A3[0], 0).then_inc(x3.sem, 1)
            general_path(pe, general3)

            def hidden4(k, b, had):
                pe.wait_ge(n4["hh"], k + 1)
                if had(1):
                    pe.wait_ge(n4["act"], k)
                wide(0, w_s1[:, :], agg_stage[:, :, 0:P], True, True).then_inc(n4["mm"], 1)

            def output4(k, b, had):
                pe.wait_ge(n4["act"], k + 1)
                if had(1):
                    pe.wait_ge(n4["out"], k)
                per_tile(2, t_stage, w_s2[:, :]).then_inc(n4["mm2"], 1)
            over_chunks(pe, (0, hidden4), (1, output4))


_PLAIN = ["L0_gnn_mW1", "L0_gnn_mb1", "L0_gnn_mW2", "L0_gnn_mb2", "L0_gnn_mW3", "L0_gnn_mb3", "L0_gnn_uW1",
          "L0_gnn_ub1", "L0_gnn_uW2", "L0_gnn_ub2", "L0_gnn_gamma", "L0_gnn_beta", "L1_gnn_W", "L1_gnn_b",
          "L2_gnn_lin_w", "L2_gnn_lin_b", "L2_gnn_w1", "L2_gnn_b1", "L2_gnn_w2", "L2_gnn_b2", "L3_gnn_W1",
          "L3_gnn_b1", "L3_gnn_W2", "L3_gnn_b2"]


def kernel(**inputs):
    import numpy as np
    import concourse.bacc as bacc
    from concourse.bass_utils import run_bass_kernel_spmd

    a = {n: np.ascontiguousarray(inputs[n]) for n in inputs}
    by_partition = {n: a[n].reshape(NG, P, G).transpose(1, 0, 2).reshape(P, NG * G) for n in ("src", "dst")}
    by_tile = {n: a[n].reshape(NG, P, G).transpose(0, 2, 1).reshape(NG, G * P) for n in ("src", "dst")}
    edge_attr_64_t = a["edge_attr_64"].reshape(NG, P, G, FE).transpose(0, 3, 2, 1).reshape(NG * FE, G * P)
    laid = [("x", a["x"]), ("src_g", by_partition["src"]), ("dst_g", by_partition["dst"]),
            ("src_rows", by_tile["src"]), ("dst_rows", by_tile["dst"]),
            ("edge_attr_128", a["edge_attr_128"]), ("edge_attr_64_t", edge_attr_64_t)]
    laid += [(n, a[n]) for n in _PLAIN]

    nc = bacc.Bacc("TRN2", target_bir_lowering=False, num_devices=1)
    arrays, args = {}, []
    for name, v in laid:
        v = np.ascontiguousarray(v)
        arrays[f"in_{name}"] = v
        args.append(nc.dram_tensor(f"in_{name}", v.shape, mybir.dt.from_np(v.dtype), kind="ExternalInput").ap())
    args.append(nc.dram_tensor("out_x", (N, F), F32, kind="ExternalOutput").ap())
    gnn_kernel(nc, *args)
    r = run_bass_kernel_spmd(nc, [arrays], core_ids=[0])
    return r.results[0]["out_x"]
```
